# Optimizing a Trainium2 kernel written in Bass

```python
import numpy as np
import jax
import jax.numpy as jnp

def _softmax(x, axis=-1):
    return jax.nn.softmax(x, axis=axis)

def _gelu(x):
    return jax.nn.gelu(x, approximate=True)

def _silu(x):
    return jax.nn.silu(x)

def _sigmoid(x):
    return jax.nn.sigmoid(x)

def _layernorm(x, axis=-1, eps=1e-05):
    m = jnp.mean(x, axis=axis, keepdims=True)
    v = jnp.var(x, axis=axis, keepdims=True)
    return (x - m) / jnp.sqrt(v + eps)

def _scatter_add(tgt, idx, src, axis=0):
    return tgt.at[idx].add(src)

def _segment_sum(src, seg, n):
    return jax.ops.segment_sum(src, seg, n)
kernel_name = 'mk_decoder_postln_d1_seqx_r8_80f83f'

def setup_inputs(seed: int=0):
    np.random.seed(seed)
    _w = jnp.asarray

    def _rec_inputs():
        import jax
        import jax.numpy as jnp
        _rk = jax.random.key(seed)
        x = -1.394e-06 + 0.9999 * jax.random.normal(jax.random.fold_in(_rk, 1), (16, 128, 128), jnp.float32)
        _lenS = 128 - jax.random.randint(jax.random.fold_in(_rk, 7), (16,), 0, max(1, 128 // 4) + 1, jnp.int32)
        _lenS2 = 128 - jax.random.randint(jax.random.fold_in(_rk, 8), (16,), 0, max(1, 128 // 4) + 1, jnp.int32)
        _ctx_1024P = jax.random.normal(jax.random.fold_in(_rk, 11), (16, 16, 128), jnp.float32)
        _ctx_1024c = jax.random.dirichlet(jax.random.fold_in(_rk, 511), 0.3 * jnp.ones((16,), jnp.float32), (16, 128))
        _ctx_1024t = jnp.einsum('bsk,bkd->bsd', _ctx_1024c, _ctx_1024P)
        _ctx_1024t = _ctx_1024t * jax.lax.rsqrt(jnp.mean(jnp.square(_ctx_1024t)) + 1e-12) * 0.953939
        ctx_1024 = -0.000292821 + 1.00034 * (_ctx_1024t + 0.3 * jax.random.normal(jax.random.fold_in(_rk, 611), (16, 128, 128), jnp.float32))
        return (x, ctx_1024)
    x, ctx_1024 = _rec_inputs()

    def _L0_attn_setup():
        import jax, jax.numpy as jnp
        import numpy as np
        DIM = 128
        DEPTH = 6
        LN_EPS = 1e-05

        def _layernorm(x, gamma, beta):
            mu = jnp.mean(x, axis=-1, keepdims=True)
            var = jnp.mean(jnp.square(x - mu), axis=-1, keepdims=True)
            return (x - mu) * jax.lax.rsqrt(var + LN_EPS) * gamma + beta
        key = jax.random.key(seed)
        ks = jax.random.split(key, 6)
        b, n, d = (4, 256, DIM)
        x = jax.random.normal(ks[0], (b, n, d), dtype=jnp.float32)
        w_qkv = jax.random.normal(ks[1], (DEPTH, d, 3 * d), dtype=jnp.float32) * 0.02
        w_out = jax.random.normal(ks[2], (DEPTH, d, d), dtype=jnp.float32) * 0.02
        b_out = jnp.zeros((DEPTH, d), dtype=jnp.float32)
        gamma = jnp.ones((DEPTH, d), dtype=jnp.float32)
        beta = jnp.zeros((DEPTH, d), dtype=jnp.float32)
        return {'x': x, 'w_qkv': w_qkv, 'w_out': w_out, 'b_out': b_out, 'gamma': gamma, 'beta': beta}
    _L0_attn_all = _L0_attn_setup()
    _L0_attn_in = {k: v for k, v in _L0_attn_all.items() if k in ('w_qkv', 'w_out', 'b_out', 'gamma', 'beta')}
    del _L0_attn_all

    def _L0_xattn_setup():
        import jax, jax.numpy as jnp
        import numpy as np
        B, S, D, H, F = (2, 256, 128, 16, 512)
        DH = D // H
        EPS = 1e-05

        def _layer_norm(x, g, b):
            mu = jnp.mean(x, axis=-1, keepdims=True)
            var = jnp.mean((x - mu) ** 2, axis=-1, keepdims=True)
            return (x - mu) * jax.lax.rsqrt(var + EPS) * g + b

        def _mha(q_in, kv_in, wq, bq, wk, bk, wv, bv, wo, bo, causal):
            b, s, d = q_in.shape
            q = (q_in @ wq + bq).reshape(b, s, H, DH).transpose(0, 2, 1, 3)
            k = (kv_in @ wk + bk).reshape(b, s, H, DH).transpose(0, 2, 1, 3)
            v = (kv_in @ wv + bv).reshape(b, s, H, DH).transpose(0, 2, 1, 3)
            scores = jnp.einsum('bhqd,bhkd->bhqk', q, k) / np.sqrt(DH).astype(np.float32)
            if causal:
                mask = jnp.tril(jnp.ones((s, s), dtype=bool))
                scores = jnp.where(mask, scores, -jnp.inf)
            attn = jax.nn.softmax(scores, axis=-1)
            out = jnp.einsum('bhqk,bhkd->bhqd', attn, v)
            out = out.transpose(0, 2, 1, 3).reshape(b, s, d)
            return out @ wo + bo
        key = jax.random.key(seed)
        ks = iter(jax.random.split(key, 24))

        def w(shape, fan_in):
            return jax.random.normal(next(ks), shape, jnp.float32) / np.sqrt(fan_in).astype(np.float32)
        inp = {'encoder_output': jax.random.normal(next(ks), (B, S, D), jnp.float32), 'decoder_input': jax.random.normal(next(ks), (B, S, D), jnp.float32)}
        for pre in ('sa', 'ca'):
            for nm in ('wq', 'wk', 'wv', 'wo'):
                inp[f'{pre}_{nm}'] = w((D, D), D)
                inp[f'{pre}_b{nm[-1]}'] = jnp.zeros((D,), jnp.float32)
            inp[f'{pre}_g'] = jnp.ones((D,), jnp.float32)
            inp[f'{pre}_bt'] = jnp.zeros((D,), jnp.float32)
        inp['f_w1'] = w((D, F), D)
        inp['f_b1'] = jnp.zeros((F,), jnp.float32)
        inp['f_w2'] = w((F, D), F)
        inp['f_b2'] = jnp.zeros((D,), jnp.float32)
        inp['f_g'] = jnp.ones((D,), jnp.float32)
        inp['f_bt'] = jnp.zeros((D,), jnp.float32)
        return inp
    _L0_xattn_all = _L0_xattn_setup()
    _L0_xattn_in = {k: v for k, v in _L0_xattn_all.items() if k in ('sa_wq', 'sa_bq', 'sa_wk', 'sa_bk', 'sa_wv', 'sa_bv', 'sa_wo', 'sa_bo', 'sa_g', 'sa_bt', 'ca_wq', 'ca_bq', 'ca_wk', 'ca_bk', 'ca_wv', 'ca_bv', 'ca_wo', 'ca_bo', 'ca_g', 'ca_bt', 'f_w1', 'f_b1', 'f_w2', 'f_b2', 'f_g', 'f_bt')}
    del _L0_xattn_all

    def _L0_ffn_setup():
        import jax, jax.numpy as jnp
        import numpy as np
        B, S, D, F, E = (2, 256, 128, 512, 8)
        LN_EPS = 1e-05

        def _xavier(key, shape, fan_in, fan_out):
            a = np.sqrt(6.0 / (fan_in + fan_out))
            return jax.random.uniform(key, shape, jnp.float32, -a, a)
        key = jax.random.key(seed)
        ks = jax.random.split(key, 8)
        tgt = jax.random.normal(ks[0], (B, S, D), jnp.float32)
        router_w = _xavier(ks[1], (E, D), D, E)
        router_b = jnp.zeros((E,), jnp.float32)
        w1 = _xavier(ks[2], (E, D, F), D, F)
        b1 = jnp.zeros((E, F), jnp.float32)
        w2 = _xavier(ks[3], (E, F, D), F, D)
        b2 = jnp.zeros((E, D), jnp.float32)
        gamma = jnp.ones((D,), jnp.float32)
        beta = jnp.zeros((D,), jnp.float32)
        return {'tgt': tgt, 'router_w': router_w, 'router_b': router_b, 'w1': w1, 'b1': b1, 'w2': w2, 'b2': b2, 'gamma': gamma, 'beta': beta}
    _L0_ffn_all = _L0_ffn_setup()
    _L0_ffn_in = {k: v for k, v in _L0_ffn_all.items() if k in ('router_w', 'router_b', 'w1', 'b1', 'w2', 'b2', 'gamma', 'beta')}
    del _L0_ffn_all
    return {'x': x, 'ctx_1024': ctx_1024, 'L0_attn_w_qkv': _L0_attn_in['w_qkv'], 'L0_attn_w_out': _L0_attn_in['w_out'], 'L0_attn_b_out': _L0_attn_in['b_out'], 'L0_attn_gamma': _L0_attn_in['gamma'], 'L0_attn_beta': _L0_attn_in['beta'], 'L0_xattn_sa_wq': _L0_xattn_in['sa_wq'], 'L0_xattn_sa_bq': _L0_xattn_in['sa_bq'], 'L0_xattn_sa_wk': _L0_xattn_in['sa_wk'], 'L0_xattn_sa_bk': _L0_xattn_in['sa_bk'], 'L0_xattn_sa_wv': _L0_xattn_in['sa_wv'], 'L0_xattn_sa_bv': _L0_xattn_in['sa_bv'], 'L0_xattn_sa_wo': _L0_xattn_in['sa_wo'], 'L0_xattn_sa_bo': _L0_xattn_in['sa_bo'], 'L0_xattn_sa_g': _L0_xattn_in['sa_g'], 'L0_xattn_sa_bt': _L0_xattn_in['sa_bt'], 'L0_xattn_ca_wq': _L0_xattn_in['ca_wq'], 'L0_xattn_ca_bq': _L0_xattn_in['ca_bq'], 'L0_xattn_ca_wk': _L0_xattn_in['ca_wk'], 'L0_xattn_ca_bk': _L0_xattn_in['ca_bk'], 'L0_xattn_ca_wv': _L0_xattn_in['ca_wv'], 'L0_xattn_ca_bv': _L0_xattn_in['ca_bv'], 'L0_xattn_ca_wo': _L0_xattn_in['ca_wo'], 'L0_xattn_ca_bo': _L0_xattn_in['ca_bo'], 'L0_xattn_ca_g': _L0_xattn_in['ca_g'], 'L0_xattn_ca_bt': _L0_xattn_in['ca_bt'], 'L0_xattn_f_w1': _L0_xattn_in['f_w1'], 'L0_xattn_f_b1': _L0_xattn_in['f_b1'], 'L0_xattn_f_w2': _L0_xattn_in['f_w2'], 'L0_xattn_f_b2': _L0_xattn_in['f_b2'], 'L0_xattn_f_g': _L0_xattn_in['f_g'], 'L0_xattn_f_bt': _L0_xattn_in['f_bt'], 'L0_ffn_router_w': _L0_ffn_in['router_w'], 'L0_ffn_router_b': _L0_ffn_in['router_b'], 'L0_ffn_w1': _L0_ffn_in['w1'], 'L0_ffn_b1': _L0_ffn_in['b1'], 'L0_ffn_w2': _L0_ffn_in['w2'], 'L0_ffn_b2': _L0_ffn_in['b2'], 'L0_ffn_gamma': _L0_ffn_in['gamma'], 'L0_ffn_beta': _L0_ffn_in['beta']}

def reference(x, ctx_1024, L0_attn_w_qkv, L0_attn_w_out, L0_attn_b_out, L0_attn_gamma, L0_attn_beta, L0_xattn_sa_wq, L0_xattn_sa_bq, L0_xattn_sa_wk, L0_xattn_sa_bk, L0_xattn_sa_wv, L0_xattn_sa_bv, L0_xattn_sa_wo, L0_xattn_sa_bo, L0_xattn_sa_g, L0_xattn_sa_bt, L0_xattn_ca_wq, L0_xattn_ca_bq, L0_xattn_ca_wk, L0_xattn_ca_bk, L0_xattn_ca_wv, L0_xattn_ca_bv, L0_xattn_ca_wo, L0_xattn_ca_bo, L0_xattn_ca_g, L0_xattn_ca_bt, L0_xattn_f_w1, L0_xattn_f_b1, L0_xattn_f_w2, L0_xattn_f_b2, L0_xattn_f_g, L0_xattn_f_bt, L0_ffn_router_w, L0_ffn_router_b, L0_ffn_w1, L0_ffn_b1, L0_ffn_w2, L0_ffn_b2, L0_ffn_gamma, L0_ffn_beta):
    import jax
    import jax.numpy as jnp

    def _L0_attn_ref(x, w_qkv, w_out, b_out, gamma, beta):
        import jax, jax.numpy as jnp
        import numpy as np
        DIM = 128
        DEPTH = 6
        LN_EPS = 1e-05

        def _layernorm(x, gamma, beta):
            mu = jnp.mean(x, axis=-1, keepdims=True)
            var = jnp.mean(jnp.square(x - mu), axis=-1, keepdims=True)
            return (x - mu) * jax.lax.rsqrt(var + LN_EPS) * gamma + beta
        depth = w_qkv.shape[0]
        for l in range(depth):
            residual = x
            h = _layernorm(x, gamma[l], beta[l])
            qkv = h @ w_qkv[l]
            q, k, v = jnp.split(qkv, 3, axis=-1)
            q = jax.nn.softmax(q, axis=1)
            k = jax.nn.softmax(k, axis=2)
            context = jnp.einsum('bic,bjc->bij', k, v)
            out = jnp.einsum('bic,bij->bjc', q, context)
            out = out @ w_out[l] + b_out[l]
            x = out + residual
        return x

    def _L0_xattn_ref(encoder_output, decoder_input, sa_wq, sa_bq, sa_wk, sa_bk, sa_wv, sa_bv, sa_wo, sa_bo, sa_g, sa_bt, ca_wq, ca_bq, ca_wk, ca_bk, ca_wv, ca_bv, ca_wo, ca_bo, ca_g, ca_bt, f_w1, f_b1, f_w2, f_b2, f_g, f_bt):
        import jax, jax.numpy as jnp
        import numpy as np
        B, S, D, H, F = (2, 256, 128, 16, 512)
        DH = D // H
        EPS = 1e-05

        def _layer_norm(x, g, b):
            mu = jnp.mean(x, axis=-1, keepdims=True)
            var = jnp.mean((x - mu) ** 2, axis=-1, keepdims=True)
            return (x - mu) * jax.lax.rsqrt(var + EPS) * g + b

        def _mha(q_in, kv_in, wq, bq, wk, bk, wv, bv, wo, bo, causal):
            b, s, d = q_in.shape
            q = (q_in @ wq + bq).reshape(b, s, H, DH).transpose(0, 2, 1, 3)
            k = (kv_in @ wk + bk).reshape(b, s, H, DH).transpose(0, 2, 1, 3)
            v = (kv_in @ wv + bv).reshape(b, s, H, DH).transpose(0, 2, 1, 3)
            scores = jnp.einsum('bhqd,bhkd->bhqk', q, k) / np.sqrt(DH).astype(np.float32)
            if causal:
                mask = jnp.tril(jnp.ones((s, s), dtype=bool))
                scores = jnp.where(mask, scores, -jnp.inf)
            attn = jax.nn.softmax(scores, axis=-1)
            out = jnp.einsum('bhqk,bhkd->bhqd', attn, v)
            out = out.transpose(0, 2, 1, 3).reshape(b, s, d)
            return out @ wo + bo
        x = _mha(decoder_input, decoder_input, sa_wq, sa_bq, sa_wk, sa_bk, sa_wv, sa_bv, sa_wo, sa_bo, True)
        x = _layer_norm(x + decoder_input, sa_g, sa_bt)
        y = _mha(x, encoder_output, ca_wq, ca_bq, ca_wk, ca_bk, ca_wv, ca_bv, ca_wo, ca_bo, False)
        y = _layer_norm(y + x, ca_g, ca_bt)
        h = jax.nn.relu(y @ f_w1 + f_b1) @ f_w2 + f_b2
        return _layer_norm(h + y, f_g, f_bt)

    def _L0_ffn_ref(tgt, router_w, router_b, w1, b1, w2, b2, gamma, beta):
        import jax, jax.numpy as jnp
        import numpy as np
        B, S, D, F, E = (2, 256, 128, 512, 8)
        LN_EPS = 1e-05

        def _xavier(key, shape, fan_in, fan_out):
            a = np.sqrt(6.0 / (fan_in + fan_out))
            return jax.random.uniform(key, shape, jnp.float32, -a, a)
        logits = jnp.einsum('bsd,ed->bse', tgt, router_w) + router_b
        rw = jax.nn.softmax(logits, axis=-1)
        rw = jnp.zeros_like(rw).at[..., 0].set(1.0)
        h = jax.nn.relu(jnp.einsum('bsd,edf->besf', tgt, w1) + b1[None, :, None, :])
        eo = jnp.einsum('besf,efd->besd', h, w2) + b2[None, :, None, :]
        tgt2 = jnp.einsum('besd,bse->bsd', eo, rw)
        x = tgt + tgt2
        mean = jnp.mean(x, axis=-1, keepdims=True)
        var = jnp.mean(jnp.square(x - mean), axis=-1, keepdims=True)
        return (x - mean) * jax.lax.rsqrt(var + LN_EPS) * gamma + beta
    x = _layernorm(x + _L0_attn_ref(x, L0_attn_w_qkv, L0_attn_w_out, L0_attn_b_out, L0_attn_gamma, L0_attn_beta), axis=-1)
    x = _layernorm(x + _L0_xattn_ref(ctx_1024, x, L0_xattn_sa_wq, L0_xattn_sa_bq, L0_xattn_sa_wk, L0_xattn_sa_bk, L0_xattn_sa_wv, L0_xattn_sa_bv, L0_xattn_sa_wo, L0_xattn_sa_bo, L0_xattn_sa_g, L0_xattn_sa_bt, L0_xattn_ca_wq, L0_xattn_ca_bq, L0_xattn_ca_wk, L0_xattn_ca_bk, L0_xattn_ca_wv, L0_xattn_ca_bv, L0_xattn_ca_wo, L0_xattn_ca_bo, L0_xattn_ca_g, L0_xattn_ca_bt, L0_xattn_f_w1, L0_xattn_f_b1, L0_xattn_f_w2, L0_xattn_f_b2, L0_xattn_f_g, L0_xattn_f_bt), axis=-1)
    x = _layernorm(x + _L0_ffn_ref(x, L0_ffn_router_w, L0_ffn_router_b, L0_ffn_w1, L0_ffn_b1, L0_ffn_w2, L0_ffn_b2, L0_ffn_gamma, L0_ffn_beta), axis=-1)
    return x

_drawn_inputs = setup_inputs


def setup_inputs(seed=0):
    import zlib

    import numpy as np

    out = dict(_drawn_inputs(seed))
    spreads = {'L0_attn_b_out': (0.0, 0.1),
     'L0_attn_gamma': (1.0, 0.6),
     'L0_attn_beta': (0.0, 0.8),
     'L0_xattn_sa_bq': (0.0, 0.744),
     'L0_xattn_sa_bk': (0.0, 0.8),
     'L0_xattn_sa_bv': (0.0, 0.1),
     'L0_xattn_sa_bo': (0.0, 0.1),
     'L0_xattn_sa_g': (1.0, 0.2),
     'L0_xattn_sa_bt': (0.0, 0.1),
     'L0_xattn_ca_bq': (0.0, 0.8),
     'L0_xattn_ca_bk': (0.0, 0.8),
     'L0_xattn_ca_bv': (0.0, 0.1),
     'L0_xattn_ca_bo': (0.0, 0.1),
     'L0_xattn_ca_g': (1.0, 0.2),
     'L0_xattn_ca_bt': (0.0, 0.1),
     'L0_xattn_f_b1': (0.0, 0.294),
     'L0_xattn_f_b2': (0.0, 0.1),
     'L0_xattn_f_g': (1.0, 0.2),
     'L0_xattn_f_bt': (0.0, 0.1),
     'L0_ffn_router_b': (0.0, 0.1),
     'L0_ffn_b1': (0.0, 0.1),
     'L0_ffn_b2': (0.0, 0.1),
     'L0_ffn_gamma': (1.0, 0.2),
     'L0_ffn_beta': (0.0, 0.1)}
    factors = {'L0_attn_w_qkv': 8.0, 'L0_attn_w_out': 8.0}
    for name, (base, spread) in spreads.items():
        noise = np.random.default_rng([zlib.crc32(name.encode()), seed]).standard_normal(out[name].shape)
        drawn = base * np.exp(spread * noise) if base else spread * noise
        out[name] = jnp.asarray(drawn.astype(out[name].dtype))
    for name, factor in factors.items():
        out[name] = (out[name] * factor).astype(out[name].dtype)
    return out
```

```python
from contextlib import ExitStack

import numpy as np

import concourse.bass as bass
from concourse import mybir

F32 = mybir.dt.float32
BF16 = mybir.dt.bfloat16
ALU = mybir.AluOpType
ACT = mybir.ActivationFunctionType
AX = mybir.AxisListType

P = 128
B = 16
DEPTH = 6
GB = 4
G = B // GB
W = GB * P
ITEMS = DEPTH * G
EPS = 1e-5

H = 16
DH = P // H
SIDES, TILES = 2, H // 2
ROWS = 6 * DH
Q_PARTS = (0, 0, 0, 1, 1, 2)
K_PARTS = (0, 1, 2, 0, 1, 0)
HALF = 2 * GB
VW = 32
MASKED = -3.0e38
SCALE = float(1.0 / np.sqrt(np.float32(DH)))

FC = 4
FFN_ITEMS = 2 * G

R_SA_BV, R_SA_BO, R_SA_G, R_SA_BT, R_CA_BV, R_CA_BO, R_CA_G, R_CA_BT = range(DEPTH, DEPTH + 8)
R_B2, R_G, R_BT = DEPTH + 8, DEPTH + 9, DEPTH + 10
NROWS = DEPTH + 14
C_BQ, C_BK, C_B1 = 2 * DEPTH, 2 * DEPTH + 1, 2 * DEPTH + 4
NCOLS = 2 * DEPTH + 4 + 2 * FC


class Names:
    pass


class Item:

    def __init__(self, n, layer, g):
        self.n, self.layer, self.g = n, layer, g


def at_least(eng, sem, count):
    if isinstance(count, int) and count <= 0:
        return
    eng.wait_ge(sem, count)


def wait_apart(eng, s, *waits):
    waits = [(sem, count if isinstance(count, int) else eng.snap(eng.to_reg(count))) for sem, count in waits]
    eng.wait_ge(s.ident_set, 2)
    for sem, count in waits:
        at_least(eng, sem, count)


def per_batch(ap):
    return ap.rearrange("p (b t) -> p b t", t=P)


def spread(ap, n):
    return ap.unsqueeze(2).to_broadcast([ap.shape[0], ap.shape[1], n])


def each_batch(ap, n=GB):
    return ap.unsqueeze(1).to_broadcast([ap.shape[0], n, ap.shape[1]])


def columns(b):
    return slice(b * P, b * P + P)


def group(g):
    return bass.ds(g * W, W)



def allocate(nc, ctx):
    def sb(name, shape, dt=F32):
        return ctx.enter_context(nc.sbuf_tensor(name, shape, dt))

    m = Names()
    m.x0 = sb("x0", [P, B * P])
    m.xr = sb("xr", [P, B * P])
    m.y = sb("y", [P, B * P])
    m.w_qkv = sb("w_qkv", [P, DEPTH, 3 * P])
    m.w_out = sb("w_out", [P, DEPTH, P])
    m.w_att = sb("w_att", [P, 8, P])
    m.w1 = sb("w1", [P, 2, FC * P])
    m.w2 = sb("w2", [P, 2, FC, P])
    m.row = sb("row", [P, NROWS, P])
    m.col = sb("col", [P, NCOLS])
    m.bq = sb("bq", [P, 2])
    m.ident = sb("ident", [P, P])
    m.ident_bf = sb("ident_bf", [P, P], BF16)
    m.mask_q = sb("mask_q", [P, GB, P], BF16)
    m.mask_k = sb("mask_k", [P, GB, P], BF16)
    m.pick = sb("pick", [P, TILES, P], BF16)
    m.minus_half = sb("minus_half", [P, GB])
    m.wq_now = sb("wq_now", [P, P])
    m.wv_now = sb("wv_now", [P, P])
    m.bn = sb("bn", [P, G, GB, 6])
    m.mv = sb("mv", [P, G, GB, 2])
    m.veps = sb("veps", [P, G, GB])
    m.rstd = sb("rstd", [P, G, GB])
    m.nmean = sb("nmean", [P, G, GB])
    m.nmr = sb("nmr", [P, G, GB])
    m.nqmax = sb("nqmax", [P, G, GB])
    m.nkmax = sb("nkmax", [P, G, GB])
    m.qsum = sb("qsum", [P, G, GB])
    m.ksum = sb("ksum", [P, G, GB])
    m.rq = sb("rq", [P, G, GB])
    m.rk = sb("rk", [P, G, GB])
    m.xT = sb("xT", [P, G, W])
    m.full = sb("full", [P, 2, W])
    m.rest = sb("rest", [P, 2, W])
    m.kp_cross = sb("kp_cross", [P, 3, B * P], BF16)
    m.v_self = sb("v_self", [P, B, P])
    m.v_cross = sb("v_cross", [P, B, P])
    m.v_pad = sb("v_pad", [P, 2, H, VW])
    m.negmax = sb("negmax", [P, 2, SIDES, TILES])
    m.negmax_rest = sb("negmax_rest", [P, 2, SIDES, TILES])
    m.negmax_parts = sb("negmax_parts", [P, 2, P], BF16)
    m.negmax_T = sb("negmax_T", [P, 2, P], BF16)
    m.o_T = sb("o_T", [P, W])
    m.o_recip = sb("o_recip", [P, 2, H])
    m.o = sb("o", [P, 2, P])
    m.att_T = sb("att_T", [P, W])
    arena = sb("arena", [P, 8 * G * W])
    eighth = lambda k: arena[:, k * G * W:(k + 1) * G * W].rearrange("p (g w) -> p g w", w=W)
    m.xn, m.hT, m.eq, m.ek, m.qt, m.vT, m.ms, m.gs = (eighth(k) for k in range(8))
    half = arena[:, :].bitcast(BF16)
    size = 2 * TILES * W
    m.q_op = half[:, 0:size].rearrange("p (r j t) -> p r j t", r=2, t=W)
    m.k_op = half[:, size:2 * size].rearrange("p (r j t) -> p r j t", r=2, t=W)
    m.q_parts = half[:, 2 * size:2 * size + 3 * B * P].rearrange("p (a t) -> p a t", a=3)
    m.kp_self = half[:, 2 * size + 3 * B * P:2 * size + 6 * B * P].rearrange("p (a t) -> p a t", a=3)
    at = size + 3 * B * P
    m.prob = arena[:, at:at + 2 * 2 * W].rearrange("p (u t) -> p u t", u=2)
    m.hidden = arena[:, 0:2 * FC * W].rearrange("p (r c t) -> p r c t", r=2, c=FC)
    m.bank = [ctx.enter_context(nc.psum_tensor(f"bank{n}", [P, W], F32)) for n in range(4, 8)]
    m.pairs = [ctx.enter_context(nc.psum_tensor(f"pair{n}", [P, 2 * W], F32)) for n in range(2)]
    m.bank = [m.pairs[0][:, 0:W], m.pairs[0][:, W:2 * W], m.pairs[1][:, 0:W], m.pairs[1][:, W:2 * W]] + \
             [t[:, :] for t in m.bank]
    return m


def semaphores(nc, ctx):
    s = Names()

    def new(name):
        return ctx.enter_context(nc.semaphore(name))

    s.x_in = [new(f"x_in{g}") for g in range(G)]
    s.ctx_in = [new(f"ctx_in{g}") for g in range(G)]
    s.op_loaded = [new(f"op_loaded{r}") for r in range(2)]
    s.x_again = new("x_again")
    s.cols_in = new("cols_in")
    s.rows_in = new("rows_in")
    s.w_att_in = new("w_att_in")
    s.w_qkv_in = new("w_qkv_in")
    s.w_out_in = new("w_out_in")
    s.w_ffn_in = new("w_ffn_in")
    s.stored = new("stored")
    s.ident_set = new("ident_set")
    s.ident_bf_set = new("ident_bf_set")
    s.half_set = new("half_set")
    s.mask_set = new("mask_set")
    s.pick_set = new("pick_set")
    s.v_pad_set = new("v_pad_set")
    s.parts_set = new("parts_set")
    s.bq_set = new("bq_set")
    s.bn_done = new("bn_done")
    s.mv_done = new("mv_done")
    s.veps_done = new("veps_done")
    s.rstd_done = new("rstd_done")
    s.nmean_done = new("nmean_done")
    s.xn_ready = new("xn_ready")
    s.bias_added = new("bias_added")
    s.T_done = new("T_done")
    s.hT_ready = new("hT_ready")
    s.wq_loaded = new("wq_loaded")
    s.wv_loaded = new("wv_loaded")
    s.Q_done = new("Q_done")
    s.K_done = new("K_done")
    s.V_done = new("V_done")
    s.TQ_done = new("TQ_done")
    s.M_done = new("M_done")
    s.G_done = new("G_done")
    s.F_done = new("F_done")
    s.nqmax_ready = new("nqmax_ready")
    s.nkmax_ready = new("nkmax_ready")
    s.eq_ready = new("eq_ready")
    s.ek_ready = new("ek_ready")
    s.rq_ready = new("rq_ready")
    s.rk_ready = new("rk_ready")
    s.qt_ready = new("qt_ready")
    s.ms_ready = new("ms_ready")
    s.gs_ready = new("gs_ready")
    s.vT_ready = new("vT_ready")
    s.x_added = new("x_added")
    s.b1_sum = new("b1_sum")
    s.b1_bn = new("b1_bn")
    s.b1_mv = new("b1_mv")
    s.b1_veps = new("b1_veps")
    s.b1_nmean = new("b1_nmean")
    s.b1_rstd = new("b1_rstd")
    s.x1_ready = new("x1_ready")
    s.y_ready = new("y_ready")
    s.t_done = new("t_done")
    s.xT_ready = new("xT_ready")
    s.proj_done = new("proj_done")
    s.full_ready = new("full_ready")
    s.rest_ready = new("rest_ready")
    s.mid_ready = new("mid_ready")
    s.parts_ready = new("parts_ready")
    s.v_done = new("v_done")
    s.v_ready = new("v_ready")
    s.v_pad_ready = new("v_pad_ready")
    s.S_done = new("S_done")
    s.max_done = new("max_done")
    s.negmax_hi = new("negmax_hi")
    s.negmax_rest_ready = new("negmax_rest_ready")
    s.negmax_mid = new("negmax_mid")
    s.negmax_lo = new("negmax_lo")
    s.TM_done = new("TM_done")
    s.negmax_T_ready = new("negmax_T_ready")
    s.ST_done = new("ST_done")
    s.exp_done = new("exp_done")
    s.PV_done = new("PV_done")
    s.o_T_ready = new("o_T_ready")
    s.AT_done = new("AT_done")
    s.o_recip_ready = new("o_recip_ready")
    s.o_ready = new("o_ready")
    s.AO_done = new("AO_done")
    s.att_T_ready = new("att_T_ready")
    s.O_done = new("O_done")
    s.y_added = new("y_added")
    s.a_bn = new("a_bn")
    s.a_mv = new("a_mv")
    s.a_veps = new("a_veps")
    s.a_nmean = new("a_nmean")
    s.a_rstd = new("a_rstd")
    s.a_nmr = new("a_nmr")
    s.a_norm = new("a_norm")
    s.a_scaled = new("a_scaled")
    s.a_shifted = new("a_shifted")
    s.y_next = new("y_next")
    s.f_base_ready = new("f_base_ready")
    s.f_D_done = new("f_D_done")
    s.f_relu = new("f_relu")
    s.f_H_done = new("f_H_done")
    s.f_sum = new("f_sum")
    s.f_bn1 = new("f_bn1")
    s.f_mv1 = new("f_mv1")
    s.f_veps1 = new("f_veps1")
    s.f_nmean1 = new("f_nmean1")
    s.f_rstd1 = new("f_rstd1")
    s.f_norm1 = new("f_norm1")
    s.f_scaled = new("f_scaled")
    s.f_sum2 = new("f_sum2")
    s.f_bn2 = new("f_bn2")
    s.f_mv2 = new("f_mv2")
    s.f_veps2 = new("f_veps2")
    s.f_nmean2 = new("f_nmean2")
    s.f_rstd2 = new("f_rstd2")
    s.f_nmr2 = new("f_nmr2")
    s.f_out = new("f_out")
    return s



def stage(i, c, back):
    n = G * i + (c - back)
    if isinstance(n, int) and not 0 <= n < ITEMS:
        return None
    return Item(n=n, layer=i + (c - back) // G, g=(c - back) % G)


def slots(eng, slot):
    for c in range(2 + G):
        slot(0, c)
    with eng.Fori(1, DEPTH - 1) as i:
        for c in range(2, 2 + G):
            slot(i, c)
    for c in range(2, 2 + G):
        slot(DEPTH - 1, c)


T_CTX, T_X1, T_X2, T_FFN = 0, 4, 8, 12
M_CTX, M_SELF, M_CROSS = 0, 4, 12
V_CTX, V_SELF = 0, 4
LOADS = 2 * SIDES * 6 * 16



def sync_program(sp, m, s, a):
    tokens = lambda dram, g: dram[GB * g:GB * g + GB].rearrange("b n d -> n b d")
    sp.dma_start(per_batch(m.xr[:, group(0)]), tokens(a.x, 0)).then_inc(s.x_in[0], 16)
    sp.dma_start(per_batch(m.y[:, group(0)]), tokens(a.context, 0)).then_inc(s.ctx_in[0], 16)
    sp.dma_start(m.col[:, :], a.cols).then_inc(s.cols_in, 16)
    sp.dma_start(m.w_att[:, :, :], a.w_att.rearrange("l d c -> d l c")).then_inc(s.w_att_in, 16)
    sp.dma_start(m.row[:, :, :], a.rows.rearrange("r (a d) -> a r d", a=1).to_broadcast([P, NROWS, P])).then_inc(s.rows_in, 16)
    for g in range(1, G):
        sp.dma_start(per_batch(m.y[:, group(g)]), tokens(a.context, g)).then_inc(s.ctx_in[g], 16)
        sp.dma_start(per_batch(m.xr[:, group(g)]), tokens(a.x, g)).then_inc(s.x_in[g], 16)
        if g == 1:
            sp.dma_start(m.w_qkv[:, :, :], a.w_qkv.rearrange("l d c -> d l c")).then_inc(s.w_qkv_in, 16)
    sp.dma_start(m.w_out[:, :, :], a.w_out.rearrange("l d c -> d l c")).then_inc(s.w_out_in, 16)
    sp.dma_start(m.x0[:, :].rearrange("p (b d) -> p b d", d=P), a.x.rearrange("b n d -> n b d")).then_inc(s.x_again, 16)
    sp.dma_start(m.w1[:, :, :], a.w1.rearrange("f d c -> d f c")).then_inc(s.w_ffn_in, 16)
    sp.dma_start(m.w2[:, :, :, :], a.w2.rearrange("f (c h) e -> h f c e", c=FC)).then_inc(s.w_ffn_in, 16)

    for phase in range(2):
        k_parts = (m.kp_self, m.kp_cross)[phase]
        for g in range(G):
            if phase == 0 and g == 0:
                sp.wait_ge(s.F_done, ITEMS)
            if phase == 1 or g >= 2:
                sp.wait_ge(s.ST_done, 2 * (B * phase + GB * (g - 1)))
            sp.wait_ge(s.parts_ready, M_CTX + G if phase else M_SELF + 2 * g + 2)
            for op, parts, order in ((m.k_op, k_parts, K_PARTS), (m.q_op, m.q_parts, Q_PARTS)):
                if phase and op is m.q_op:
                    sp.wait_ge(s.parts_ready, M_CROSS + g + 1)
                for side in range(SIDES):
                    for pair in range(6):
                        to = 64 * side + DH * pair
                        sp.dma_start(op[to:to + DH, g % 2, :, :], parts[64 * side:64 * side + 64, order[pair], group(g)])\
                          .then_inc(s.op_loaded[g % 2], 16)

    for g in range(G):
        sp.wait_ge(s.f_out, G + g + 1)
        sp.dma_start(tokens(a.out, g), per_batch(m.y[:, group(g)])).then_inc(s.stored, 16)
    sp.wait_ge(s.stored, 16 * G)



def gpsimd_program(pool, m, s):
    pool.memset(m.ident[:, :], 0.0).then_inc(s.ident_set, 1)
    pool.memset(m.ident_bf[:, :], 0.0).then_inc(s.ident_bf_set, 1)
    pool.memset(m.minus_half[:, :], -0.5).then_inc(s.half_set, 1)
    pool.wait_ge(s.ident_set, 1)
    pool.affine_select(out=m.ident[:, :], in_=m.ident[:, :], compare_op=ALU.not_equal, fill=1.0, base=0,
                       pattern=[[-1, P]], channel_multiplier=1).then_inc(s.ident_set, 1)
    pool.wait_ge(s.ident_bf_set, 1)
    pool.affine_select(out=m.ident_bf[:, :], in_=m.ident_bf[:, :], compare_op=ALU.not_equal, fill=1.0, base=0,
                       pattern=[[-1, P]], channel_multiplier=1).then_inc(s.ident_bf_set, 1)
    pool.wait_ge(s.half_set, 1)
    pool.wait_ge(s.rows_in, 16)

    def norm(it):
        n, g = it.n, it.g
        wait_apart(pool, s, (s.mv_done, GB * n + GB),
                            (s.xn_ready, n - 3))
        pool.tensor_scalar(m.veps[:, g, :], m.mv[:, g, :, 1], EPS, None, ALU.add).then_inc(s.veps_done, 1)
        pool.tensor_scalar(m.nmean[:, g, :], m.mv[:, g, :, 0], -1.0, None, ALU.mult).then_inc(s.nmean_done, 1)
        pool.wait_ge(s.veps_done, n + 1)
        pool.tensor_tensor(m.rstd[:, g, :], m.veps[:, g, :], m.minus_half[:, :], ALU.pow).then_inc(s.rstd_done, 1)
        wait_apart(pool, s, (s.nmean_done, n + 1), (s.rstd_done, n + 1),
                            (s.T_done, n - 3))
        for b in range(GB):
            last = pool.tensor_scalar(m.xn[:, g, columns(b)], m.xr[:, columns(GB * g + b)],
                                      m.nmean[:, g, b:b + 1], m.rstd[:, g, b:b + 1], ALU.add, ALU.mult)
        last.then_inc(s.xn_ready, 1)
        wait_apart(pool, s, (s.xn_ready, n + 1))
        xg = per_batch(m.xr[:, group(g)])
        pool.tensor_tensor(xg, xg, each_batch(m.row[:, it.layer, :]), ALU.add).then_inc(s.bias_added, 1)

    def middle_part(k, parts):
        pool.wait_ge(s.rest_ready, k + 1)
        pool.tensor_copy(parts, m.rest[:, k % 2, :]).then_inc(s.mid_ready, 1)

    norm(stage(0, 0, 0))
    norm(stage(0, 1, 0))
    for g in range(G):
        middle_part(M_CTX + g, m.kp_cross[:, 1, group(g)])

    def slot(i, c):
        coming = stage(i, c, -2)
        if coming:
            norm(coming)

    slots(pool, slot)

    pool.memset(m.mask_q[:, :, :], 0.0).then_inc(s.mask_set, 1)
    pool.memset(m.mask_k[:, :, :], 0.0).then_inc(s.mask_set, 1)
    pool.memset(m.pick[:, :, :], 0.0).then_inc(s.pick_set, 1)
    pool.memset(m.v_pad[:, :, :, :], 0.0).then_inc(s.v_pad_set, 1)
    pool.memset(m.negmax_parts[:, :, :], 0.0).then_inc(s.parts_set, 1)
    pool.wait_ge(s.mask_set, 2)
    pool.affine_select(out=m.mask_q[:, :, :], in_=m.mask_q[:, :, :], compare_op=ALU.is_ge, fill=MASKED, base=0,
                       pattern=[[0, GB], [-1, P]], channel_multiplier=1).then_inc(s.mask_set, 1)
    pool.affine_select(out=m.mask_k[:, :, :], in_=m.mask_k[:, :, :], compare_op=ALU.is_ge, fill=MASKED, base=0,
                       pattern=[[0, GB], [1, P]], channel_multiplier=-1).then_inc(s.mask_set, 1)
    for k, first in enumerate(64 * side + TILES * part for side in range(SIDES) for part in range(3)):
        pool.wait_ge(s.pick_set, k + 1)
        pool.affine_select(out=m.pick[:, :, :], in_=m.pick[:, :, :], compare_op=ALU.not_equal, fill=1.0, base=-first,
                           pattern=[[-1, TILES], [0, P]], channel_multiplier=1).then_inc(s.pick_set, 1)
    pool.wait_ge(s.v_pad_set, 1)
    pool.memset(m.v_pad[:, :, :, DH:DH + 1], 1.0).then_inc(s.v_pad_set, 1)
    pool.wait_ge(s.v_pad_set, 2)

    for g in range(G):
        pool.wait_ge(s.b1_mv, GB * g + GB)
        if g == 0:
            pool.wait_ge(s.xn_ready, ITEMS)
        pool.tensor_scalar(m.veps[:, g, :], m.mv[:, g, :, 1], EPS, None, ALU.add).then_inc(s.b1_veps, 1)
        pool.tensor_scalar(m.nmean[:, g, :], m.mv[:, g, :, 0], -1.0, None, ALU.mult).then_inc(s.b1_nmean, 1)
        pool.wait_ge(s.b1_veps, g + 1)
        pool.tensor_tensor(m.rstd[:, g, :], m.veps[:, g, :], m.minus_half[:, :], ALU.pow).then_inc(s.b1_rstd, 1)
        pool.wait_ge(s.b1_nmean, g + 1)
        pool.wait_ge(s.b1_rstd, g + 1)
        for b in range(GB):
            last = pool.tensor_scalar(m.x0[:, columns(GB * g + b)], m.xr[:, columns(GB * g + b)],
                                      m.nmean[:, g, b:b + 1], m.rstd[:, g, b:b + 1], ALU.add, ALU.mult)
        last.then_inc(s.x1_ready, 1)
        if g:
            middle_part(M_SELF + 2 * g - 2, m.q_parts[:, 1, group(g - 1)])
            middle_part(M_SELF + 2 * g - 1, m.kp_self[:, 1, group(g - 1)])
        pool.wait_ge(s.x1_ready, g + 1)
        pool.tensor_tensor(per_batch(m.y[:, group(g)]), per_batch(m.x0[:, group(g)]), each_batch(m.row[:, R_SA_BO, :]),
                           ALU.add).then_inc(s.y_ready, 1)
    middle_part(M_SELF + 6, m.q_parts[:, 1, group(3)])
    middle_part(M_SELF + 7, m.kp_self[:, 1, group(3)])

    def attention(phase):
        v = (m.v_self, m.v_cross)[phase]
        r_g, r_bt = ((R_SA_G, R_SA_BT), (R_CA_G, R_CA_BT))[phase]
        with pool.Fori(0, 2) as it:
            n0, g0 = HALF * it + B * phase, 2 * it + G * phase
            for n in range(HALF + 3):
                if n < HALF:
                    if n == 0:
                        pool.wait_ge(s.v_ready, V_SELF + G if phase == 0 else V_CTX + G)
                    if n >= 2:
                        pool.wait_ge(s.PV_done, 2 * n0 + 2 * (n - 1))
                    pool.tensor_copy(m.v_pad[:, n % 2, :, 0:DH],
                                     v[:, bass.ds(HALF * it + n, 1), :].rearrange("p a (h d) -> p (a h) d", d=DH))\
                        .then_inc(s.v_pad_ready, 1)
                if n in (GB + 2, HALF + 2):
                    gg = (n - 2) // GB - 1
                    g = 2 * it + gg
                    yg = m.y[:, group(g)]
                    wait_apart(pool, s, (s.a_mv, GB * g0 + GB * gg + GB))
                    pool.tensor_scalar(m.veps[:, gg, :], m.mv[:, gg, :, 1], EPS, None, ALU.add).then_inc(s.a_veps, 1)
                    pool.tensor_scalar(m.nmean[:, gg, :], m.mv[:, gg, :, 0], -1.0, None, ALU.mult).then_inc(s.a_nmean, 1)
                    pool.wait_ge(s.a_veps, g0 + gg + 1)
                    pool.tensor_tensor(m.rstd[:, gg, :], m.veps[:, gg, :], m.minus_half[:, :], ALU.pow).then_inc(s.a_rstd, 1)
                    pool.wait_ge(s.a_nmean, g0 + gg + 1)
                    pool.wait_ge(s.a_rstd, g0 + gg + 1)
                    pool.tensor_tensor(m.nmr[:, gg, :], m.nmean[:, gg, :], m.rstd[:, gg, :], ALU.mult).then_inc(s.a_nmr, 1)
                if n in (GB + 3, HALF + 2):
                    wait_apart(pool, s, (s.a_norm, g0 + gg + 1))
                    pool.tensor_tensor(per_batch(yg), per_batch(yg), each_batch(m.row[:, r_g, :]), ALU.mult).then_inc(s.a_scaled, 1)
                    wait_apart(pool, s, (s.a_scaled, g0 + gg + 1))
                    pool.tensor_tensor(per_batch(yg), per_batch(yg), each_batch(m.row[:, r_bt, :]), ALU.add).then_inc(s.a_shifted, 1)
            pool.wait_ge(s.PV_done, 2 * n0 + 2 * HALF)

    attention(0)

    for g in range(G):
        middle_part(M_CROSS + g, m.q_parts[:, 1, group(g)])
        pool.wait_ge(s.t_done, T_X2 + g + 1)
        yg = per_batch(m.y[:, group(g)])
        pool.tensor_tensor(yg, yg, each_batch(m.row[:, R_CA_BO, :]), ALU.add).then_inc(s.y_next, 1)

    attention(1)

    for k in range(FFN_ITEMS + 2):
        if k < FFN_ITEMS:
            f, g = k // G, k % G
            yg, xg, bg = (per_batch(t[:, group(g)]) for t in (m.y, m.xr, m.x0))
            if f == 0:
                pool.wait_ge(s.a_shifted, G + g + 1)
            else:
                pool.wait_ge(s.f_out, k - G + 1)
            pool.tensor_tensor(xg, yg, each_batch(m.row[:, R_B2 + 3 * f, :]), ALU.add).then_inc(s.f_base_ready, 1)
            pool.tensor_tensor(bg, bg if f == 0 else yg, each_batch(m.row[:, R_BT + 3 * f, :]), ALU.add).then_inc(s.f_base_ready, 1)
        if 1 <= k <= FFN_ITEMS:
            j, g = k - 1, (k - 1) % G
            pool.wait_ge(s.f_mv1, GB * j + GB)
            pool.tensor_scalar(m.veps[:, g, :], m.mv[:, g, :, 1], EPS, None, ALU.add).then_inc(s.f_veps1, 1)
            pool.tensor_scalar(m.nmean[:, g, :], m.mv[:, g, :, 0], -1.0, None, ALU.mult).then_inc(s.f_nmean1, 1)
            pool.wait_ge(s.f_veps1, j + 1)
            pool.tensor_tensor(m.rstd[:, g, :], m.veps[:, g, :], m.minus_half[:, :], ALU.pow).then_inc(s.f_rstd1, 1)
            pool.wait_ge(s.f_nmean1, j + 1)
            pool.wait_ge(s.f_rstd1, j + 1)
            for b in range(GB):
                xb = m.xr[:, columns(GB * g + b)]
                last = pool.tensor_scalar(xb, xb, m.nmean[:, g, b:b + 1], m.rstd[:, g, b:b + 1], ALU.add, ALU.mult)
            last.then_inc(s.f_norm1, 1)
        if k >= 2:
            j, g = k - 2, (k - 2) % G
            pool.wait_ge(s.f_mv2, GB * j + GB)
            pool.tensor_scalar(m.veps[:, g, :], m.mv[:, g, :, 1], EPS, None, ALU.add).then_inc(s.f_veps2, 1)
            pool.tensor_scalar(m.nmean[:, g, :], m.mv[:, g, :, 0], -1.0, None, ALU.mult).then_inc(s.f_nmean2, 1)
            pool.wait_ge(s.f_veps2, j + 1)
            pool.tensor_tensor(m.rstd[:, g, :], m.veps[:, g, :], m.minus_half[:, :], ALU.pow).then_inc(s.f_rstd2, 1)
            pool.wait_ge(s.f_nmean2, j + 1)
            pool.wait_ge(s.f_rstd2, j + 1)
            pool.tensor_tensor(m.nmr[:, g, :], m.nmean[:, g, :], m.rstd[:, g, :], ALU.mult).then_inc(s.f_nmr2, 1)



def vector_program(dve, m, s):
    pT, pTQ, pQ, pK, pV, pM, pG, pF = m.bank

    def stats(it, first):
        n, g = it.n, it.g
        if first:
            dve.wait_ge(s.x_in[g], 16)
        else:
            wait_apart(dve, s, (s.x_added, n - 3),
                               (s.mv_done, GB * (n - 3)))
        for b in range(GB):
            last = dve.bn_stats(m.bn[:, g, b, :], m.xr[:, columns(GB * g + b)])
        last.then_inc(s.bn_done, 1)
        wait_apart(dve, s, (s.bn_done, n + 1),
                           (s.nmean_done, n - 3), (s.veps_done, n - 3))
        for b in range(GB):
            dve.bn_aggr(m.mv[:, g, b, :], m.bn[:, g, b, :]).then_inc(s.mv_done, 1)

    def first_rest(k, part):
        dve.wait_ge(s.full_ready, k + 1)
        at_least(dve, s.mid_ready, k - 1)
        at_least(dve, s.parts_ready, k - 1)
        dve.tensor_tensor(m.rest[:, k % 2, :], m.full[:, k % 2, :], part, ALU.subtract).then_inc(s.rest_ready, 1)

    def last_part(k, middle, part):
        dve.wait_ge(s.mid_ready, k + 1)
        dve.tensor_tensor(part, m.rest[:, k % 2, :], middle, ALU.subtract).then_inc(s.parts_ready, 1)

    def values(k, v, g, bias):
        dve.wait_ge(s.v_done, k + 1)
        dve.tensor_tensor(v[:, GB * g:GB * g + GB, :], per_batch(m.bank[3]), each_batch(m.row[:, bias, :]), ALU.add)\
           .then_inc(s.v_ready, 1)

    stats(stage(0, 0, 0), True)
    stats(stage(0, 1, 0), True)
    dve.wait_ge(s.cols_in, 16)
    for side in range(2):
        last = dve.tensor_scalar(m.bq[:, side:side + 1], m.col[:, C_BQ + 2 * side:C_BQ + 2 * side + 1], SCALE, None, ALU.mult)
        last.then_inc(s.bq_set, 1)
    dve.wait_ge(s.w_qkv_in, 16)
    dve.tensor_copy(m.wq_now[:, :], m.w_qkv[:, 0, 0:P]).then_inc(s.wq_loaded, 1)
    dve.tensor_copy(m.wv_now[:, :], m.w_qkv[:, 0, 2 * P:3 * P]).then_inc(s.wv_loaded, 1)

    dve.wait_ge(s.rows_in, 16)
    for g in range(G + 1):
        if g < G:
            first_rest(M_CTX + g, m.kp_cross[:, 0, group(g)])
        if g:
            last_part(M_CTX + g - 1, m.kp_cross[:, 1, group(g - 1)], m.kp_cross[:, 2, group(g - 1)])
        if g < G:
            values(V_CTX + g, m.v_cross, g, R_CA_BV)

    def slot(i, c):
        now, one, two, coming = (stage(i, c, back) for back in (0, 1, 2, -2))
        if one:
            n, g = one.n, one.g
            dve.wait_ge(s.ek_ready, n + 1)
            at_least(dve, s.qt_ready, n - 3)
            dve.reciprocal(m.rk[:, g, :], m.ksum[:, g, :]).then_inc(s.rk_ready, 1)
            dve.wait_ge(s.eq_ready, n + 1)
            at_least(dve, s.ms_ready, n - 3)
            dve.reciprocal(m.rq[:, g, :], m.qsum[:, g, :]).then_inc(s.rq_ready, 1)
            dve.wait_ge(s.TQ_done, n + 1)
            dve.wait_ge(s.rk_ready, n + 1)
            at_least(dve, s.M_done, n - 3)
            dve.tensor_tensor(per_batch(m.qt[:, g, :]), per_batch(pTQ), spread(m.rk[:, g, :], P), ALU.mult).then_inc(s.qt_ready, 1)
        if two:
            n, g = two.n, two.g
            dve.wait_ge(s.F_done, n + 1)
            dve.wait_ge(s.bias_added, n + 1)
            dve.tensor_tensor(m.xr[:, group(g)], pF, m.xr[:, group(g)], ALU.add).then_inc(s.x_added, 1)
        if now:
            n, g = now.n, now.g
            if c == G:
                dve.wait_ge(s.V_done, n)
                dve.tensor_copy(m.wv_now[:, :], m.w_qkv[:, now.layer, 2 * P:3 * P]).then_inc(s.wv_loaded, 1)
            dve.wait_ge(s.Q_done, n + 1)
            at_least(dve, s.eq_ready, n - 3)
            dve.tensor_reduce(m.nqmax[:, g, :], per_batch(pQ), AX.X, ALU.max, negate=True).then_inc(s.nqmax_ready, 1)
            after = stage(i, c, -1)
            if c == G - 1 and after:
                dve.tensor_copy(m.wq_now[:, :], m.w_qkv[:, after.layer, 0:P]).then_inc(s.wq_loaded, 1)
        if one:
            n, g = one.n, one.g
            dve.wait_ge(s.M_done, n + 1)
            dve.wait_ge(s.rq_ready, n + 1)
            at_least(dve, s.G_done, n - 3)
            dve.tensor_tensor(per_batch(m.ms[:, g, :]), per_batch(pM), spread(m.rq[:, g, :], P), ALU.mult).then_inc(s.ms_ready, 1)
        if now:
            n, g = now.n, now.g
            dve.wait_ge(s.K_done, n + 1)
            at_least(dve, s.ek_ready, n - 3)
            dve.tensor_reduce(m.nkmax[:, g, :], per_batch(pK), AX.X, ALU.max, negate=True).then_inc(s.nkmax_ready, 1)
        if coming:
            stats(coming, first=isinstance(i, int) and i == 0 and c < 2)

    slots(dve, slot)

    for g in range(G):
        dve.wait_ge(s.x_added, ITEMS - G + g + 1)
        if g == 0:
            dve.wait_ge(s.x_again, 16)
            dve.wait_ge(s.mv_done, GB * ITEMS)
            dve.wait_ge(s.xn_ready, ITEMS)
        dve.tensor_tensor(m.xr[:, group(g)], m.xr[:, group(g)], m.x0[:, group(g)], ALU.add).then_inc(s.b1_sum, 1)
        dve.wait_ge(s.b1_sum, g + 1)
        for b in range(GB):
            last = dve.bn_stats(m.bn[:, g, b, :], m.xr[:, columns(GB * g + b)])
        last.then_inc(s.b1_bn, 1)
        dve.wait_ge(s.b1_bn, g + 1)
        for b in range(GB):
            dve.bn_aggr(m.mv[:, g, b, :], m.bn[:, g, b, :]).then_inc(s.b1_mv, 1)

    dve.wait_ge(s.F_done, ITEMS)
    for g in range(G + 1):
        for w, parts in enumerate((m.q_parts, m.kp_self)):
            k = M_SELF + 2 * g + w
            if g < G:
                first_rest(k, parts[:, 0, group(g)])
            if g < G and k > M_SELF or g == G and w == 0:
                before, gb = (m.kp_self, g - 1) if w == 0 else (m.q_parts, g)
                last_part(k - 1, before[:, 1, group(gb)], before[:, 2, group(gb)])
        if g < G:
            values(V_SELF + g, m.v_self, g, R_SA_BV)

    def attention(phase):
        with dve.Fori(0, 2) as it:
            n0, g0 = HALF * it + B * phase, 2 * it + G * phase

            def maximum(n, u):
                dve.wait_ge(s.S_done, 2 * n0 + 2 * n + u + 1)
                if u == 0:
                    at_least(dve, s.negmax_rest_ready, n0 + n - 1 if n >= 2 else 0)
                dve.tensor_reduce(m.negmax[:, n % 2, :, GB * u:GB * u + GB],
                                  m.pairs[0][:, :].rearrange("p (s j t) -> p s j t", s=SIDES, t=P), AX.X, ALU.max, negate=True)\
                   .then_inc(s.max_done, 1)

            for n in range(HALF + 3):
                if n < HALF:
                    maximum(n, 0)
                if 2 <= n < HALF + 2:
                    k = n - 2
                    o = m.bank[5].rearrange("p (h e) -> p h e", e=VW)
                    dve.wait_ge(s.AT_done, n0 + k + 1)
                    if k >= 2:
                        dve.wait_ge(s.o_ready, n0 + k - 1)
                    dve.reciprocal(m.o_recip[:, k % 2, :].unsqueeze(2), o[:, :, DH:DH + 1]).then_inc(s.o_recip_ready, 1)
                    dve.wait_ge(s.o_recip_ready, n0 + k + 1)
                    if k >= 2:
                        dve.wait_ge(s.AO_done, n0 + k - 1)
                    dve.tensor_tensor(m.o[:, k % 2, :].rearrange("p (h d) -> p h d", d=DH), o[:, :, 0:DH],
                                      spread(m.o_recip[:, k % 2, :], DH), ALU.mult).then_inc(s.o_ready, 1)
                if n < HALF:
                    maximum(n, 1)
                    parts = m.negmax_parts[:, n % 2, :].rearrange("p (s a j) -> p s a j", s=SIDES, j=TILES)
                    neg, rest = m.negmax[:, n % 2, :, :], m.negmax_rest[:, n % 2, :, :]
                    if phase == 0 and n == 0:
                        dve.wait_ge(s.parts_set, 1)
                    dve.wait_ge(s.max_done, 2 * n0 + 2 * n + 2)
                    if n >= 2:
                        dve.wait_ge(s.TM_done, n0 + n - 1)
                    dve.tensor_copy(parts[:, :, 0, :], neg).then_inc(s.negmax_hi, 1)
                    dve.wait_ge(s.negmax_hi, n0 + n + 1)
                    if n >= 2:
                        dve.wait_ge(s.negmax_lo, n0 + n - 1)
                    dve.tensor_tensor(rest, neg, parts[:, :, 0, :], ALU.subtract).then_inc(s.negmax_rest_ready, 1)
                    dve.wait_ge(s.negmax_rest_ready, n0 + n + 1)
                    dve.tensor_copy(parts[:, :, 1, :], rest).then_inc(s.negmax_mid, 1)
                    dve.wait_ge(s.negmax_mid, n0 + n + 1)
                    dve.tensor_tensor(parts[:, :, 2, :], rest, parts[:, :, 1, :], ALU.subtract).then_inc(s.negmax_lo, 1)
                if n in (GB + 2, HALF + 2):
                    gg = (n - 2) // GB - 1
                    g = 2 * it + gg
                    dve.wait_ge(s.O_done, g0 + gg + 1)
                    if phase == 0:
                        dve.wait_ge(s.y_ready, G)
                    else:
                        dve.wait_ge(s.y_next, G)
                    dve.tensor_tensor(m.y[:, group(g)], m.bank[7], m.y[:, group(g)], ALU.add).then_inc(s.y_added, 1)
                    wait_apart(dve, s, (s.y_added, g0 + gg + 1))
                    for b in range(GB):
                        last = dve.bn_stats(m.bn[:, gg, b, :], m.y[:, bass.ds(g * W + b * P, P)])
                    last.then_inc(s.a_bn, 1)
                    wait_apart(dve, s, (s.a_bn, g0 + gg + 1))
                    for b in range(GB):
                        dve.bn_aggr(m.mv[:, gg, b, :], m.bn[:, gg, b, :]).then_inc(s.a_mv, 1)
            dve.wait_ge(s.a_norm, g0 + 2)
            dve.wait_ge(s.negmax_T_ready, n0 + HALF)
            dve.wait_ge(s.AO_done, n0 + HALF)
            dve.wait_ge(s.a_mv, GB * g0 + 2 * GB)
            dve.wait_ge(s.negmax_lo, n0 + HALF)
            dve.wait_ge(s.o_ready, n0 + HALF)

    attention(0)

    for g in range(G + 1):
        if g < G:
            first_rest(M_CROSS + g, m.q_parts[:, 0, group(g)])
        if g:
            last_part(M_CROSS + g - 1, m.q_parts[:, 1, group(g - 1)], m.q_parts[:, 2, group(g - 1)])

    attention(1)

    for k in range(FFN_ITEMS + 1):
        if k < FFN_ITEMS:
            g = k % G
            dve.wait_ge(s.f_D_done, k + 1)
            dve.wait_ge(s.f_base_ready, 2 * k + 2)
            dve.tensor_tensor(m.xr[:, group(g)], m.bank[4 + k % 2], m.xr[:, group(g)], ALU.add).then_inc(s.f_sum, 1)
            dve.wait_ge(s.f_sum, k + 1)
            if k >= G:
                dve.wait_ge(s.f_mv2, GB * (k - G) + GB)
                dve.wait_ge(s.f_nmean2, k - G + 1)
                dve.wait_ge(s.f_veps2, k - G + 1)
            for b in range(GB):
                last = dve.bn_stats(m.bn[:, g, b, :], m.xr[:, columns(GB * g + b)])
            last.then_inc(s.f_bn1, 1)
            dve.wait_ge(s.f_bn1, k + 1)
            for b in range(GB):
                dve.bn_aggr(m.mv[:, g, b, :], m.bn[:, g, b, :]).then_inc(s.f_mv1, 1)
        if k >= 1:
            j, g = k - 1, (k - 1) % G
            dve.wait_ge(s.f_norm1, j + 1)
            xg = per_batch(m.xr[:, group(g)])
            dve.tensor_tensor(xg, xg, each_batch(m.row[:, R_G + 3 * (j // G), :]), ALU.mult).then_inc(s.f_scaled, 1)
            dve.wait_ge(s.f_scaled, j + 1)
            dve.tensor_tensor(m.xr[:, group(g)], m.xr[:, group(g)], m.x0[:, group(g)], ALU.add).then_inc(s.f_sum2, 1)
            dve.wait_ge(s.f_sum2, j + 1)
            dve.wait_ge(s.f_mv1, GB * j + GB)
            for b in range(GB):
                last = dve.bn_stats(m.bn[:, g, b, :], m.xr[:, columns(GB * g + b)])
            last.then_inc(s.f_bn2, 1)
            dve.wait_ge(s.f_bn2, j + 1)
            for b in range(GB):
                dve.bn_aggr(m.mv[:, g, b, :], m.bn[:, g, b, :]).then_inc(s.f_mv2, 1)



def scalar_program(act, m, s):
    pT, pTQ, pQ, pK, pV, pM, pG, pF = m.bank

    def transposed(t):
        act.wait_ge(s.t_done, t + 1)
        act.activation(m.xT[:, t % G, :], m.bank[0], ACT.Copy).then_inc(s.xT_ready, 1)

    def first_part(k, part, bias, scale):
        act.wait_ge(s.proj_done, k + 1)
        at_least(act, s.rest_ready, k - 1)
        act.activation(m.full[:, k % 2, :], m.bank[1 + k % 2], ACT.Identity, bias=bias, scale=scale)
        act.activation(part, m.bank[1 + k % 2], ACT.Identity, bias=bias, scale=scale).then_inc(s.full_ready, 1)

    act.wait_ge(s.cols_in, 16)
    for g in range(G):
        transposed(T_CTX + g)
        first_part(M_CTX + g, m.kp_cross[:, 0, group(g)], m.col[:, C_BK + 2:C_BK + 3], 1.0)

    def slot(i, c):
        now, one = (stage(i, c, back) for back in (0, 1))
        if now:
            n, g = now.n, now.g
            wait_apart(act, s, (s.T_done, n + 1), (s.V_done, n - 3))
            act.activation(m.hT[:, g, :], pT, ACT.Identity, bias=m.col[:, bass.ds(DEPTH + now.layer, 1)],
                           scale=m.col[:, bass.ds(now.layer, 1)]).then_inc(s.hT_ready, 1)
            act.wait_ge(s.nqmax_ready, n + 1)
            at_least(act, s.TQ_done, n - 3)
            at_least(act, s.rq_ready, n - 3)
            for b in range(GB):
                last = act.activation(m.eq[:, g, columns(b)], pQ[:, columns(b)], ACT.Exp, bias=m.nqmax[:, g, b:b + 1],
                                      accum_out=m.qsum[:, g, b:b + 1])
            last.then_inc(s.eq_ready, 1)
            act.wait_ge(s.nkmax_ready, n + 1)
            at_least(act, s.M_done, n - 3)
            at_least(act, s.rk_ready, n - 3)
            for b in range(GB):
                last = act.activation(m.ek[:, g, columns(b)], pK[:, columns(b)], ACT.Exp, bias=m.nkmax[:, g, b:b + 1],
                                      accum_out=m.ksum[:, g, b:b + 1])
            last.then_inc(s.ek_ready, 1)
        if one:
            n, g = one.n, one.g
            act.wait_ge(s.G_done, n + 1)
            at_least(act, s.F_done, n - 3)
            act.activation(m.gs[:, g, :], pG, ACT.Copy).then_inc(s.gs_ready, 1)
        if now:
            n, g = now.n, now.g
            act.wait_ge(s.V_done, n + 1)
            at_least(act, s.F_done, n - 3)
            act.activation(m.vT[:, g, :], pV, ACT.Copy).then_inc(s.vT_ready, 1)

    slots(act, slot)

    act.wait_ge(s.F_done, ITEMS)
    act.wait_ge(s.bq_set, 2)
    for g in range(G):
        transposed(T_X1 + g)
        first_part(M_SELF + 2 * g, m.q_parts[:, 0, group(g)], m.bq[:, 0:1], SCALE)
        first_part(M_SELF + 2 * g + 1, m.kp_self[:, 0, group(g)], m.col[:, C_BK:C_BK + 1], 1.0)

    def attention(phase):
        with act.Fori(0, 2) as it:
            n0, g0 = HALF * it + B * phase, 2 * it + G * phase

            def exponentials(n, u):
                act.wait_ge(s.ST_done, 2 * n0 + 2 * n + u + 1)
                if n >= 1:
                    act.wait_ge(s.PV_done, 2 * n0 + 2 * (n - 1) + u + 1)
                act.activation(m.prob[:, u, :], m.pairs[1][:, :], ACT.Exp).then_inc(s.exp_done, 1)

            for n in range(HALF + 3):
                if 2 <= n < HALF + 2:
                    k = n - 2
                    act.wait_ge(s.PV_done, 2 * n0 + 2 * k + 2)
                    if k >= 1:
                        act.wait_ge(s.AT_done, n0 + k)
                    act.activation(m.o_T[:, :], m.bank[6], ACT.Copy).then_inc(s.o_T_ready, 1)
                if 1 <= n < HALF + 1:
                    exponentials(n - 1, 0)
                    exponentials(n - 1, 1)
                if n < HALF:
                    act.wait_ge(s.TM_done, n0 + n + 1)
                    if n >= 2:
                        act.wait_ge(s.ST_done, 2 * n0 + 2 * (n - 1))
                    act.activation(m.negmax_T[:, n % 2, :], m.bank[4].bitcast(BF16)[:, 0:P], ACT.Copy).then_inc(s.negmax_T_ready, 1)
                if n in (GB + 1, HALF + 1):
                    gg = (n - 1) // GB - 1
                    act.wait_ge(s.AO_done, n0 + GB * gg + GB)
                    if gg:
                        act.wait_ge(s.O_done, g0 + gg)
                    act.activation(m.att_T[:, :], m.bank[7], ACT.Copy).then_inc(s.att_T_ready, 1)
                if n in (GB + 3, HALF + 2):
                    gg = (n - 2) // GB - 1
                    wait_apart(act, s, (s.a_nmr, g0 + gg + 1))
                    for b in range(GB):
                        yb = m.y[:, bass.ds((2 * it + gg) * W + b * P, P)]
                        last = act.activation(yb, yb, ACT.Identity, bias=m.nmr[:, gg, b:b + 1], scale=m.rstd[:, gg, b:b + 1])
                    last.then_inc(s.a_norm, 1)
            act.wait_ge(s.O_done, g0 + 2)

    attention(0)

    for g in range(G):
        transposed(T_X2 + g)
        first_part(M_CROSS + g, m.q_parts[:, 0, group(g)], m.bq[:, 1:2], SCALE)

    attention(1)

    for k in range(FFN_ITEMS + 2):
        if k < FFN_ITEMS:
            f = k // G
            act.wait_ge(s.t_done, T_FFN + k + 1)
            act.activation(m.xT[:, k % G, :], m.bank[6 + k % 2], ACT.Copy).then_inc(s.xT_ready, 1)
            for c in range(FC):
                act.wait_ge(s.f_H_done, FC * k + c + 1)
                if k >= 2:
                    act.wait_ge(s.f_D_done, k - 1)
                act.activation(m.hidden[:, k % 2, c, :], m.bank[c], ACT.Relu, bias=m.col[:, C_B1 + FC * f + c:C_B1 + FC * f + c + 1])\
                   .then_inc(s.f_relu, 1)
        if k >= 2:
            j, g = k - 2, (k - 2) % G
            act.wait_ge(s.f_nmr2, j + 1)
            act.wait_ge(s.t_done, T_FFN + j + 1)
            act.wait_ge(s.f_base_ready, 2 * j + 2)
            for b in range(GB):
                last = act.activation(m.y[:, columns(GB * g + b)], m.xr[:, columns(GB * g + b)], ACT.Identity,
                                      bias=m.nmr[:, g, b:b + 1], scale=m.rstd[:, g, b:b + 1])
            last.then_inc(s.f_out, 1)



def tensor_program(pe, m, s):
    pT, pTQ, pQ, pK, pV, pM, pG, pF = m.bank

    def transpose(t, src, g):
        at_least(pe, s.xT_ready, t)
        for b in range(GB):
            last = pe.transpose(m.bank[0][:, columns(b)], src[:, columns(GB * g + b)], m.ident[:, :])
        last.then_inc(s.t_done, 1)

    def project(k, t, w):
        pe.wait_ge(s.xT_ready, t + 1)
        at_least(pe, s.full_ready, k - 1)
        pe.matmul(m.bank[1 + k % 2], m.w_att[:, w, :], m.xT[:, t % G, :], start=True, stop=True).then_inc(s.proj_done, 1)

    def values(k, t, w):
        at_least(pe, s.v_ready, k)
        for b in range(GB):
            last = pe.matmul(m.bank[3][:, columns(b)], m.xT[:, t % G, columns(b)], m.w_att[:, w, :], start=True, stop=True)
        last.then_inc(s.v_done, 1)

    pe.wait_ge(s.ident_set, 2)
    pe.wait_ge(s.w_att_in, 16)
    for g in range(G + 1):
        if g < G:
            pe.wait_ge(s.ctx_in[g], 16)
            transpose(T_CTX + g, m.y, g)
        if g:
            project(M_CTX + g - 1, T_CTX + g - 1, 5)
            values(V_CTX + g - 1, T_CTX + g - 1, 6)
    pe.wait_ge(s.full_ready, M_CTX + G)
    pe.wait_ge(s.v_ready, V_CTX + G)
    pe.wait_ge(s.w_qkv_in, 16)

    def slot(i, c):
        now, one, two = (stage(i, c, back) for back in (0, 1, 2))
        if now:
            n, g = now.n, now.g
            pe.wait_ge(s.xn_ready, n + 1)
            at_least(pe, s.hT_ready, n)
            for b in range(GB):
                last = pe.transpose(pT[:, columns(b)], m.xn[:, g, columns(b)], m.ident[:, :])
            last.then_inc(s.T_done, 1)
        if one:
            n, g = one.n, one.g
            pe.wait_ge(s.eq_ready, n + 1)
            at_least(pe, s.qt_ready, n)
            for b in range(GB):
                last = pe.transpose(pTQ[:, columns(b)], m.eq[:, g, columns(b)], m.ident[:, :])
            last.then_inc(s.TQ_done, 1)
        if two:
            n, g = two.n, two.g
            pe.wait_ge(s.gs_ready, n + 1)
            pe.wait_ge(s.vT_ready, n + 1)
            at_least(pe, s.x_added, n)
            for b in range(GB):
                last = pe.matmul(pF[:, columns(b)], m.vT[:, g, columns(b)], m.gs[:, g, columns(b)], start=True, stop=True)
            last.then_inc(s.F_done, 1)
        if now:
            n, g = now.n, now.g
            pe.wait_ge(s.hT_ready, n + 1)
            pe.wait_ge(s.wq_loaded, now.layer + 1)
            at_least(pe, s.eq_ready, n)
            pe.matmul(pQ, m.wq_now[:, :], m.hT[:, g, :], start=True, stop=True).then_inc(s.Q_done, 1)
        if one:
            n, g = one.n, one.g
            pe.wait_ge(s.qt_ready, n + 1)
            pe.wait_ge(s.ek_ready, n + 1)
            at_least(pe, s.ms_ready, n)
            for b in range(GB):
                last = pe.matmul(pM[:, columns(b)], m.qt[:, g, columns(b)], m.ek[:, g, columns(b)], start=True, stop=True)
            last.then_inc(s.M_done, 1)
        if now:
            n, g = now.n, now.g
            at_least(pe, s.ek_ready, n)
            for b in range(GB):
                last = pe.matmul(pK[:, columns(b)], m.hT[:, g, columns(b)], m.w_qkv[:, now.layer, P:2 * P], start=True, stop=True)
            last.then_inc(s.K_done, 1)
        if one:
            n, g = one.n, one.g
            if isinstance(i, int) and i == 0 and c == 1:
                pe.wait_ge(s.w_out_in, 16)
            pe.wait_ge(s.ms_ready, n + 1)
            at_least(pe, s.gs_ready, n)
            for b in range(GB):
                last = pe.matmul(pG[:, columns(b)], m.ms[:, g, columns(b)], m.w_out[:, one.layer, :], start=True, stop=True)
            last.then_inc(s.G_done, 1)
        if now:
            n, g = now.n, now.g
            at_least(pe, s.vT_ready, n)
            pe.wait_ge(s.wv_loaded, now.layer + 1)
            pe.matmul(pV, m.wv_now[:, :], m.hT[:, g, :], start=True, stop=True).then_inc(s.V_done, 1)

    slots(pe, slot)

    pe.wait_ge(s.hT_ready, ITEMS)
    pe.wait_ge(s.qt_ready, ITEMS)
    pe.wait_ge(s.ek_ready, ITEMS)
    for g in range(G + 1):
        if g < G:
            pe.wait_ge(s.x1_ready, g + 1)
            transpose(T_X1 + g, m.x0, g)
        if g:
            project(M_SELF + 2 * g - 2, T_X1 + g - 1, 0)
            project(M_SELF + 2 * g - 1, T_X1 + g - 1, 1)
            values(V_SELF + g - 1, T_X1 + g - 1, 2)
    pe.wait_ge(s.full_ready, M_SELF + 2 * G)
    pe.wait_ge(s.v_ready, V_SELF + G)
    pe.wait_ge(s.mask_set, 4)
    pe.wait_ge(s.pick_set, 7)
    pe.wait_ge(s.ident_bf_set, 2)
    pe.wait_ge(s.x_added, ITEMS)
    pe.wait_ge(s.gs_ready, ITEMS)
    pe.wait_ge(s.vT_ready, ITEMS)

    def attention(phase):
        causal = phase == 0
        with pe.Fori(0, 2) as it:
            n0, g0 = HALF * it + B * phase, 2 * it + G * phase

            def scores(n, u, pair, of_keys):
                r, t = n // GB % 2, columns(n % GB)
                left, right = (m.k_op, m.q_op) if of_keys else (m.q_op, m.k_op)
                mask = m.mask_k if of_keys else m.mask_q
                for side in range(SIDES):
                    if causal:
                        pe.matmul(pair[:, side * W:side * W + W], m.ident_bf[:, :], mask[:, :, :], start=True, stop=False,
                                  skip_group_check=True)
                for jj in range(GB):
                    for side in range(SIDES):
                        rows = slice(64 * side, 64 * side + ROWS)
                        j = GB * u + jj
                        to = pair[:, side * W + jj * P:side * W + jj * P + P]
                        last = pe.matmul(to, left[rows, r, j, t], right[rows, r, j, t], start=not causal, stop=not of_keys,
                                         skip_group_check=True)
                        if of_keys:
                            rows = slice(64 * side, 64 * side + 3 * TILES)
                            last = pe.matmul(to, m.pick[rows, j, :], m.negmax_T[rows, n % 2, :], start=False, stop=True,
                                             skip_group_check=True)
                return last

            def weighted(n, u):
                for side in range(SIDES):
                    for jj in range(GB):
                        h = TILES * side + GB * u + jj
                        at = 2 * side + u
                        last = pe.matmul(m.bank[6][VW * jj:VW * jj + VW, columns(at)], m.v_pad[:, n % 2, h, :],
                                         m.prob[:, u, side * W + jj * P:side * W + jj * P + P], start=True, stop=True)
                last.then_inc(s.PV_done, 1)

            for n in range(HALF + 3):
                if n < HALF:
                    if n % GB == 0:
                        pe.wait_ge(s.op_loaded[n // GB], LOADS * it + LOADS * (2 * phase + 1))
                    if n:
                        pe.wait_ge(s.max_done, 2 * n0 + 2 * n)
                    scores(n, 0, m.pairs[0], False).then_inc(s.S_done, 1)
                if n in (GB + 2, HALF + 2):
                    gg = (n - 2) // GB - 1
                    pe.wait_ge(s.att_T_ready, g0 + gg + 1)
                    for b in range(GB):
                        last = pe.matmul(m.bank[7][:, columns(b)], m.att_T[:, columns(b)], m.w_att[:, 4 * phase + 3, :],
                                         start=True, stop=True)
                    last.then_inc(s.O_done, 1)
                if 2 <= n < HALF + 2:
                    pe.wait_ge(s.exp_done, 2 * n0 + 2 * (n - 2) + 2)
                    weighted(n - 2, 1)
                if 1 <= n < HALF + 1:
                    pe.wait_ge(s.negmax_T_ready, n0 + n)
                    if n >= 2:
                        pe.wait_ge(s.exp_done, 2 * n0 + 2 * (n - 1))
                    scores(n - 1, 0, m.pairs[1], True).then_inc(s.ST_done, 1)
                if n < HALF:
                    pe.wait_ge(s.max_done, 2 * n0 + 2 * n + 1)
                    scores(n, 1, m.pairs[0], False).then_inc(s.S_done, 1)
                if 2 <= n < HALF + 2:
                    k = n - 2
                    pe.wait_ge(s.o_T_ready, n0 + k + 1)
                    if k:
                        pe.wait_ge(s.o_ready, n0 + k)
                    for at in range(GB):
                        last = pe.transpose(m.bank[5][:, columns(at)], m.o_T[:, columns(at)], m.ident[:, :])
                    last.then_inc(s.AT_done, 1)
                if 1 <= n < HALF + 1:
                    pe.wait_ge(s.exp_done, 2 * n0 + 2 * (n - 1) + 1)
                    scores(n - 1, 1, m.pairs[1], True).then_inc(s.ST_done, 1)
                    pe.wait_ge(s.v_pad_ready, n0 + n)
                    if n >= 2:
                        pe.wait_ge(s.o_T_ready, n0 + n - 1)
                    weighted(n - 1, 0)
                if n < HALF:
                    pe.wait_ge(s.negmax_lo, n0 + n + 1)
                    if n:
                        pe.wait_ge(s.negmax_T_ready, n0 + n)
                    pe.transpose(m.bank[4].bitcast(BF16)[:, 0:P], m.negmax_parts[:, n % 2, :], m.ident_bf[:, :]).then_inc(s.TM_done, 1)
                if 2 <= n < HALF + 2:
                    k = n - 2
                    pe.wait_ge(s.o_ready, n0 + k + 1)
                    if k == GB:
                        pe.wait_ge(s.y_added, g0 + 1)
                    last = pe.transpose(m.bank[7][:, columns(k % GB)], m.o[:, k % 2, :], m.ident[:, :])
                    last.then_inc(s.AO_done, 1)
            pe.wait_ge(s.y_added, g0 + 2)

    attention(0)

    for g in range(G + 1):
        if g < G:
            pe.wait_ge(s.a_shifted, g + 1)
            transpose(T_X2 + g, m.y, g)
        if g:
            project(M_CROSS + g - 1, T_X2 + g - 1, 4)
    pe.wait_ge(s.full_ready, M_CROSS + G)

    attention(1)

    pe.wait_ge(s.w_ffn_in, 32)
    for k in range(FFN_ITEMS + 1):
        if k < FFN_ITEMS:
            f, g = k // G, k % G
            if f == 0:
                pe.wait_ge(s.a_shifted, G + g + 1)
            else:
                pe.wait_ge(s.f_out, g + 1)
            if k >= 2:
                pe.wait_ge(s.xT_ready, T_FFN + k - 1)
            for b in range(GB):
                last = pe.transpose(m.bank[6 + k % 2][:, columns(b)], m.y[:, columns(GB * g + b)], m.ident[:, :])
            last.then_inc(s.t_done, 1)
        if k:
            j = k - 1
            pe.wait_ge(s.f_relu, FC * j + FC)
            if j >= 2:
                pe.wait_ge(s.f_sum, j - 1)
            for b in range(GB):
                for c in range(FC):
                    last = pe.matmul(m.bank[4 + j % 2][:, columns(b)], m.hidden[:, j % 2, c, columns(b)], m.w2[:, j // G, c, :],
                                     start=c == 0, stop=c == FC - 1)
            last.then_inc(s.f_D_done, 1)
        if k < FFN_ITEMS:
            pe.wait_ge(s.xT_ready, T_FFN + k + 1)
            for c in range(FC):
                at_least(pe, s.f_relu, FC * (k - 1) + c + 1)
                pe.matmul(m.bank[c], m.w1[:, f, columns(c)], m.xT[:, g, :], start=True, stop=True).then_inc(s.f_H_done, 1)


def decoder_kernel(nc, x, context, w_qkv, w_out, w_att, w1, w2, rows, cols, out):
    a = Names()
    a.x, a.context, a.w_qkv, a.w_out, a.w_att, a.w1, a.w2, a.rows, a.cols, a.out = \
        x, context, w_qkv, w_out, w_att, w1, w2, rows, cols, out
    with ExitStack() as ctx:
        m = allocate(nc, ctx)
        s = semaphores(nc, ctx)
        block = ctx.enter_context(nc.Block())

        @block.sync
        def _(sp):
            sync_program(sp, m, s, a)

        @block.gpsimd
        def _(pool):
            gpsimd_program(pool, m, s)

        @block.vector
        def _(dve):
            vector_program(dve, m, s)

        @block.scalar
        def _(act):
            scalar_program(act, m, s)

        @block.tensor
        def _(pe):
            tensor_program(pe, m, s)



def kernel(**inputs):
    import numpy as _np
    import concourse.bacc as _bacc
    from concourse import mybir as _mybir
    from concourse.bass_utils import run_bass_kernel_spmd as _run

    def by_feature(w):
        w = _np.asarray(w)
        return w.reshape(w.shape[:-1] + (SIDES, TILES, DH)).swapaxes(-1, -2).reshape(w.shape)

    v = {k: _np.asarray(a) for k, a in inputs.items()}
    att, xat, ffn = "L0_attn_", "L0_xattn_", "L0_ffn_"
    arrays = {
        "x": v["x"],
        "context": v["ctx_1024"],
        "w_qkv": v[att + "w_qkv"],
        "w_out": v[att + "w_out"],
        "w_att": _np.stack([by_feature(v[f"{xat}{p}_w{n}"]) if n in "qk" else v[f"{xat}{p}_w{n}"]
                            for p in ("sa", "ca") for n in "qkvo"]),
        "w1": _np.stack([v[xat + "f_w1"], v[ffn + "w1"][0]]),
        "w2": _np.stack([v[xat + "f_w2"], v[ffn + "w2"][0]]),
        "rows": _np.concatenate([v[att + "b_out"]] + [v[f"{xat}{p}_{n}"][None] for p in ("sa", "ca") for n in ("bv", "bo", "g", "bt")]
                                + [v[xat + n][None] for n in ("f_b2", "f_g", "f_bt")]
                                + [v[ffn + "b2"][0:1], v[ffn + "gamma"][None], v[ffn + "beta"][None]]),
        "cols": _np.concatenate([v[att + "gamma"].T, v[att + "beta"].T]
                                + [by_feature(v[f"{xat}{p}_b{n}"])[:, None] for p in ("sa", "ca") for n in "qk"]
                                + [v[xat + "f_b1"].reshape(FC, P).T, v[ffn + "b1"][0].reshape(FC, P).T], axis=1),
    }
    nc = _bacc.Bacc("TRN2", target_bir_lowering=False, num_devices=1)
    args = []
    arrays = {f"in_{name}": _np.ascontiguousarray(array) for name, array in arrays.items()}
    for name, array in arrays.items():
        args.append(nc.dram_tensor(name, array.shape, _mybir.dt.from_np(array.dtype), kind="ExternalInput").ap())
    args.append(nc.dram_tensor("out", (B, P, P), _mybir.dt.float32, kind="ExternalOutput").ap())
    decoder_kernel(nc, *args)
    r = _run(nc, [arrays], core_ids=[0])
    return r.results[0]["out"]
```

```python
from contextlib import ExitStack

import numpy as np

import concourse.bass as bass
from concourse import mybir

F32 = mybir.dt.float32
BF16 = mybir.dt.bfloat16
ALU = mybir.AluOpType
ACT = mybir.ActivationFunctionType
AX = mybir.AxisListType

P = 128
B = 16
DEPTH = 6
GB = 4
G = B // GB
W = GB * P
ITEMS = DEPTH * G
EPS = 1e-5

H = 16
DH = P // H
SIDES, TILES = 2, H // 2
PAIRS = 6
ROWS = PAIRS * DH
Q_PARTS = (0, 0, 0, 1, 1, 2)
K_PARTS = (0, 1, 2, 0, 1, 0)
OP = SIDES * ROWS
MAX_ROWS = slice(OP, OP + 3)
UNITS = 4
UT = TILES // UNITS
HALF = 2 * GB
ALL = 2 * B
VW = 32
MASKED = -3.0e38
SCALE = float(1.0 / np.sqrt(np.float32(DH)))

FC = 4
FFN_ITEMS = 2 * G

R_SA_BV, R_SA_BO, R_SA_G, R_SA_BT, R_CA_BV, R_CA_BO, R_CA_G, R_CA_BT = range(DEPTH, DEPTH + 8)
R_B2, R_G, R_BT = DEPTH + 8, DEPTH + 9, DEPTH + 10
NROWS = DEPTH + 14
C_BQ, C_BK, C_B1 = 2 * DEPTH, 2 * DEPTH + 1, 2 * DEPTH + 4
NCOLS = 2 * DEPTH + 4 + 2 * FC


class Names:
    pass


class Item:

    def __init__(self, n, layer, g):
        self.n, self.layer, self.g = n, layer, g


def at_least(eng, sem, count):
    if isinstance(count, int) and count <= 0:
        return
    eng.wait_ge(sem, count)


def wait_apart(eng, s, *waits):
    waits = [(sem, count if isinstance(count, int) else eng.snap(eng.to_reg(count))) for sem, count in waits]
    eng.wait_ge(s.ident_set, 2)
    for sem, count in waits:
        at_least(eng, sem, count)


def per_batch(ap):
    return ap.rearrange("p (b t) -> p b t", t=P)


def spread(ap, n):
    return ap.unsqueeze(2).to_broadcast([ap.shape[0], ap.shape[1], n])


def each_batch(ap, n=GB):
    return ap.unsqueeze(1).to_broadcast([ap.shape[0], n, ap.shape[1]])


def columns(b):
    return slice(b * P, b * P + P)


def group(g):
    return bass.ds(g * W, W)



def allocate(nc, ctx):
    def sb(name, shape, dt=F32):
        return ctx.enter_context(nc.sbuf_tensor(name, shape, dt))

    m = Names()
    m.x0 = sb("x0", [P, B * P])
    m.xr = sb("xr", [P, B * P])
    m.y = sb("y", [P, B * P])
    m.w_qkv = sb("w_qkv", [P, DEPTH, 3 * P])
    m.w_out = sb("w_out", [P, DEPTH, P])
    m.w_att = sb("w_att", [P, 8, P])
    m.w1 = sb("w1", [P, 2, FC * P])
    m.w2 = sb("w2", [P, 2, FC, P])
    m.row = sb("row", [P, NROWS, P])
    m.col = sb("col", [P, NCOLS])
    m.bq = sb("bq", [P, 2])
    m.ident = sb("ident", [P, P])
    m.ident_bf = sb("ident_bf", [P, P], BF16)
    m.mask = sb("mask", [P, GB, P], BF16)
    m.minus_half = sb("minus_half", [P, GB])
    m.wq_now = sb("wq_now", [P, P])
    m.wv_now = sb("wv_now", [P, P])
    m.bn = sb("bn", [P, G, GB, 6])
    m.mv = sb("mv", [P, G, GB, 2])
    m.veps = sb("veps", [P, G, GB])
    m.rstd = sb("rstd", [P, G, GB])
    m.nmean = sb("nmean", [P, G, GB])
    m.nmr = sb("nmr", [P, G, GB])
    m.nqmax = sb("nqmax", [P, G, GB])
    m.nkmax = sb("nkmax", [P, G, GB])
    m.qsum = sb("qsum", [P, G, GB])
    m.ksum = sb("ksum", [P, G, GB])
    m.rq = sb("rq", [P, G, GB])
    m.rk = sb("rk", [P, G, GB])
    m.xT = sb("xT", [P, G, W])
    m.full = sb("full", [P, 2, W])
    m.rest = sb("rest", [P, 2, W])
    m.kp_cross = sb("kp_cross", [P, 3, B * P], BF16)
    m.v_self = sb("v_self", [P, B, P])
    m.v_cross = sb("v_cross", [P, B, P])
    m.v_pad = sb("v_pad", [P, 2, H, VW])
    m.negmax = sb("negmax", [P, 2, TILES * SIDES])
    m.negmax_rest = sb("negmax_rest", [P, 2, TILES * SIDES])
    m.negmax_parts = sb("negmax_parts", [P, 2, 3 * H], BF16)
    m.negmax_T = sb("negmax_T", [3 * H, 2, P], BF16)
    m.o_T = sb("o_T", [P, W])
    m.o_recip = sb("o_recip", [P, 2, H])
    m.o = sb("o", [P, 2, P])
    m.att_T = sb("att_T", [P, W])
    arena = sb("arena", [P, 11 * G * W])
    eighth = lambda k: arena[:, (k + 3) * G * W:(k + 4) * G * W].rearrange("p (g w) -> p g w", w=W)
    m.ek, m.qt, m.ms, m.xn, m.hT, m.eq, m.gs, m.vT = (eighth(k) for k in range(8))
    half = arena[:, :].bitcast(BF16)
    q_size, k_size, parts_size = TILES * SIDES * W, TILES * W, 3 * B * P
    m.q_op = [half[:, r * (q_size + k_size):r * (q_size + k_size) + q_size]
              .rearrange("p (j s t) -> p j s t", s=SIDES, t=W) for r in range(2)]
    m.k_op = [half[:, r * (q_size + k_size) + q_size:(r + 1) * (q_size + k_size)]
              .rearrange("p (j t) -> p j t", t=W) for r in range(2)]
    m.q_zero = arena[:, 0:q_size // 2]
    at = 2 * (q_size + k_size)
    m.q_parts = half[:, at:at + parts_size].rearrange("p (a t) -> p a t", a=3)
    m.kp_self = half[:, at + parts_size:at + 2 * parts_size].rearrange("p (a t) -> p a t", a=3)
    at = at // 2 + parts_size
    m.prob = arena[:, at:at + UNITS * W].rearrange("p (u t) -> p u t", u=UNITS)
    m.hidden = arena[:, 0:2 * FC * W].rearrange("p (r c t) -> p r c t", r=2, c=FC)
    m.bank = [ctx.enter_context(nc.psum_tensor(f"bank{n}", [P, W], F32))[:, :] for n in range(8)]
    return m


def semaphores(nc, ctx):
    s = Names()

    def new(name):
        return ctx.enter_context(nc.semaphore(name))

    s.x_in = [new(f"x_in{g}") for g in range(G)]
    s.ctx_in = [new(f"ctx_in{g}") for g in range(G)]
    s.op_loaded = [new(f"op_loaded{r}") for r in range(2)]
    s.max_loaded = [new(f"max_loaded{r}") for r in range(2)]
    s.spilled = [new(f"spilled{j}") for j in range(2 * G)]
    s.x_again = new("x_again")
    s.cols_in = new("cols_in")
    s.rows_in = new("rows_in")
    s.w_att_in = new("w_att_in")
    s.w_qkv_in = new("w_qkv_in")
    s.w_out_in = new("w_out_in")
    s.w_ffn_in = new("w_ffn_in")
    s.stored = new("stored")
    s.ident_set = new("ident_set")
    s.ident_bf_set = new("ident_bf_set")
    s.half_set = new("half_set")
    s.mask_set = new("mask_set")
    s.v_pad_set = new("v_pad_set")
    s.zero_set = new("zero_set")
    s.ones_set = new("ones_set")
    s.ring_set = new("ring_set")
    s.bq_set = new("bq_set")
    s.bn_done = new("bn_done")
    s.mv_done = new("mv_done")
    s.veps_done = new("veps_done")
    s.rstd_done = new("rstd_done")
    s.nmean_done = new("nmean_done")
    s.xn_ready = new("xn_ready")
    s.bias_added = new("bias_added")
    s.T_done = new("T_done")
    s.hT_ready = new("hT_ready")
    s.wq_loaded = new("wq_loaded")
    s.wv_loaded = new("wv_loaded")
    s.Q_done = new("Q_done")
    s.K_done = new("K_done")
    s.V_done = new("V_done")
    s.TQ_done = new("TQ_done")
    s.M_done = new("M_done")
    s.G_done = new("G_done")
    s.F_done = new("F_done")
    s.nqmax_ready = new("nqmax_ready")
    s.nkmax_ready = new("nkmax_ready")
    s.eq_ready = new("eq_ready")
    s.ek_ready = new("ek_ready")
    s.rq_ready = new("rq_ready")
    s.rk_ready = new("rk_ready")
    s.qt_ready = new("qt_ready")
    s.ms_ready = new("ms_ready")
    s.gs_ready = new("gs_ready")
    s.vT_ready = new("vT_ready")
    s.x_added = new("x_added")
    s.b1_sum = new("b1_sum")
    s.b1_bn = new("b1_bn")
    s.b1_mv = new("b1_mv")
    s.b1_veps = new("b1_veps")
    s.b1_nmean = new("b1_nmean")
    s.b1_rstd = new("b1_rstd")
    s.x1_ready = new("x1_ready")
    s.y_ready = new("y_ready")
    s.t_done = new("t_done")
    s.xT_ready = new("xT_ready")
    s.proj_done = new("proj_done")
    s.full_ready = new("full_ready")
    s.rest_ready = new("rest_ready")
    s.mid_ready = new("mid_ready")
    s.parts_ready = new("parts_ready")
    s.v_done = new("v_done")
    s.v_ready = new("v_ready")
    s.v_pad_ready = new("v_pad_ready")
    s.S_done = new("S_done")
    s.max_done = new("max_done")
    s.negmax_hi = new("negmax_hi")
    s.negmax_rest_ready = new("negmax_rest_ready")
    s.negmax_mid = new("negmax_mid")
    s.negmax_lo = new("negmax_lo")
    s.TM_done = new("TM_done")
    s.negmax_T_ready = new("negmax_T_ready")
    s.ST_done = new("ST_done")
    s.exp_done = new("exp_done")
    s.prob_masked = new("prob_masked")
    s.PV_done = new("PV_done")
    s.o_T_ready = new("o_T_ready")
    s.AT_done = new("AT_done")
    s.o_recip_ready = new("o_recip_ready")
    s.o_ready = new("o_ready")
    s.AO_done = new("AO_done")
    s.att_T_ready = new("att_T_ready")
    s.O_done = new("O_done")
    s.y_added = new("y_added")
    s.a_bn = new("a_bn")
    s.a_mv = new("a_mv")
    s.a_veps = new("a_veps")
    s.a_nmean = new("a_nmean")
    s.a_rstd = new("a_rstd")
    s.a_nmr = new("a_nmr")
    s.a_norm = new("a_norm")
    s.a_scaled = new("a_scaled")
    s.a_shifted = new("a_shifted")
    s.y_next = new("y_next")
    s.f_base_ready = new("f_base_ready")
    s.f_D_done = new("f_D_done")
    s.f_relu = new("f_relu")
    s.f_H_done = new("f_H_done")
    s.f_sum = new("f_sum")
    s.f_bn1 = new("f_bn1")
    s.f_mv1 = new("f_mv1")
    s.f_veps1 = new("f_veps1")
    s.f_nmean1 = new("f_nmean1")
    s.f_rstd1 = new("f_rstd1")
    s.f_norm1 = new("f_norm1")
    s.f_scaled = new("f_scaled")
    s.f_sum2 = new("f_sum2")
    s.f_bn2 = new("f_bn2")
    s.f_mv2 = new("f_mv2")
    s.f_veps2 = new("f_veps2")
    s.f_nmean2 = new("f_nmean2")
    s.f_rstd2 = new("f_rstd2")
    s.f_nmr2 = new("f_nmr2")
    s.f_out = new("f_out")
    return s



def stage(i, c, back):
    n = G * i + (c - back)
    if isinstance(n, int) and not 0 <= n < ITEMS:
        return None
    return Item(n=n, layer=i + (c - back) // G, g=(c - back) % G)


def slots(eng, slot):
    for c in range(2 + G):
        slot(0, c)
    with eng.Fori(1, DEPTH - 1) as i:
        for c in range(2, 2 + G):
            slot(i, c)
    for c in range(2, 2 + G):
        slot(DEPTH - 1, c)


T_CTX, T_X1, T_X2, T_FFN = 0, 4, 8, 12
M_CTX, M_SELF, M_CROSS = 0, 4, 12
V_CTX, V_SELF = 0, 4
PROJ = (2, 4)
SPILLS = 2 * SIDES * 3 * 16
LOADS = 3 * 16



def sync_program(sp, m, s, a):
    tokens = lambda dram, g: dram[GB * g:GB * g + GB].rearrange("b n d -> n b d")
    sp.dma_start(per_batch(m.xr[:, group(0)]), tokens(a.x, 0)).then_inc(s.x_in[0], 16)
    sp.dma_start(per_batch(m.y[:, group(0)]), tokens(a.context, 0)).then_inc(s.ctx_in[0], 16)
    sp.dma_start(m.col[:, :], a.cols).then_inc(s.cols_in, 16)
    sp.dma_start(m.w_att[:, :, :], a.w_att.rearrange("l d c -> d l c")).then_inc(s.w_att_in, 16)
    sp.dma_start(m.row[:, :, :], a.rows.rearrange("r (a d) -> a r d", a=1).to_broadcast([P, NROWS, P])).then_inc(s.rows_in, 16)
    for g in range(1, G):
        sp.dma_start(per_batch(m.y[:, group(g)]), tokens(a.context, g)).then_inc(s.ctx_in[g], 16)
        sp.dma_start(per_batch(m.xr[:, group(g)]), tokens(a.x, g)).then_inc(s.x_in[g], 16)
        if g == 1:
            sp.dma_start(m.w_qkv[:, :, :], a.w_qkv.rearrange("l d c -> d l c")).then_inc(s.w_qkv_in, 16)
    sp.dma_start(m.w_out[:, :, :], a.w_out.rearrange("l d c -> d l c")).then_inc(s.w_out_in, 16)
    sp.dma_start(m.x0[:, :].rearrange("p (b d) -> p b d", d=P), a.x.rearrange("b n d -> n b d")).then_inc(s.x_again, 16)
    sp.dma_start(m.w1[:, :, :], a.w1.rearrange("f d c -> d f c")).then_inc(s.w_ffn_in, 16)
    sp.dma_start(m.w2[:, :, :, :], a.w2.rearrange("f (c h) e -> h f c e", c=FC)).then_inc(s.w_ffn_in, 16)

    def spill(j, scratch, parts, order):
        for side in range(SIDES):
            to = scratch[j, side].rearrange("a (f i) t -> (f i) a t", i=TILES)
            first = 0
            while first < PAIRS:
                step = order[first + 1] - order[first] if first + 1 < PAIRS else 0
                last = first
                while last + 1 < PAIRS and order[last + 1] - order[last] == step and step >= 0:
                    last += 1
                n, source = last + 1 - first, parts[64 * side:64 * side + 64, :, group(j % G)]
                source = source[:, order[first]:order[first] + n, :] if step == 1 else \
                    source[:, order[first]:order[first] + 1, :].to_broadcast([64, n, W])
                sp.dma_start(to[:, first:first + n, :], source).then_inc(s.spilled[j], 16)
                first = last + 1

    def load(j):
        ring = j % 2
        sp.wait_ge(s.spilled[j], SPILLS)
        for side in range(SIDES):
            sp.dma_start(m.q_op[ring][side * ROWS:side * ROWS + ROWS, :, side, :],
                         a.q_rows[j, side].rearrange("a (f i) t -> (a f) i t", i=TILES)).then_inc(s.op_loaded[ring], 16)
        sp.dma_start(m.k_op[ring][0:OP, :, :], a.k_rows[j].rearrange("s a (f i) t -> (s a f) i t", i=TILES))\
          .then_inc(s.op_loaded[ring], 16)

    for g in range(G):
        sp.wait_ge(s.parts_ready, M_CTX + g + 1)
        spill(G + g, a.k_rows, m.kp_cross, K_PARTS)
    sp.wait_ge(s.G_done, ITEMS)
    sp.wait_ge(s.zero_set, 1)
    sp.wait_ge(s.ones_set, 1)
    sp.dma_start(m.q_op[1][0:OP, :, :, :], m.q_op[0][0:OP, :, :, :]).then_inc(s.ring_set, 16)
    sp.dma_start(m.k_op[1][MAX_ROWS, :, :], m.k_op[0][MAX_ROWS, :, :]).then_inc(s.ring_set, 16)
    for g in range(G):
        sp.wait_ge(s.parts_ready, M_SELF + 2 * g + 2)
        spill(g, a.k_rows, m.kp_self, K_PARTS)
        spill(g, a.q_rows, m.q_parts, Q_PARTS)
        if g == 0:
            sp.wait_ge(s.ring_set, 32)
        if g < 2:
            load(g)
    for j in range(2, 2 * G):
        if j >= G:
            sp.wait_ge(s.parts_ready, M_CROSS + j - G + 1)
            spill(j, a.q_rows, m.q_parts, Q_PARTS)
        sp.wait_ge(s.ST_done, UNITS * GB * (j - 1))
        load(j)

    for g in range(G):
        sp.wait_ge(s.f_out, G + g + 1)
        sp.dma_start(tokens(a.out, g), per_batch(m.y[:, group(g)])).then_inc(s.stored, 16)
    sp.wait_ge(s.stored, 16 * G)



def gpsimd_program(pool, m, s):
    pool.memset(m.ident[:, :], 0.0).then_inc(s.ident_set, 1)
    pool.memset(m.ident_bf[:, :], 0.0).then_inc(s.ident_bf_set, 1)
    pool.memset(m.minus_half[:, :], -0.5).then_inc(s.half_set, 1)
    pool.wait_ge(s.ident_set, 1)
    pool.affine_select(out=m.ident[:, :], in_=m.ident[:, :], compare_op=ALU.not_equal, fill=1.0, base=0,
                       pattern=[[-1, P]], channel_multiplier=1).then_inc(s.ident_set, 1)
    pool.wait_ge(s.ident_bf_set, 1)
    pool.affine_select(out=m.ident_bf[:, :], in_=m.ident_bf[:, :], compare_op=ALU.not_equal, fill=1.0, base=0,
                       pattern=[[-1, P]], channel_multiplier=1).then_inc(s.ident_bf_set, 1)
    pool.wait_ge(s.half_set, 1)
    pool.wait_ge(s.rows_in, 16)

    def norm(it):
        n, g = it.n, it.g
        wait_apart(pool, s, (s.mv_done, GB * n + GB),
                            (s.xn_ready, n - 3))
        pool.tensor_scalar(m.veps[:, g, :], m.mv[:, g, :, 1], EPS, None, ALU.add).then_inc(s.veps_done, 1)
        pool.tensor_scalar(m.nmean[:, g, :], m.mv[:, g, :, 0], -1.0, None, ALU.mult).then_inc(s.nmean_done, 1)
        pool.wait_ge(s.veps_done, n + 1)
        pool.tensor_tensor(m.rstd[:, g, :], m.veps[:, g, :], m.minus_half[:, :], ALU.pow).then_inc(s.rstd_done, 1)
        wait_apart(pool, s, (s.nmean_done, n + 1), (s.rstd_done, n + 1),
                            (s.T_done, n - 3))
        for b in range(GB):
            last = pool.tensor_scalar(m.xn[:, g, columns(b)], m.xr[:, columns(GB * g + b)],
                                      m.nmean[:, g, b:b + 1], m.rstd[:, g, b:b + 1], ALU.add, ALU.mult)
        last.then_inc(s.xn_ready, 1)
        wait_apart(pool, s, (s.xn_ready, n + 1))
        xg = per_batch(m.xr[:, group(g)])
        pool.tensor_tensor(xg, xg, each_batch(m.row[:, it.layer, :]), ALU.add).then_inc(s.bias_added, 1)

    def middle_part(k, parts):
        pool.wait_ge(s.rest_ready, k + 1)
        pool.tensor_copy(parts, m.rest[:, k % 2, :]).then_inc(s.mid_ready, 1)

    norm(stage(0, 0, 0))
    norm(stage(0, 1, 0))
    for g in range(G):
        middle_part(M_CTX + g, m.kp_cross[:, 1, group(g)])

    def slot(i, c):
        coming = stage(i, c, -2)
        if coming:
            norm(coming)
        if not isinstance(i, int) or i:
            return
        if c == 0:
            pool.memset(m.mask[:, :, :], 0.0).then_inc(s.mask_set, 1)
            pool.wait_ge(s.mask_set, 1)
            pool.affine_select(out=m.mask[:, :, :], in_=m.mask[:, :, :], compare_op=ALU.is_ge, fill=MASKED, base=0,
                               pattern=[[0, GB], [-1, P]], channel_multiplier=1).then_inc(s.mask_set, 1)
        if c == 1:
            pool.memset(m.v_pad[:, :, :, :], 0.0).then_inc(s.v_pad_set, 1)
            pool.wait_ge(s.v_pad_set, 1)
            pool.memset(m.v_pad[:, :, :, DH:DH + 1], 1.0).then_inc(s.v_pad_set, 1)
        if c == 2:
            pool.memset(m.q_zero, 0.0).then_inc(s.zero_set, 1)
        if c == 3:
            pool.wait_ge(s.bias_added, coming.n + 1)
            pool.memset(m.k_op[0][MAX_ROWS, :, :], 1.0).then_inc(s.ones_set, 1)
            pool.wait_ge(s.ones_set, 1)

    slots(pool, slot)

    for g in range(G):
        pool.wait_ge(s.b1_mv, GB * g + GB)
        if g == 0:
            pool.wait_ge(s.xn_ready, ITEMS)
        pool.tensor_scalar(m.veps[:, g, :], m.mv[:, g, :, 1], EPS, None, ALU.add).then_inc(s.b1_veps, 1)
        pool.tensor_scalar(m.nmean[:, g, :], m.mv[:, g, :, 0], -1.0, None, ALU.mult).then_inc(s.b1_nmean, 1)
        pool.wait_ge(s.b1_veps, g + 1)
        pool.tensor_tensor(m.rstd[:, g, :], m.veps[:, g, :], m.minus_half[:, :], ALU.pow).then_inc(s.b1_rstd, 1)
        pool.wait_ge(s.b1_nmean, g + 1)
        pool.wait_ge(s.b1_rstd, g + 1)
        for b in range(GB):
            last = pool.tensor_scalar(m.x0[:, columns(GB * g + b)], m.xr[:, columns(GB * g + b)],
                                      m.nmean[:, g, b:b + 1], m.rstd[:, g, b:b + 1], ALU.add, ALU.mult)
        last.then_inc(s.x1_ready, 1)
        if g:
            middle_part(M_SELF + 2 * g - 2, m.q_parts[:, 1, group(g - 1)])
            middle_part(M_SELF + 2 * g - 1, m.kp_self[:, 1, group(g - 1)])
        pool.wait_ge(s.x1_ready, g + 1)
        pool.tensor_tensor(per_batch(m.y[:, group(g)]), per_batch(m.x0[:, group(g)]), each_batch(m.row[:, R_SA_BO, :]),
                           ALU.add).then_inc(s.y_ready, 1)
    middle_part(M_SELF + 6, m.q_parts[:, 1, group(3)])
    middle_part(M_SELF + 7, m.kp_self[:, 1, group(3)])

    pool.wait_ge(s.v_pad_set, 2)
    for n in range(ALL + 6):
        k = n - 2
        if 0 <= k < ALL:
            pool.wait_ge(s.v_ready, V_SELF + G if k < B else V_CTX + G)
            at_least(pool, s.PV_done, UNITS * (k - 1))
            v = (m.v_self, m.v_cross)[k // B]
            pool.tensor_copy(m.v_pad[:, k % 2, :, 0:DH], v[:, k % B, :].rearrange("p (h d) -> p h d", d=DH))\
                .then_inc(s.v_pad_ready, 1)
        for u in range(UNITS):
            if 0 <= k < B:
                pool.wait_ge(s.exp_done, UNITS * k + u + 1)
                prob = m.prob[:, u, :].rearrange("p (h t) -> p h t", t=P)
                pool.affine_select(out=prob, in_=prob, compare_op=ALU.is_ge, fill=0.0, base=0,
                                   pattern=[[0, GB], [1, P]], channel_multiplier=-1).then_inc(s.prob_masked, 1)
            gg = (n - 8) // GB
            if u == 2 and n % GB == 0 and 0 <= gg < 2 * G:
                g = gg % G
                pool.wait_ge(s.a_mv, GB * gg + GB)
                pool.tensor_scalar(m.veps[:, g, :], m.mv[:, g, :, 1], EPS, None, ALU.add).then_inc(s.a_veps, 1)
                pool.tensor_scalar(m.nmean[:, g, :], m.mv[:, g, :, 0], -1.0, None, ALU.mult).then_inc(s.a_nmean, 1)
                pool.wait_ge(s.a_veps, gg + 1)
                pool.tensor_tensor(m.rstd[:, g, :], m.veps[:, g, :], m.minus_half[:, :], ALU.pow).then_inc(s.a_rstd, 1)
                pool.wait_ge(s.a_nmean, gg + 1)
                pool.wait_ge(s.a_rstd, gg + 1)
                pool.tensor_tensor(m.nmr[:, g, :], m.nmean[:, g, :], m.rstd[:, g, :], ALU.mult).then_inc(s.a_nmr, 1)
            g = (n - 11) // GB
            if u == 1 and n % GB == 3 and 0 <= g < G:
                pool.wait_ge(s.t_done, T_X2 + g + 1)
                yg = per_batch(m.y[:, group(g)])
                pool.tensor_tensor(yg, yg, each_batch(m.row[:, R_CA_BO, :]), ALU.add).then_inc(s.y_next, 1)
        gg = (n - 9) // GB
        if n % GB == 1 and 0 <= gg < 2 * G:
            r_g, r_bt = ((R_SA_G, R_SA_BT), (R_CA_G, R_CA_BT))[gg // G]
            yg = per_batch(m.y[:, group(gg % G)])
            pool.wait_ge(s.a_norm, gg + 1)
            pool.tensor_tensor(yg, yg, each_batch(m.row[:, r_g, :]), ALU.mult).then_inc(s.a_scaled, 1)
            pool.wait_ge(s.a_scaled, gg + 1)
            pool.tensor_tensor(yg, yg, each_batch(m.row[:, r_bt, :]), ALU.add).then_inc(s.a_shifted, 1)
        g = (n - 12) // GB
        if n % GB == 0 and 0 <= g < G:
            middle_part(M_CROSS + g, m.q_parts[:, 1, group(g)])

    for k in range(FFN_ITEMS + 2):
        if k < FFN_ITEMS:
            f, g = k // G, k % G
            yg, xg, bg = (per_batch(t[:, group(g)]) for t in (m.y, m.xr, m.x0))
            if f == 0:
                pool.wait_ge(s.a_shifted, G + g + 1)
            else:
                pool.wait_ge(s.f_out, k - G + 1)
            pool.tensor_tensor(xg, yg, each_batch(m.row[:, R_B2 + 3 * f, :]), ALU.add).then_inc(s.f_base_ready, 1)
            pool.tensor_tensor(bg, bg if f == 0 else yg, each_batch(m.row[:, R_BT + 3 * f, :]), ALU.add).then_inc(s.f_base_ready, 1)
        if 1 <= k <= FFN_ITEMS:
            j, g = k - 1, (k - 1) % G
            pool.wait_ge(s.f_mv1, GB * j + GB)
            pool.tensor_scalar(m.veps[:, g, :], m.mv[:, g, :, 1], EPS, None, ALU.add).then_inc(s.f_veps1, 1)
            pool.tensor_scalar(m.nmean[:, g, :], m.mv[:, g, :, 0], -1.0, None, ALU.mult).then_inc(s.f_nmean1, 1)
            pool.wait_ge(s.f_veps1, j + 1)
            pool.tensor_tensor(m.rstd[:, g, :], m.veps[:, g, :], m.minus_half[:, :], ALU.pow).then_inc(s.f_rstd1, 1)
            pool.wait_ge(s.f_nmean1, j + 1)
            pool.wait_ge(s.f_rstd1, j + 1)
            for b in range(GB):
                xb = m.xr[:, columns(GB * g + b)]
                last = pool.tensor_scalar(xb, xb, m.nmean[:, g, b:b + 1], m.rstd[:, g, b:b + 1], ALU.add, ALU.mult)
            last.then_inc(s.f_norm1, 1)
        if k >= 2:
            j, g = k - 2, (k - 2) % G
            pool.wait_ge(s.f_mv2, GB * j + GB)
            pool.tensor_scalar(m.veps[:, g, :], m.mv[:, g, :, 1], EPS, None, ALU.add).then_inc(s.f_veps2, 1)
            pool.tensor_scalar(m.nmean[:, g, :], m.mv[:, g, :, 0], -1.0, None, ALU.mult).then_inc(s.f_nmean2, 1)
            pool.wait_ge(s.f_veps2, j + 1)
            pool.tensor_tensor(m.rstd[:, g, :], m.veps[:, g, :], m.minus_half[:, :], ALU.pow).then_inc(s.f_rstd2, 1)
            pool.wait_ge(s.f_nmean2, j + 1)
            pool.wait_ge(s.f_rstd2, j + 1)
            pool.tensor_tensor(m.nmr[:, g, :], m.nmean[:, g, :], m.rstd[:, g, :], ALU.mult).then_inc(s.f_nmr2, 1)



def vector_program(dve, m, s):
    pT, pTQ, pQ, pK, pV, pM, pG, pF = m.bank

    def stats(it, first):
        n, g = it.n, it.g
        if first:
            dve.wait_ge(s.x_in[g], 16)
        else:
            wait_apart(dve, s, (s.x_added, n - 3),
                               (s.mv_done, GB * (n - 3)))
        for b in range(GB):
            last = dve.bn_stats(m.bn[:, g, b, :], m.xr[:, columns(GB * g + b)])
        last.then_inc(s.bn_done, 1)
        wait_apart(dve, s, (s.bn_done, n + 1),
                           (s.nmean_done, n - 3), (s.veps_done, n - 3))
        for b in range(GB):
            dve.bn_aggr(m.mv[:, g, b, :], m.bn[:, g, b, :]).then_inc(s.mv_done, 1)

    def first_rest(k, part):
        dve.wait_ge(s.full_ready, k + 1)
        at_least(dve, s.mid_ready, k - 1)
        at_least(dve, s.parts_ready, k - 1)
        dve.tensor_tensor(m.rest[:, k % 2, :], m.full[:, k % 2, :], part, ALU.subtract).then_inc(s.rest_ready, 1)

    def last_part(k, middle, part):
        dve.wait_ge(s.mid_ready, k + 1)
        dve.tensor_tensor(part, m.rest[:, k % 2, :], middle, ALU.subtract).then_inc(s.parts_ready, 1)

    def values(k, v, g, bias):
        dve.wait_ge(s.v_done, k + 1)
        dve.tensor_tensor(v[:, GB * g:GB * g + GB, :], per_batch(m.bank[3]), each_batch(m.row[:, bias, :]), ALU.add)\
           .then_inc(s.v_ready, 1)

    def outcome(g):
        dve.wait_ge(s.x_added, ITEMS - G + g + 1)
        dve.wait_ge(s.x_again, 16)
        dve.wait_ge(s.xn_ready, ITEMS - G + g + 1)
        dve.wait_ge(s.bias_added, ITEMS - G + g + 1)
        dve.tensor_tensor(m.xr[:, group(g)], m.xr[:, group(g)], m.x0[:, group(g)], ALU.add).then_inc(s.b1_sum, 1)
        dve.wait_ge(s.b1_sum, g + 1)
        dve.wait_ge(s.mv_done, GB * (ITEMS - G + g + 1))
        for b in range(GB):
            last = dve.bn_stats(m.bn[:, g, b, :], m.xr[:, columns(GB * g + b)])
        last.then_inc(s.b1_bn, 1)
        dve.wait_ge(s.b1_bn, g + 1)
        dve.wait_ge(s.nmean_done, ITEMS - G + g + 1)
        dve.wait_ge(s.veps_done, ITEMS - G + g + 1)
        for b in range(GB):
            dve.bn_aggr(m.mv[:, g, b, :], m.bn[:, g, b, :]).then_inc(s.b1_mv, 1)

    stats(stage(0, 0, 0), True)
    stats(stage(0, 1, 0), True)
    dve.wait_ge(s.cols_in, 16)
    for side in range(2):
        last = dve.tensor_scalar(m.bq[:, side:side + 1], m.col[:, C_BQ + 2 * side:C_BQ + 2 * side + 1], SCALE, None, ALU.mult)
        last.then_inc(s.bq_set, 1)
    dve.wait_ge(s.w_qkv_in, 16)
    dve.tensor_copy(m.wq_now[:, :], m.w_qkv[:, 0, 0:P]).then_inc(s.wq_loaded, 1)
    dve.tensor_copy(m.wv_now[:, :], m.w_qkv[:, 0, 2 * P:3 * P]).then_inc(s.wv_loaded, 1)

    dve.wait_ge(s.rows_in, 16)
    for g in range(G + 1):
        if g < G:
            first_rest(M_CTX + g, m.kp_cross[:, 0, group(g)])
        if g:
            last_part(M_CTX + g - 1, m.kp_cross[:, 1, group(g - 1)], m.kp_cross[:, 2, group(g - 1)])
        if g < G:
            values(V_CTX + g, m.v_cross, g, R_CA_BV)

    def slot(i, c):
        now, one, two, coming = (stage(i, c, back) for back in (0, 1, 2, -2))
        if one:
            n, g = one.n, one.g
            dve.wait_ge(s.ek_ready, n + 1)
            at_least(dve, s.qt_ready, n - 3)
            dve.reciprocal(m.rk[:, g, :], m.ksum[:, g, :]).then_inc(s.rk_ready, 1)
            dve.wait_ge(s.eq_ready, n + 1)
            at_least(dve, s.ms_ready, n - 3)
            dve.reciprocal(m.rq[:, g, :], m.qsum[:, g, :]).then_inc(s.rq_ready, 1)
            dve.wait_ge(s.TQ_done, n + 1)
            dve.wait_ge(s.rk_ready, n + 1)
            at_least(dve, s.M_done, n - 3)
            dve.tensor_tensor(per_batch(m.qt[:, g, :]), per_batch(pTQ), spread(m.rk[:, g, :], P), ALU.mult).then_inc(s.qt_ready, 1)
        if two:
            n, g = two.n, two.g
            dve.wait_ge(s.F_done, n + 1)
            dve.wait_ge(s.bias_added, n + 1)
            dve.tensor_tensor(m.xr[:, group(g)], pF, m.xr[:, group(g)], ALU.add).then_inc(s.x_added, 1)
        if now:
            n, g = now.n, now.g
            if c == G:
                dve.wait_ge(s.V_done, n)
                dve.tensor_copy(m.wv_now[:, :], m.w_qkv[:, now.layer, 2 * P:3 * P]).then_inc(s.wv_loaded, 1)
            dve.wait_ge(s.Q_done, n + 1)
            at_least(dve, s.eq_ready, n - 3)
            dve.tensor_reduce(m.nqmax[:, g, :], per_batch(pQ), AX.X, ALU.max, negate=True).then_inc(s.nqmax_ready, 1)
            after = stage(i, c, -1)
            if c == G - 1 and after:
                dve.tensor_copy(m.wq_now[:, :], m.w_qkv[:, after.layer, 0:P]).then_inc(s.wq_loaded, 1)
        if one:
            n, g = one.n, one.g
            dve.wait_ge(s.M_done, n + 1)
            dve.wait_ge(s.rq_ready, n + 1)
            at_least(dve, s.G_done, n - 3)
            dve.tensor_tensor(per_batch(m.ms[:, g, :]), per_batch(pM), spread(m.rq[:, g, :], P), ALU.mult).then_inc(s.ms_ready, 1)
        if now:
            n, g = now.n, now.g
            dve.wait_ge(s.K_done, n + 1)
            at_least(dve, s.ek_ready, n - 3)
            dve.tensor_reduce(m.nkmax[:, g, :], per_batch(pK), AX.X, ALU.max, negate=True).then_inc(s.nkmax_ready, 1)
        if coming:
            stats(coming, first=isinstance(i, int) and i == 0 and c < 2)
        if two and isinstance(i, int) and i == DEPTH - 1:
            outcome(two.g)

    slots(dve, slot)

    dve.wait_ge(s.TQ_done, ITEMS)
    dve.wait_ge(s.V_done, ITEMS)
    for g in range(G + 1):
        for w, parts in enumerate((m.q_parts, m.kp_self)):
            k = M_SELF + 2 * g + w
            if g < G:
                first_rest(k, parts[:, 0, group(g)])
            if g < G and k > M_SELF or g == G and w == 0:
                before, gb = (m.kp_self, g - 1) if w == 0 else (m.q_parts, g)
                last_part(k - 1, before[:, 1, group(gb)], before[:, 2, group(gb)])
        if g < G:
            values(V_SELF + g, m.v_self, g, R_SA_BV)

    for n in range(ALL + 5):
        for u in range(UNITS):
            if n < ALL:
                dve.wait_ge(s.S_done, UNITS * n + u + 1)
                at_least(dve, s.negmax_rest_ready, n - 1)
                dve.tensor_reduce(m.negmax[:, n % 2, GB * u:GB * u + GB], per_batch(m.bank[u % 2]), AX.X, ALU.max, negate=True)\
                   .then_inc(s.max_done, 1)
            k = n - 4
            if u == 1 and 0 <= k < ALL:
                o = m.bank[5].rearrange("p (h e) -> p h e", e=VW)
                dve.wait_ge(s.AT_done, k + 1)
                at_least(dve, s.o_ready, k - 1)
                dve.reciprocal(m.o_recip[:, k % 2, :].unsqueeze(2), o[:, :, DH:DH + 1]).then_inc(s.o_recip_ready, 1)
                dve.wait_ge(s.o_recip_ready, k + 1)
                at_least(dve, s.AO_done, k - 1)
                dve.tensor_tensor(m.o[:, k % 2, :].rearrange("p (s j d) -> p j s d", s=SIDES, d=DH),
                                  m.bank[5].rearrange("p (j s e) -> p j s e", s=SIDES, e=VW)[:, :, :, 0:DH],
                                  m.o_recip[:, k % 2, :].rearrange("p (j s) -> p j s", s=SIDES).unsqueeze(3)
                                  .to_broadcast([P, TILES, SIDES, DH]), ALU.mult).then_inc(s.o_ready, 1)
            gg = (n - 8) // GB
            if u == 1 and n % GB == 0 and 0 <= gg < 2 * G:
                g = gg % G
                dve.wait_ge(s.O_done, gg + 1)
                dve.wait_ge(*((s.y_ready, gg + 1) if gg < G else (s.y_next, gg - G + 1)))
                dve.tensor_tensor(m.y[:, group(g)], m.bank[7], m.y[:, group(g)], ALU.add).then_inc(s.y_added, 1)
                dve.wait_ge(s.y_added, gg + 1)
                if gg >= G:
                    dve.wait_ge(s.a_mv, GB * (gg - G) + GB)
                for b in range(GB):
                    last = dve.bn_stats(m.bn[:, g, b, :], m.y[:, columns(GB * g + b)])
                last.then_inc(s.a_bn, 1)
                dve.wait_ge(s.a_bn, gg + 1)
                if gg < G:
                    dve.wait_ge(s.b1_nmean, gg + 1)
                    dve.wait_ge(s.b1_veps, gg + 1)
                else:
                    dve.wait_ge(s.a_nmean, gg - G + 1)
                    dve.wait_ge(s.a_veps, gg - G + 1)
                for b in range(GB):
                    dve.bn_aggr(m.mv[:, g, b, :], m.bn[:, g, b, :]).then_inc(s.a_mv, 1)
            g = (n - 12) // GB
            if u == 1 and n % GB == 0 and 0 <= g < G:
                first_rest(M_CROSS + g, m.q_parts[:, 0, group(g)])
            g = (n - 13) // GB
            if u == 0 and n % GB == 1 and 0 <= g < G:
                last_part(M_CROSS + g, m.q_parts[:, 1, group(g)], m.q_parts[:, 2, group(g)])
        if n < ALL:
            parts = m.negmax_parts[:, n % 2, :].rearrange("p (a h) -> p a h", a=3)
            neg, rest = m.negmax[:, n % 2, :], m.negmax_rest[:, n % 2, :]
            dve.wait_ge(s.max_done, UNITS * n + UNITS)
            at_least(dve, s.TM_done, n - 1)
            dve.tensor_copy(parts[:, 0, :], neg).then_inc(s.negmax_hi, 1)
            dve.wait_ge(s.negmax_hi, n + 1)
            at_least(dve, s.negmax_lo, n - 1)
            dve.tensor_tensor(rest, neg, parts[:, 0, :], ALU.subtract).then_inc(s.negmax_rest_ready, 1)
            dve.wait_ge(s.negmax_rest_ready, n + 1)
            dve.tensor_copy(parts[:, 1, :], rest).then_inc(s.negmax_mid, 1)
            dve.wait_ge(s.negmax_mid, n + 1)
            dve.tensor_tensor(parts[:, 2, :], rest, parts[:, 1, :], ALU.subtract).then_inc(s.negmax_lo, 1)

    for k in range(FFN_ITEMS + 1):
        if k < FFN_ITEMS:
            g = k % G
            dve.wait_ge(s.f_D_done, k + 1)
            dve.wait_ge(s.f_base_ready, 2 * k + 2)
            dve.tensor_tensor(m.xr[:, group(g)], m.bank[4 + k % 2], m.xr[:, group(g)], ALU.add).then_inc(s.f_sum, 1)
            dve.wait_ge(s.f_sum, k + 1)
            if k >= G:
                dve.wait_ge(s.f_mv2, GB * (k - G) + GB)
                dve.wait_ge(s.f_nmean2, k - G + 1)
                dve.wait_ge(s.f_veps2, k - G + 1)
            for b in range(GB):
                last = dve.bn_stats(m.bn[:, g, b, :], m.xr[:, columns(GB * g + b)])
            last.then_inc(s.f_bn1, 1)
            dve.wait_ge(s.f_bn1, k + 1)
            for b in range(GB):
                dve.bn_aggr(m.mv[:, g, b, :], m.bn[:, g, b, :]).then_inc(s.f_mv1, 1)
        if k >= 1:
            j, g = k - 1, (k - 1) % G
            dve.wait_ge(s.f_norm1, j + 1)
            xg = per_batch(m.xr[:, group(g)])
            dve.tensor_tensor(xg, xg, each_batch(m.row[:, R_G + 3 * (j // G), :]), ALU.mult).then_inc(s.f_scaled, 1)
            dve.wait_ge(s.f_scaled, j + 1)
            dve.tensor_tensor(m.xr[:, group(g)], m.xr[:, group(g)], m.x0[:, group(g)], ALU.add).then_inc(s.f_sum2, 1)
            dve.wait_ge(s.f_sum2, j + 1)
            dve.wait_ge(s.f_mv1, GB * j + GB)
            for b in range(GB):
                last = dve.bn_stats(m.bn[:, g, b, :], m.xr[:, columns(GB * g + b)])
            last.then_inc(s.f_bn2, 1)
            dve.wait_ge(s.f_bn2, j + 1)
            for b in range(GB):
                dve.bn_aggr(m.mv[:, g, b, :], m.bn[:, g, b, :]).then_inc(s.f_mv2, 1)



def scalar_program(act, m, s):
    pT, pTQ, pQ, pK, pV, pM, pG, pF = m.bank

    def transposed(t, bank=0):
        act.wait_ge(s.t_done, t + 1)
        act.activation(m.xT[:, t % G, :], m.bank[bank], ACT.Copy).then_inc(s.xT_ready, 1)

    def first_part(k, bank, part, bias, scale):
        act.wait_ge(s.proj_done, k + 1)
        at_least(act, s.rest_ready, k - 1)
        act.activation(m.full[:, k % 2, :], m.bank[bank], ACT.Identity, bias=bias, scale=scale)
        act.activation(part, m.bank[bank], ACT.Identity, bias=bias, scale=scale).then_inc(s.full_ready, 1)

    act.wait_ge(s.cols_in, 16)
    for g in range(G):
        transposed(T_CTX + g)
        first_part(M_CTX + g, PROJ[g % 2], m.kp_cross[:, 0, group(g)], m.col[:, C_BK + 2:C_BK + 3], 1.0)

    def slot(i, c):
        now, one = (stage(i, c, back) for back in (0, 1))
        if now:
            n, g = now.n, now.g
            wait_apart(act, s, (s.T_done, n + 1), (s.V_done, n - 3))
            act.activation(m.hT[:, g, :], pT, ACT.Identity, bias=m.col[:, bass.ds(DEPTH + now.layer, 1)],
                           scale=m.col[:, bass.ds(now.layer, 1)]).then_inc(s.hT_ready, 1)
            act.wait_ge(s.nqmax_ready, n + 1)
            at_least(act, s.TQ_done, n - 3)
            at_least(act, s.rq_ready, n - 3)
            for b in range(GB):
                last = act.activation(m.eq[:, g, columns(b)], pQ[:, columns(b)], ACT.Exp, bias=m.nqmax[:, g, b:b + 1],
                                      accum_out=m.qsum[:, g, b:b + 1])
            last.then_inc(s.eq_ready, 1)
            act.wait_ge(s.nkmax_ready, n + 1)
            at_least(act, s.M_done, n - 3)
            at_least(act, s.rk_ready, n - 3)
            for b in range(GB):
                last = act.activation(m.ek[:, g, columns(b)], pK[:, columns(b)], ACT.Exp, bias=m.nkmax[:, g, b:b + 1],
                                      accum_out=m.ksum[:, g, b:b + 1])
            last.then_inc(s.ek_ready, 1)
        if one:
            n, g = one.n, one.g
            act.wait_ge(s.G_done, n + 1)
            at_least(act, s.F_done, n - 3)
            act.activation(m.gs[:, g, :], pG, ACT.Copy).then_inc(s.gs_ready, 1)
        if now:
            n, g = now.n, now.g
            act.wait_ge(s.V_done, n + 1)
            at_least(act, s.F_done, n - 3)
            act.activation(m.vT[:, g, :], pV, ACT.Copy).then_inc(s.vT_ready, 1)
        if isinstance(i, int) and i == DEPTH - 1 and c >= G:
            if c == G:
                act.wait_ge(s.bq_set, 2)
            else:
                act.wait_ge(s.TQ_done, ITEMS)
                act.wait_ge(s.V_done, ITEMS)
            self_step(c - G)

    def self_step(g):
        if g < G:
            transposed(T_X1 + g)
        if g:
            first_part(M_SELF + 2 * g - 2, PROJ[0], m.q_parts[:, 0, group(g - 1)], m.bq[:, 0:1], SCALE)
            first_part(M_SELF + 2 * g - 1, PROJ[1], m.kp_self[:, 0, group(g - 1)], m.col[:, C_BK:C_BK + 1], 1.0)

    slots(act, slot)
    for g in range(2, G + 1):
        self_step(g)

    act.wait_ge(s.F_done, ITEMS)
    for n in range(ALL + 6):
        for u in range(UNITS):
            k = n - 2
            if 0 <= k < ALL:
                act.wait_ge(s.ST_done, UNITS * k + u + 1)
                at_least(act, s.PV_done, UNITS * (k - 1) + u + 1)
                act.activation(m.prob[:, u, :], m.bank[2 + u % 2], ACT.Exp).then_inc(s.exp_done, 1)
            g = (n - 9) // GB
            if u == 0 and n % GB == 1 and 0 <= g < 2 * G:
                act.wait_ge(s.a_nmr, g + 1)
                for b in range(GB):
                    yb = m.y[:, columns(GB * (g % G) + b)]
                    last = act.activation(yb, yb, ACT.Identity, bias=m.nmr[:, g % G, b:b + 1], scale=m.rstd[:, g % G, b:b + 1])
                last.then_inc(s.a_norm, 1)
            g = (n - 11) // GB
            if u == 0 and n % GB == 3 and 0 <= g < G:
                transposed(T_X2 + g, 5)
            g = (n - 12) // GB
            if u == 0 and n % GB == 0 and 0 <= g < G:
                act.wait_ge(s.spilled[g], SPILLS)
                first_part(M_CROSS + g, 5, m.q_parts[:, 0, group(g)], m.bq[:, 1:2], SCALE)
            k = n - 1
            if u == 1 and 0 <= k < ALL:
                act.wait_ge(s.TM_done, k + 1)
                at_least(act, s.max_loaded[k % 2], 16 * (k // 2))
                act.activation(m.negmax_T[:, k % 2, :], m.bank[4].bitcast(BF16)[0:3 * H, 0:P], ACT.Copy).then_inc(s.negmax_T_ready, 1)
                act.wait_ge(s.negmax_T_ready, k + 1)
                at_least(act, s.ST_done, UNITS * (k - 7))
                act.dma_start(m.q_op[k // GB % 2][MAX_ROWS, :, :, columns(k % GB)].rearrange("a j s t -> a (j s) t"),
                              m.negmax_T[:, k % 2, :]).then_inc(s.max_loaded[k % 2], 16)
        k = n - 3
        if 0 <= k < ALL:
            act.wait_ge(s.PV_done, UNITS * k + UNITS)
            at_least(act, s.AT_done, k)
            act.activation(m.o_T[:, :], m.bank[6], ACT.Copy).then_inc(s.o_T_ready, 1)
        g = (n - 7) // GB
        if n % GB == 3 and 0 <= g < 2 * G:
            act.wait_ge(s.AO_done, GB * g + GB)
            at_least(act, s.O_done, g)
            act.activation(m.att_T[:, :], m.bank[7], ACT.Copy).then_inc(s.att_T_ready, 1)

    for k in range(FFN_ITEMS + 2):
        if k < FFN_ITEMS:
            f = k // G
            act.wait_ge(s.t_done, T_FFN + k + 1)
            act.activation(m.xT[:, k % G, :], m.bank[6 + k % 2], ACT.Copy).then_inc(s.xT_ready, 1)
            for c in range(FC):
                act.wait_ge(s.f_H_done, FC * k + c + 1)
                if k >= 2:
                    act.wait_ge(s.f_D_done, k - 1)
                act.activation(m.hidden[:, k % 2, c, :], m.bank[c], ACT.Relu, bias=m.col[:, C_B1 + FC * f + c:C_B1 + FC * f + c + 1])\
                   .then_inc(s.f_relu, 1)
        if k >= 2:
            j, g = k - 2, (k - 2) % G
            act.wait_ge(s.f_nmr2, j + 1)
            act.wait_ge(s.t_done, T_FFN + j + 1)
            act.wait_ge(s.f_base_ready, 2 * j + 2)
            for b in range(GB):
                last = act.activation(m.y[:, columns(GB * g + b)], m.xr[:, columns(GB * g + b)], ACT.Identity,
                                      bias=m.nmr[:, g, b:b + 1], scale=m.rstd[:, g, b:b + 1])
            last.then_inc(s.f_out, 1)



def tensor_program(pe, m, s):
    pT, pTQ, pQ, pK, pV, pM, pG, pF = m.bank

    def transpose(t, src, g, bank=0):
        at_least(pe, s.xT_ready, t)
        for b in range(GB):
            last = pe.transpose(m.bank[bank][:, columns(b)], src[:, columns(GB * g + b)], m.ident[:, :])
        last.then_inc(s.t_done, 1)

    def project(k, t, w, bank=None):
        pe.wait_ge(s.xT_ready, t + 1)
        at_least(pe, s.full_ready, k - 1)
        pe.matmul(m.bank[PROJ[k % 2] if bank is None else bank], m.w_att[:, w, :], m.xT[:, t % G, :], start=True, stop=True).then_inc(s.proj_done, 1)

    def values(k, t, w):
        at_least(pe, s.v_ready, k)
        for b in range(GB):
            last = pe.matmul(m.bank[3][:, columns(b)], m.xT[:, t % G, columns(b)], m.w_att[:, w, :], start=True, stop=True)
        last.then_inc(s.v_done, 1)

    pe.wait_ge(s.ident_set, 2)
    pe.wait_ge(s.w_att_in, 16)
    for g in range(G + 1):
        if g < G:
            pe.wait_ge(s.ctx_in[g], 16)
            transpose(T_CTX + g, m.y, g)
        if g:
            project(M_CTX + g - 1, T_CTX + g - 1, 5)
            values(V_CTX + g - 1, T_CTX + g - 1, 6)
    pe.wait_ge(s.full_ready, M_CTX + G)
    pe.wait_ge(s.v_ready, V_CTX + G)
    pe.wait_ge(s.w_qkv_in, 16)

    def slot(i, c):
        now, one, two = (stage(i, c, back) for back in (0, 1, 2))
        if now:
            n, g = now.n, now.g
            pe.wait_ge(s.xn_ready, n + 1)
            at_least(pe, s.hT_ready, n)
            for b in range(GB):
                last = pe.transpose(pT[:, columns(b)], m.xn[:, g, columns(b)], m.ident[:, :])
            last.then_inc(s.T_done, 1)
        if one:
            n, g = one.n, one.g
            pe.wait_ge(s.eq_ready, n + 1)
            at_least(pe, s.qt_ready, n)
            for b in range(GB):
                last = pe.transpose(pTQ[:, columns(b)], m.eq[:, g, columns(b)], m.ident[:, :])
            last.then_inc(s.TQ_done, 1)
        if two:
            n, g = two.n, two.g
            pe.wait_ge(s.gs_ready, n + 1)
            pe.wait_ge(s.vT_ready, n + 1)
            at_least(pe, s.x_added, n)
            for b in range(GB):
                last = pe.matmul(pF[:, columns(b)], m.vT[:, g, columns(b)], m.gs[:, g, columns(b)], start=True, stop=True)
            last.then_inc(s.F_done, 1)
        if now:
            n, g = now.n, now.g
            pe.wait_ge(s.hT_ready, n + 1)
            pe.wait_ge(s.wq_loaded, now.layer + 1)
            at_least(pe, s.eq_ready, n)
            pe.matmul(pQ, m.wq_now[:, :], m.hT[:, g, :], start=True, stop=True).then_inc(s.Q_done, 1)
        if one:
            n, g = one.n, one.g
            pe.wait_ge(s.qt_ready, n + 1)
            pe.wait_ge(s.ek_ready, n + 1)
            at_least(pe, s.ms_ready, n)
            for b in range(GB):
                last = pe.matmul(pM[:, columns(b)], m.qt[:, g, columns(b)], m.ek[:, g, columns(b)], start=True, stop=True)
            last.then_inc(s.M_done, 1)
        if now:
            n, g = now.n, now.g
            at_least(pe, s.ek_ready, n)
            for b in range(GB):
                last = pe.matmul(pK[:, columns(b)], m.hT[:, g, columns(b)], m.w_qkv[:, now.layer, P:2 * P], start=True, stop=True)
            last.then_inc(s.K_done, 1)
        if one:
            n, g = one.n, one.g
            if isinstance(i, int) and i == 0 and c == 1:
                pe.wait_ge(s.w_out_in, 16)
            pe.wait_ge(s.ms_ready, n + 1)
            at_least(pe, s.gs_ready, n)
            for b in range(GB):
                last = pe.matmul(pG[:, columns(b)], m.ms[:, g, columns(b)], m.w_out[:, one.layer, :], start=True, stop=True)
            last.then_inc(s.G_done, 1)
        if now:
            n, g = now.n, now.g
            at_least(pe, s.vT_ready, n)
            pe.wait_ge(s.wv_loaded, now.layer + 1)
            pe.matmul(pV, m.wv_now[:, :], m.hT[:, g, :], start=True, stop=True).then_inc(s.V_done, 1)
        if isinstance(i, int) and i == DEPTH - 1 and c >= G:
            if c == G:
                pe.wait_ge(s.hT_ready, ITEMS)
                pe.wait_ge(s.eq_ready, ITEMS)
                pe.wait_ge(s.ek_ready, ITEMS)
                pe.wait_ge(s.vT_ready, ITEMS)
            self_step(c - G)

    def self_step(g):
        if g < G:
            pe.wait_ge(s.x1_ready, g + 1)
            transpose(T_X1 + g, m.x0, g)
        if g:
            project(M_SELF + 2 * g - 2, T_X1 + g - 1, 0)
            project(M_SELF + 2 * g - 1, T_X1 + g - 1, 1)
            values(V_SELF + g - 1, T_X1 + g - 1, 2)

    slots(pe, slot)

    for g in range(2, G + 1):
        self_step(g)

    pe.wait_ge(s.full_ready, M_SELF + 2 * G)
    pe.wait_ge(s.v_ready, V_SELF + G)
    pe.wait_ge(s.mask_set, 2)
    pe.wait_ge(s.ident_bf_set, 2)
    pe.wait_ge(s.qt_ready, ITEMS)
    pe.wait_ge(s.ms_ready, ITEMS)
    pe.wait_ge(s.gs_ready, ITEMS)
    pe.wait_ge(s.x_added, ITEMS)

    def scores(n, u):
        q, k, t, bank = m.q_op[n // GB % 2], m.k_op[n // GB % 2], columns(n % GB), m.bank[u % 2]
        at_least(pe, s.max_done, UNITS * n + u - 1)
        if n < B:
            pe.matmul(bank, m.ident_bf[:, :], m.mask[:, :, :], start=True, stop=False, skip_group_check=True)
        for jj in range(UT):
            for side in range(SIDES):
                j = UT * u + jj
                last = pe.matmul(bank[:, columns(SIDES * jj + side)], q[0:OP, j, side, t], k[0:OP, j, t],
                                 start=n >= B, stop=True, skip_group_check=True)
        last.then_inc(s.S_done, 1)

    def scores_T(n, u):
        q, k, t, bank = m.q_op[n // GB % 2], m.k_op[n // GB % 2], columns(n % GB), m.bank[2 + u % 2]
        at_least(pe, s.exp_done, UNITS * n + u - 1)
        for jj in range(UT):
            j = UT * u + jj
            last = pe.matmul(bank[:, 2 * P * jj:2 * P * jj + 2 * P], k[0:OP + 3, j, t], q[0:OP + 3, j, :, t], start=True, stop=True)
        last.then_inc(s.ST_done, 1)

    def weighted(n, u):
        pe.wait_ge(s.prob_masked if n < B else s.exp_done, UNITS * n + u + 1)
        for jj in range(UT):
            for side in range(SIDES):
                at = SIDES * jj + side
                last = pe.matmul(m.bank[6][VW * at:VW * at + VW, columns(u)], m.v_pad[:, n % 2, TILES * side + UT * u + jj, :],
                                 m.prob[:, u, columns(at)], start=True, stop=True)
        last.then_inc(s.PV_done, 1)

    for n in range(ALL + 5):
        for u in range(UNITS):
            if n < ALL:
                if u == 0 and n % GB == 0:
                    pe.wait_ge(s.op_loaded[n // GB % 2], LOADS * (n // HALF + 1))
                scores(n, u)
            k = n - 2
            if 0 <= k < ALL:
                if u == 0:
                    pe.wait_ge(s.max_loaded[k % 2], 16 * (k // 2 + 1))
                scores_T(k, u)
            k = n - 3
            if 0 <= k < ALL:
                if u == 0:
                    pe.wait_ge(s.v_pad_ready, k + 1)
                    at_least(pe, s.o_T_ready, k)
                weighted(k, u)
            g = (n - 8) // GB
            if u == 0 and n % GB == 0 and 0 <= g < 2 * G:
                pe.wait_ge(s.att_T_ready, g + 1)
                for b in range(GB):
                    last = pe.matmul(m.bank[7][:, columns(b)], m.att_T[:, columns(b)], m.w_att[:, 4 * (g // G) + 3, :],
                                     start=True, stop=True)
                last.then_inc(s.O_done, 1)
            k = n - 1
            if u == 1 and 0 <= k < ALL:
                pe.wait_ge(s.negmax_lo, k + 1)
                at_least(pe, s.negmax_T_ready, k)
                pe.transpose(m.bank[4].bitcast(BF16)[0:3 * H, 0:P], m.negmax_parts[:, k % 2, :], m.ident_bf[:, :]).then_inc(s.TM_done, 1)
            k = n - 4
            if u == 1 and 0 <= k < ALL:
                pe.wait_ge(s.o_T_ready, k + 1)
                at_least(pe, s.o_ready, k)
                if 11 <= n < 11 + B and n % GB == 3:
                    pe.wait_ge(s.xT_ready, T_X2 + (n - 11) // GB + 1)
                if 12 <= n < 12 + B and n % GB == 0:
                    pe.wait_ge(s.full_ready, M_CROSS + (n - 12) // GB + 1)
                for at in range(UNITS):
                    last = pe.transpose(m.bank[5][:, columns(at)], m.o_T[:, columns(at)], m.ident[:, :])
                last.then_inc(s.AT_done, 1)
        k = n - 4
        if 0 <= k < ALL:
            pe.wait_ge(s.o_ready, k + 1)
            if k % GB == 0:
                at_least(pe, s.y_added, k // GB)
            pe.transpose(m.bank[7][:, columns(k % GB)], m.o[:, k % 2, :], m.ident[:, :]).then_inc(s.AO_done, 1)
        g = (n - 10) // GB
        if n % GB == 2 and 0 <= g < G:
            pe.wait_ge(s.a_shifted, g + 1)
            transpose(T_X2 + g, m.y, g, 5)
        g = (n - 11) // GB
        if n % GB == 3 and 0 <= g < G:
            project(M_CROSS + g, T_X2 + g, 4, 5)
    pe.wait_ge(s.y_added, 2 * G)

    pe.wait_ge(s.w_ffn_in, 32)
    for k in range(FFN_ITEMS + 1):
        if k < FFN_ITEMS:
            f, g = k // G, k % G
            if f == 0:
                pe.wait_ge(s.a_shifted, G + g + 1)
            else:
                pe.wait_ge(s.f_out, g + 1)
            if k >= 2:
                pe.wait_ge(s.xT_ready, T_FFN + k - 1)
            for b in range(GB):
                last = pe.transpose(m.bank[6 + k % 2][:, columns(b)], m.y[:, columns(GB * g + b)], m.ident[:, :])
            last.then_inc(s.t_done, 1)
        if k:
            j = k - 1
            pe.wait_ge(s.f_relu, FC * j + FC)
            if j >= 2:
                pe.wait_ge(s.f_sum, j - 1)
            for b in range(GB):
                for c in range(FC):
                    last = pe.matmul(m.bank[4 + j % 2][:, columns(b)], m.hidden[:, j % 2, c, columns(b)], m.w2[:, j // G, c, :],
                                     start=c == 0, stop=c == FC - 1)
            last.then_inc(s.f_D_done, 1)
        if k < FFN_ITEMS:
            pe.wait_ge(s.xT_ready, T_FFN + k + 1)
            for c in range(FC):
                at_least(pe, s.f_relu, FC * (k - 1) + c + 1)
                pe.matmul(m.bank[c], m.w1[:, f, columns(c)], m.xT[:, g, :], start=True, stop=True).then_inc(s.f_H_done, 1)


def decoder_kernel(nc, x, context, w_qkv, w_out, w_att, w1, w2, rows, cols, q_rows, k_rows, out):
    a = Names()
    a.x, a.context, a.w_qkv, a.w_out, a.w_att, a.w1, a.w2, a.rows, a.cols, a.q_rows, a.k_rows, a.out = \
        x, context, w_qkv, w_out, w_att, w1, w2, rows, cols, q_rows, k_rows, out
    with ExitStack() as ctx:
        m = allocate(nc, ctx)
        s = semaphores(nc, ctx)
        block = ctx.enter_context(nc.Block())

        @block.sync
        def _(sp):
            sync_program(sp, m, s, a)

        @block.gpsimd
        def _(pool):
            gpsimd_program(pool, m, s)

        @block.vector
        def _(dve):
            vector_program(dve, m, s)

        @block.scalar
        def _(act):
            scalar_program(act, m, s)

        @block.tensor
        def _(pe):
            tensor_program(pe, m, s)



def kernel(**inputs):
    import numpy as _np
    import concourse.bacc as _bacc
    from concourse import mybir as _mybir
    from concourse.bass_utils import run_bass_kernel_spmd as _run

    def by_feature(w):
        w = _np.asarray(w)
        return w.reshape(w.shape[:-1] + (SIDES, TILES, DH)).swapaxes(-1, -2).reshape(w.shape)

    v = {k: _np.asarray(a) for k, a in inputs.items()}
    att, xat, ffn = "L0_attn_", "L0_xattn_", "L0_ffn_"
    arrays = {
        "x": v["x"],
        "context": v["ctx_1024"],
        "w_qkv": v[att + "w_qkv"],
        "w_out": v[att + "w_out"],
        "w_att": _np.stack([by_feature(v[f"{xat}{p}_w{n}"]) if n in "qk" else v[f"{xat}{p}_w{n}"]
                            for p in ("sa", "ca") for n in "qkvo"]),
        "w1": _np.stack([v[xat + "f_w1"], v[ffn + "w1"][0]]),
        "w2": _np.stack([v[xat + "f_w2"], v[ffn + "w2"][0]]),
        "rows": _np.concatenate([v[att + "b_out"]] + [v[f"{xat}{p}_{n}"][None] for p in ("sa", "ca") for n in ("bv", "bo", "g", "bt")]
                                + [v[xat + n][None] for n in ("f_b2", "f_g", "f_bt")]
                                + [v[ffn + "b2"][0:1], v[ffn + "gamma"][None], v[ffn + "beta"][None]]),
        "cols": _np.concatenate([v[att + "gamma"].T, v[att + "beta"].T]
                                + [by_feature(v[f"{xat}{p}_b{n}"])[:, None] for p in ("sa", "ca") for n in "qk"]
                                + [v[xat + "f_b1"].reshape(FC, P).T, v[ffn + "b1"][0].reshape(FC, P).T], axis=1),
    }
    nc = _bacc.Bacc("TRN2", target_bir_lowering=False, num_devices=1)
    args = []
    arrays = {f"in_{name}": _np.ascontiguousarray(array) for name, array in arrays.items()}
    for name, array in arrays.items():
        args.append(nc.dram_tensor(name, array.shape, _mybir.dt.from_np(array.dtype), kind="ExternalInput").ap())
    for name in ("q_rows", "k_rows"):
        args.append(nc.dram_tensor(name, (2 * G, SIDES, PAIRS, DH * TILES, W), _mybir.dt.bfloat16, kind="Internal").ap())
    args.append(nc.dram_tensor("out", (B, P, P), _mybir.dt.float32, kind="ExternalOutput").ap())
    decoder_kernel(nc, *args)
    r = _run(nc, [arrays], core_ids=[0])
    return r.results[0]["out"]
```

```python
from contextlib import ExitStack

import numpy as np

import concourse.bass as bass
from concourse import mybir

F32 = mybir.dt.float32
BF16 = mybir.dt.bfloat16
ALU = mybir.AluOpType
ACT = mybir.ActivationFunctionType
AX = mybir.AxisListType

P = 128
B = 16
DEPTH = 6
GB = 4
G = B // GB
W = GB * P
ITEMS = DEPTH * G
EPS = 1e-5

H = 16
DH = P // H
SIDES, TILES = 2, H // 2
PAIRS = 6
ROWS = PAIRS * DH
Q_PARTS = (0, 0, 0, 1, 1, 2)
K_PARTS = (0, 1, 2, 0, 1, 0)
OP = SIDES * ROWS
MAX_ROWS = slice(OP, OP + 3)
UNITS = 4
UT = TILES // UNITS
HALF = 2 * GB
ALL = 2 * B
VW = 32
MASKED = -3.0e38
SCALE = float(1.0 / np.sqrt(np.float32(DH)))

FC = 4
FFN_ITEMS = 2 * G

R_SA_BV, R_SA_BO, R_SA_G, R_SA_BT, R_CA_BV, R_CA_BO, R_CA_G, R_CA_BT = range(DEPTH, DEPTH + 8)
R_B2, R_G, R_BT = DEPTH + 8, DEPTH + 9, DEPTH + 10
NROWS = DEPTH + 14
C_BQ, C_BK, C_B1 = 2 * DEPTH, 2 * DEPTH + 1, 2 * DEPTH + 4
C_SA_G, C_SA_BT = C_B1 + 2 * FC, C_B1 + 2 * FC + 1
NCOLS = C_SA_BT + 1


class Names:
    pass


class Item:

    def __init__(self, n, layer, g):
        self.n, self.layer, self.g = n, layer, g


def at_least(eng, sem, count):
    if isinstance(count, int) and count <= 0:
        return
    eng.wait_ge(sem, count)


def wait_apart(eng, s, *waits):
    waits = [(sem, count if isinstance(count, int) else eng.snap(eng.to_reg(count))) for sem, count in waits]
    eng.wait_ge(s.ident_set, 2)
    for sem, count in waits:
        at_least(eng, sem, count)


def per_batch(ap):
    return ap.rearrange("p (b t) -> p b t", t=P)


def spread(ap, n):
    return ap.unsqueeze(2).to_broadcast([ap.shape[0], ap.shape[1], n])


def each_batch(ap, n=GB):
    return ap.unsqueeze(1).to_broadcast([ap.shape[0], n, ap.shape[1]])


def unit_at(n, u, lag):
    k, v = divmod(UNITS * n + u - lag, UNITS)
    return (k, v) if 0 <= k < ALL else (-1, 0)


def columns(b):
    return slice(b * P, b * P + P)


def group(g):
    return bass.ds(g * W, W)



def allocate(nc, ctx):
    def sb(name, shape, dt=F32):
        return ctx.enter_context(nc.sbuf_tensor(name, shape, dt))

    m = Names()
    m.x0 = sb("x0", [P, B * P])
    m.xr = sb("xr", [P, B * P])
    m.y = sb("y", [P, B * P])
    m.w_qkv = sb("w_qkv", [P, DEPTH, 3 * P])
    m.w_out = sb("w_out", [P, DEPTH, P])
    m.w_att = sb("w_att", [P, 8, P])
    m.w1 = sb("w1", [P, 2, FC * P])
    m.w2 = sb("w2", [P, 2, FC, P])
    m.row = sb("row", [P, NROWS, P])
    m.col = sb("col", [P, NCOLS])
    m.ident = sb("ident", [P, P])
    m.ident_bf = sb("ident_bf", [P, P], BF16)
    m.mask = sb("mask", [P, GB, P], BF16)
    m.minus_half = sb("minus_half", [P, GB])
    m.wq_now = sb("wq_now", [P, P])
    m.wv_now = sb("wv_now", [P, P])
    m.bn = sb("bn", [P, G, GB, 6])
    m.mv = sb("mv", [P, G, GB, 2])
    m.veps = sb("veps", [P, G, GB])
    m.rstd = sb("rstd", [P, G, GB])
    m.nmean = sb("nmean", [P, G, GB])
    m.nmr = sb("nmr", [P, G, GB])
    m.nqmax = sb("nqmax", [P, G, GB])
    m.nkmax = sb("nkmax", [P, G, GB])
    m.qsum = sb("qsum", [P, G, GB])
    m.ksum = sb("ksum", [P, G, GB])
    m.rq = sb("rq", [P, G, GB])
    m.rk = sb("rk", [P, G, GB])
    m.xT = sb("xT", [P, G, W])
    m.rest = sb("rest", [P, 2, W])
    m.kp_cross = sb("kp_cross", [P, 3, B * P], BF16)
    m.v_self = sb("v_self", [P, B, P])
    m.v_cross = sb("v_cross", [P, B, P])
    m.v_pad = sb("v_pad", [P, 2, H, VW])
    m.negmax = sb("negmax", [P, 2, TILES * SIDES])
    m.negmax_rest = sb("negmax_rest", [P, 2, TILES * SIDES])
    m.negmax_parts = sb("negmax_parts", [P, 2, 3 * H], BF16)
    m.negmax_T = sb("negmax_T", [3 * H, 2, P], BF16)
    m.o_T = sb("o_T", [P, W])
    m.o_recip = sb("o_recip", [P, 2, H])
    m.o = sb("o", [P, 2, P])
    m.att_T = sb("att_T", [P, W])
    arena = sb("arena", [P, 11 * G * W])
    eighth = lambda k: arena[:, (k + 3) * G * W:(k + 4) * G * W].rearrange("p (g w) -> p g w", w=W)
    m.ek, m.qt, m.ms, m.xn, m.hT, m.eq, m.gs, m.vT = (eighth(k) for k in range(8))
    half = arena[:, :].bitcast(BF16)
    q_size, k_size, parts_size = TILES * SIDES * W, TILES * W, 3 * B * P
    m.q_op = [half[:, r * (q_size + k_size):r * (q_size + k_size) + q_size]
              .rearrange("p (j s t) -> p j s t", s=SIDES, t=W) for r in range(2)]
    m.k_op = [half[:, r * (q_size + k_size) + q_size:(r + 1) * (q_size + k_size)]
              .rearrange("p (j t) -> p j t", t=W) for r in range(2)]
    m.q_zero = arena[:, 0:q_size // 2]
    at = 2 * (q_size + k_size)
    m.q_parts = half[:, at:at + parts_size].rearrange("p (a t) -> p a t", a=3)
    m.kp_self = half[:, at + parts_size:at + 2 * parts_size].rearrange("p (a t) -> p a t", a=3)
    at = at // 2 + parts_size
    m.prob = arena[:, at:at + UNITS * W].rearrange("p (u t) -> p u t", u=UNITS)
    m.hidden = arena[:, 0:2 * FC * W].rearrange("p (r c t) -> p r c t", r=2, c=FC)
    m.bank = [ctx.enter_context(nc.psum_tensor(f"bank{n}", [P, W], F32))[:, :] for n in range(8)]
    return m


def semaphores(nc, ctx):
    s = Names()

    def new(name):
        return ctx.enter_context(nc.semaphore(name))

    s.x_in = [new(f"x_in{g}") for g in range(G)]
    s.ctx_in = [new(f"ctx_in{g}") for g in range(G)]
    s.op_loaded = [[new(f"op_loaded{r}_{part}") for part in range(2)] for r in range(2)]
    s.max_loaded = [new(f"max_loaded{r}") for r in range(2)]
    s.q_spilled = [new(f"q_spilled{j}") for j in range(2 * G)]
    s.k_spilled = [new(f"k_spilled{j}") for j in range(2 * G)]
    s.k_spilled_0 = [new(f"k_spilled_0_{j}") for j in range(G)]
    s.x_again = new("x_again")
    s.cols_in = new("cols_in")
    s.rows_in = new("rows_in")
    s.w_att_in = new("w_att_in")
    s.w_qkv_in = new("w_qkv_in")
    s.w_out_in = new("w_out_in")
    s.w_ffn_in = new("w_ffn_in")
    s.stored = new("stored")
    s.ident_set = new("ident_set")
    s.ident_bf_set = new("ident_bf_set")
    s.half_set = new("half_set")
    s.mask_set = new("mask_set")
    s.v_pad_set = new("v_pad_set")
    s.zero_set = new("zero_set")
    s.ones_set = new("ones_set")
    s.shift_set = new("shift_set")
    s.ring_set = new("ring_set")
    s.bn_done = new("bn_done")
    s.mv_done = new("mv_done")
    s.veps_done = new("veps_done")
    s.rstd_done = new("rstd_done")
    s.nmean_done = new("nmean_done")
    s.xn_ready = new("xn_ready")
    s.bias_added = new("bias_added")
    s.T_done = new("T_done")
    s.hT_ready = new("hT_ready")
    s.wq_loaded = new("wq_loaded")
    s.wv_loaded = new("wv_loaded")
    s.Q_done = new("Q_done")
    s.K_done = new("K_done")
    s.V_done = new("V_done")
    s.TQ_done = new("TQ_done")
    s.M_done = new("M_done")
    s.G_done = new("G_done")
    s.F_done = new("F_done")
    s.nqmax_ready = new("nqmax_ready")
    s.nkmax_ready = new("nkmax_ready")
    s.eq_ready = new("eq_ready")
    s.ek_ready = new("ek_ready")
    s.rq_ready = new("rq_ready")
    s.rk_ready = new("rk_ready")
    s.qt_ready = new("qt_ready")
    s.ms_ready = new("ms_ready")
    s.gs_ready = new("gs_ready")
    s.vT_ready = new("vT_ready")
    s.x_added = new("x_added")
    s.b1_sum = new("b1_sum")
    s.b1_bn = new("b1_bn")
    s.b1_mv = new("b1_mv")
    s.b1_veps = new("b1_veps")
    s.b1_nmean = new("b1_nmean")
    s.b1_rstd = new("b1_rstd")
    s.x1_ready = new("x1_ready")
    s.y_ready = new("y_ready")
    s.t_done = new("t_done")
    s.xT_ready = new("xT_ready")
    s.proj_done = new("proj_done")
    s.first_ready = new("first_ready")
    s.rest_ready = new("rest_ready")
    s.mid_ready = new("mid_ready")
    s.parts_ready = new("parts_ready")
    s.v_done = new("v_done")
    s.v_ready = new("v_ready")
    s.v_pad_ready = new("v_pad_ready")
    s.S_done = new("S_done")
    s.max_done = new("max_done")
    s.negmax_hi = new("negmax_hi")
    s.negmax_rest_ready = new("negmax_rest_ready")
    s.negmax_mid = new("negmax_mid")
    s.negmax_lo = new("negmax_lo")
    s.TM_done = new("TM_done")
    s.negmax_T_ready = new("negmax_T_ready")
    s.ST_done = new("ST_done")
    s.exp_done = new("exp_done")
    s.prob_masked = new("prob_masked")
    s.PV_done = new("PV_done")
    s.o_T_ready = new("o_T_ready")
    s.AT_done = new("AT_done")
    s.o_recip_ready = new("o_recip_ready")
    s.o_ready = new("o_ready")
    s.AO_done = new("AO_done")
    s.att_T_ready = new("att_T_ready")
    s.O_done = new("O_done")
    s.y_added = new("y_added")
    s.a_bn = new("a_bn")
    s.a_mv = new("a_mv")
    s.a_veps = new("a_veps")
    s.a_nmean = new("a_nmean")
    s.a_rstd = new("a_rstd")
    s.a_nmr = new("a_nmr")
    s.a_norm = new("a_norm")
    s.a_scaled = new("a_scaled")
    s.a_shifted = new("a_shifted")
    s.f_base_ready = new("f_base_ready")
    s.f_D_done = new("f_D_done")
    s.f_relu = new("f_relu")
    s.f_H_done = new("f_H_done")
    s.f_sum = new("f_sum")
    s.f_bn1 = new("f_bn1")
    s.f_mv1 = new("f_mv1")
    s.f_veps1 = new("f_veps1")
    s.f_nmean1 = new("f_nmean1")
    s.f_rstd1 = new("f_rstd1")
    s.f_norm1 = new("f_norm1")
    s.f_scaled = new("f_scaled")
    s.f_sum2 = new("f_sum2")
    s.f_bn2 = new("f_bn2")
    s.f_mv2 = new("f_mv2")
    s.f_veps2 = new("f_veps2")
    s.f_nmean2 = new("f_nmean2")
    s.f_rstd2 = new("f_rstd2")
    s.f_nmr1 = new("f_nmr1")
    s.f_nmr2 = new("f_nmr2")
    s.f_out = new("f_out")
    return s



def stage(i, c, back):
    n = G * i + (c - back)
    if isinstance(n, int) and not 0 <= n < ITEMS:
        return None
    return Item(n=n, layer=i + (c - back) // G, g=(c - back) % G)


def slots(eng, slot):
    for c in range(2 + G):
        slot(0, c)
    with eng.Fori(1, DEPTH - 1) as i:
        for c in range(2, 2 + G):
            slot(i, c)
    for c in range(2, 2 + G):
        slot(DEPTH - 1, c)


T_CTX, T_X1, T_X2, T_FFN = 0, 4, 8, 12
M_CTX, M_SELF, M_CROSS = 0, 4, 12
V_CTX, V_SELF = 0, 4
T_BANK, D_BANK = (6, 5), (4, 7)
PROJ = (2, 4)
V_BANK = (3, 1, 3, 1, 3, 1, 1, 3)

LAG_T, LAG_V = 10, 12
SPILLS = 3 * 16
LOADS = 3 * 16


def spill(eng, j, scratch, parts, order, done, sides=range(SIDES)):
    for side in sides:
        to = scratch[j, side].rearrange("a (f i) t -> (f i) a t", i=TILES)
        first = 0
        while first < PAIRS:
            step = order[first + 1] - order[first] if first + 1 < PAIRS else 0
            last = first
            while last + 1 < PAIRS and order[last + 1] - order[last] == step and step >= 0:
                last += 1
            n, source = last + 1 - first, parts[64 * side:64 * side + 64, :, group(j % G)]
            source = source[:, order[first]:order[first] + n, :] if step == 1 else \
                source[:, order[first]:order[first] + 1, :].to_broadcast([64, n, W])
            eng.dma_start(to[:, first:first + n, :], source).then_inc(done[j], 16)
            first = last + 1



def sync_program(sp, m, s, a):
    tokens = lambda dram, g: dram[GB * g:GB * g + GB].rearrange("b n d -> n b d")
    sp.dma_start(per_batch(m.xr[:, group(0)]), tokens(a.x, 0)).then_inc(s.x_in[0], 16)
    sp.dma_start(per_batch(m.y[:, group(0)]), tokens(a.context, 0)).then_inc(s.ctx_in[0], 16)
    sp.dma_start(m.col[:, :], a.cols).then_inc(s.cols_in, 16)
    sp.dma_start(m.w_att[:, :, :], a.w_att.rearrange("l d c -> d l c")).then_inc(s.w_att_in, 16)
    sp.dma_start(m.row[:, :, :], a.rows.rearrange("r (a d) -> a r d", a=1).to_broadcast([P, NROWS, P])).then_inc(s.rows_in, 16)
    for g in range(1, G):
        sp.dma_start(per_batch(m.y[:, group(g)]), tokens(a.context, g)).then_inc(s.ctx_in[g], 16)
        sp.dma_start(per_batch(m.xr[:, group(g)]), tokens(a.x, g)).then_inc(s.x_in[g], 16)
        if g == 1:
            sp.dma_start(m.w_qkv[:, :, :], a.w_qkv.rearrange("l d c -> d l c")).then_inc(s.w_qkv_in, 16)
    sp.dma_start(m.w_out[:, :, :], a.w_out.rearrange("l d c -> d l c")).then_inc(s.w_out_in, 16)
    sp.dma_start(m.x0[:, :].rearrange("p (b d) -> p b d", d=P), a.x.rearrange("b n d -> n b d")).then_inc(s.x_again, 16)
    sp.dma_start(m.w1[:, :, :], a.w1.rearrange("f d c -> d f c")).then_inc(s.w_ffn_in, 16)
    sp.dma_start(m.w2[:, :, :, :], a.w2.rearrange("f (c h) e -> h f c e", c=FC)).then_inc(s.w_ffn_in, 16)

    def load(j):
        ring = j % 2
        sp.wait_ge(s.q_spilled[j], SIDES * SPILLS)
        if 0 < j < G:
            sp.wait_ge(s.k_spilled[j], SPILLS)
            sp.wait_ge(s.k_spilled_0[j], SPILLS)
        else:
            sp.wait_ge(s.k_spilled[j], SIDES * SPILLS)
        for part in range(2):
            tiles = slice(part * TILES // 2, (part + 1) * TILES // 2)
            for side in range(SIDES):
                sp.dma_start(m.q_op[ring][side * ROWS:side * ROWS + ROWS, tiles, side, :],
                             a.q_rows[j, side].rearrange("a (f i) t -> (a f) i t", i=TILES)[:, tiles, :])\
                  .then_inc(s.op_loaded[ring][part], 16)
            sp.dma_start(m.k_op[ring][0:OP, tiles, :], a.k_rows[j].rearrange("s a (f i) t -> (s a f) i t", i=TILES)[:, tiles, :])\
              .then_inc(s.op_loaded[ring][part], 16)

    for g in range(G):
        sp.wait_ge(s.parts_ready, M_CTX + g + 1)
        spill(sp, G + g, a.k_rows, m.kp_cross, K_PARTS, s.k_spilled)
    sp.wait_ge(s.G_done, ITEMS)
    sp.wait_ge(s.zero_set, 1)
    sp.wait_ge(s.ones_set, 1)
    sp.dma_start(m.q_op[1][0:OP, :, :, :], m.q_op[0][0:OP, :, :, :]).then_inc(s.ring_set, 16)
    sp.dma_start(m.k_op[1][MAX_ROWS, :, :], m.k_op[0][MAX_ROWS, :, :]).then_inc(s.ring_set, 16)
    def self_spill(g):
        sp.wait_ge(s.parts_ready, M_SELF + 2 * g + 1)
        spill(sp, g, a.q_rows, m.q_parts, Q_PARTS, s.q_spilled)
        sp.wait_ge(s.parts_ready, M_SELF + 2 * g + 2)
        spill(sp, g, a.k_rows, m.kp_self, K_PARTS, s.k_spilled, (1,) if g else (0, 1))

    self_spill(0)
    sp.wait_ge(s.ring_set, 32)
    load(0)
    self_spill(1)
    for k in range(ALL):
        sp.wait_ge(s.negmax_T_ready, k + 1)
        at_least(sp, s.ST_done, UNITS * (k - 7))
        sp.dma_start(m.q_op[k // GB % 2][MAX_ROWS, :, :, columns(k % GB)].rearrange("a j s t -> a (j s) t"),
                     m.negmax_T[:, k % 2, :]).then_inc(s.max_loaded[k % 2], 16)
        if k == 0:
            load(1)
        if k in (1, 3):
            self_spill((k + 3) // 2)
        g = (k - 11) // GB
        if k % GB == 3 and 0 <= g < G:
            sp.wait_ge(s.parts_ready, M_CROSS + g + 1)
            spill(sp, G + g, a.q_rows, m.q_parts, Q_PARTS, s.q_spilled)
        j = (k + 3) // GB
        if k % GB == 1 and 2 <= j < 2 * G:
            sp.wait_ge(s.ST_done, UNITS * GB * (j - 1))
            load(j)

    for g in range(G):
        sp.wait_ge(s.f_out, G + g + 1)
        sp.dma_start(tokens(a.out, g), per_batch(m.y[:, group(g)])).then_inc(s.stored, 16)
    sp.wait_ge(s.stored, 16 * G)



def gpsimd_program(pool, m, s, a):
    pool.memset(m.ident[:, :], 0.0).then_inc(s.ident_set, 1)
    pool.memset(m.ident_bf[:, :], 0.0).then_inc(s.ident_bf_set, 1)
    pool.memset(m.minus_half[:, :], -0.5).then_inc(s.half_set, 1)
    pool.wait_ge(s.ident_set, 1)
    pool.affine_select(out=m.ident[:, :], in_=m.ident[:, :], compare_op=ALU.not_equal, fill=1.0, base=0,
                       pattern=[[-1, P]], channel_multiplier=1).then_inc(s.ident_set, 1)
    pool.wait_ge(s.ident_bf_set, 1)
    pool.affine_select(out=m.ident_bf[:, :], in_=m.ident_bf[:, :], compare_op=ALU.not_equal, fill=1.0, base=0,
                       pattern=[[-1, P]], channel_multiplier=1).then_inc(s.ident_bf_set, 1)
    pool.wait_ge(s.half_set, 1)

    def norm(it):
        n, g = it.n, it.g
        wait_apart(pool, s, (s.mv_done, GB * n + GB),
                            (s.xn_ready, n - 3))
        pool.tensor_scalar(m.veps[:, g, :], m.mv[:, g, :, 1], EPS, None, ALU.add).then_inc(s.veps_done, 1)
        pool.tensor_scalar(m.nmean[:, g, :], m.mv[:, g, :, 0], -1.0, None, ALU.mult).then_inc(s.nmean_done, 1)
        pool.wait_ge(s.veps_done, n + 1)
        pool.tensor_tensor(m.rstd[:, g, :], m.veps[:, g, :], m.minus_half[:, :], ALU.pow).then_inc(s.rstd_done, 1)
        wait_apart(pool, s, (s.nmean_done, n + 1), (s.rstd_done, n + 1),
                            (s.T_done, n - 3))
        for b in range(GB):
            last = pool.tensor_scalar(m.xn[:, g, columns(b)], m.xr[:, columns(GB * g + b)],
                                      m.nmean[:, g, b:b + 1], m.rstd[:, g, b:b + 1], ALU.add, ALU.mult)
        last.then_inc(s.xn_ready, 1)
        if isinstance(n, int) and n < 2:
            pool.wait_ge(s.rows_in, 16)
        wait_apart(pool, s, (s.xn_ready, n + 1))
        xg = per_batch(m.xr[:, group(g)])
        pool.tensor_tensor(xg, xg, each_batch(m.row[:, it.layer, :]), ALU.add).then_inc(s.bias_added, 1)

    norm(stage(0, 0, 0))
    norm(stage(0, 1, 0))
    def slot(i, c):
        coming = stage(i, c, -2)
        if coming:
            norm(coming)
        if not isinstance(i, int) or i:
            return
        if c == 0:
            pool.memset(m.mask[:, :, :], 0.0).then_inc(s.mask_set, 1)
            pool.wait_ge(s.mask_set, 1)
            pool.affine_select(out=m.mask[:, :, :], in_=m.mask[:, :, :], compare_op=ALU.is_ge, fill=MASKED, base=0,
                               pattern=[[0, GB], [-1, P]], channel_multiplier=1).then_inc(s.mask_set, 1)
        if c == 1:
            pool.memset(m.v_pad[:, :, :, :], 0.0).then_inc(s.v_pad_set, 1)
            pool.wait_ge(s.v_pad_set, 1)
            pool.memset(m.v_pad[:, :, :, DH:DH + 1], 1.0).then_inc(s.v_pad_set, 1)
        if c == 2:
            pool.memset(m.q_zero, 0.0).then_inc(s.zero_set, 1)
        if c == 3:
            pool.wait_ge(s.bias_added, coming.n + 1)
            pool.memset(m.k_op[0][MAX_ROWS, :, :], 1.0).then_inc(s.ones_set, 1)
            pool.wait_ge(s.ones_set, 1)
        if c == 4:
            pool.tensor_tensor(m.row[:, R_SA_BT, :], m.row[:, R_SA_BT, :], m.row[:, R_CA_BO, :], ALU.add).then_inc(s.shift_set, 1)

    slots(pool, slot)

    for g in range(G):
        pool.wait_ge(s.b1_mv, GB * g + GB)
        if g == 0:
            pool.wait_ge(s.xn_ready, ITEMS)
        pool.tensor_scalar(m.veps[:, g, :], m.mv[:, g, :, 1], EPS, None, ALU.add).then_inc(s.b1_veps, 1)
        pool.tensor_scalar(m.nmean[:, g, :], m.mv[:, g, :, 0], -1.0, None, ALU.mult).then_inc(s.b1_nmean, 1)
        pool.wait_ge(s.b1_veps, g + 1)
        pool.tensor_tensor(m.rstd[:, g, :], m.veps[:, g, :], m.minus_half[:, :], ALU.pow).then_inc(s.b1_rstd, 1)
        pool.wait_ge(s.b1_nmean, g + 1)
        pool.wait_ge(s.b1_rstd, g + 1)
        for b in range(GB):
            last = pool.tensor_scalar(m.x0[:, columns(GB * g + b)], m.xr[:, columns(GB * g + b)],
                                      m.nmean[:, g, b:b + 1], m.rstd[:, g, b:b + 1], ALU.add, ALU.mult)
        last.then_inc(s.x1_ready, 1)
    for g in range(1, G):
        pool.wait_ge(s.parts_ready, M_SELF + 2 * g + 2)
        spill(pool, g, a.k_rows, m.kp_self, K_PARTS, s.k_spilled_0, (0,))
    for g in range(G):
        pool.wait_ge(s.x1_ready, g + 1)
        pool.tensor_tensor(per_batch(m.y[:, group(g)]), per_batch(m.x0[:, group(g)]), each_batch(m.row[:, R_SA_BO, :]),
                           ALU.add).then_inc(s.y_ready, 1)

    def bases(k):
        f, g = k // G, k % G
        yg, xg, bg = (per_batch(t[:, group(g)]) for t in (m.y, m.xr, m.x0))
        if f == 0:
            pool.wait_ge(s.a_shifted, G + g + 1)
        else:
            pool.wait_ge(s.f_out, k - G + 1)
        pool.tensor_tensor(xg, yg, each_batch(m.row[:, R_B2 + 3 * f, :]), ALU.add).then_inc(s.f_base_ready, 1)
        pool.tensor_tensor(bg, bg if f == 0 else yg, each_batch(m.row[:, R_BT + 3 * f, :]), ALU.add).then_inc(s.f_base_ready, 1)

    pool.wait_ge(s.v_pad_set, 2)
    for n in range(ALL + 7):
        for u in range(UNITS):
            k, v = unit_at(n, u, LAG_T)
            if 0 <= k < B:
                pool.wait_ge(s.exp_done, UNITS * k + v + 1)
                prob = m.prob[:, v, :].rearrange("p (h t) -> p h t", t=P)
                pool.affine_select(out=prob, in_=prob, compare_op=ALU.is_ge, fill=0.0, base=0,
                                   pattern=[[0, GB], [1, P]], channel_multiplier=-1).then_inc(s.prob_masked, 1)
            k = n - 2
            if u == 1 and 0 <= k < ALL:
                pool.wait_ge(s.v_ready, V_SELF + G if k < B else V_CTX + G)
                at_least(pool, s.PV_done, UNITS * (k - 1))
                v = (m.v_self, m.v_cross)[k // B]
                pool.tensor_copy(m.v_pad[:, k % 2, :, 0:DH], v[:, k % B, :].rearrange("p (h d) -> p h d", d=DH))\
                    .then_inc(s.v_pad_ready, 1)
            gg = (n - 9) // GB
            if u == 0 and n % GB == 1 and 0 <= gg < 2 * G:
                g = gg % G
                pool.wait_ge(s.a_mv, GB * gg + GB)
                pool.tensor_scalar(m.veps[:, g, :], m.mv[:, g, :, 1], EPS, None, ALU.add).then_inc(s.a_veps, 1)
                pool.tensor_scalar(m.nmean[:, g, :], m.mv[:, g, :, 0], -1.0, None, ALU.mult).then_inc(s.a_nmean, 1)
                pool.wait_ge(s.a_veps, gg + 1)
                pool.tensor_tensor(m.rstd[:, g, :], m.veps[:, g, :], m.minus_half[:, :], ALU.pow).then_inc(s.a_rstd, 1)
                pool.wait_ge(s.a_nmean, gg + 1)
                pool.wait_ge(s.a_rstd, gg + 1)
                pool.tensor_tensor(m.nmr[:, g, :], m.nmean[:, g, :], m.rstd[:, g, :], ALU.mult).then_inc(s.a_nmr, 1)
            gg = (n - 10) // GB
            if n % GB == 2 and 0 <= gg < 2 * G:
                r_g, r_bt = ((R_SA_G, R_SA_BT), (R_CA_G, R_CA_BT))[gg // G]
                yg = per_batch(m.y[:, group(gg % G)])
                if u == 1:
                    pool.wait_ge(s.a_norm, 2 * gg + 2)
                    if gg < G:
                        pool.wait_ge(s.shift_set, 1)
                        pool.wait_ge(s.t_done, T_X2 + gg + 1)
                    pool.tensor_tensor(yg, yg, each_batch(m.row[:, r_g, :]), ALU.mult).then_inc(s.a_scaled, 1)
                if u == 3:
                    pool.wait_ge(s.a_scaled, gg + 1)
                    pool.tensor_tensor(yg, yg, each_batch(m.row[:, r_bt, :]), ALU.add).then_inc(s.a_shifted, 1)
        g = (n - 11) // GB - G
        if n % GB == 3 and 0 <= g < G - 1:
            bases(g)

    for k in range(FFN_ITEMS + 2):
        if G - 1 <= k < FFN_ITEMS:
            bases(k)
        if 1 <= k <= FFN_ITEMS:
            j, g = k - 1, (k - 1) % G
            pool.wait_ge(s.f_mv1, GB * j + GB)
            pool.tensor_scalar(m.veps[:, g, :], m.mv[:, g, :, 1], EPS, None, ALU.add).then_inc(s.f_veps1, 1)
            pool.tensor_scalar(m.nmean[:, g, :], m.mv[:, g, :, 0], -1.0, None, ALU.mult).then_inc(s.f_nmean1, 1)
            pool.wait_ge(s.f_veps1, j + 1)
            pool.tensor_tensor(m.rstd[:, g, :], m.veps[:, g, :], m.minus_half[:, :], ALU.pow).then_inc(s.f_rstd1, 1)
            pool.wait_ge(s.f_nmean1, j + 1)
            pool.wait_ge(s.f_rstd1, j + 1)
            pool.tensor_tensor(m.nmr[:, g, :], m.nmean[:, g, :], m.rstd[:, g, :], ALU.mult).then_inc(s.f_nmr1, 1)
        if k >= 2:
            j, g = k - 2, (k - 2) % G
            pool.wait_ge(s.f_mv2, GB * j + GB)
            pool.tensor_scalar(m.veps[:, g, :], m.mv[:, g, :, 1], EPS, None, ALU.add).then_inc(s.f_veps2, 1)
            pool.tensor_scalar(m.nmean[:, g, :], m.mv[:, g, :, 0], -1.0, None, ALU.mult).then_inc(s.f_nmean2, 1)
            pool.wait_ge(s.f_veps2, j + 1)
            pool.tensor_tensor(m.rstd[:, g, :], m.veps[:, g, :], m.minus_half[:, :], ALU.pow).then_inc(s.f_rstd2, 1)
            pool.wait_ge(s.f_nmean2, j + 1)
            pool.wait_ge(s.f_rstd2, j + 1)
            pool.tensor_tensor(m.nmr[:, g, :], m.nmean[:, g, :], m.rstd[:, g, :], ALU.mult).then_inc(s.f_nmr2, 1)



def vector_program(dve, m, s):
    pT, pTQ, pQ, pK, pV, pM, pG, pF = m.bank

    def stats(it, first):
        n, g = it.n, it.g
        if first:
            dve.wait_ge(s.x_in[g], 16)
        else:
            wait_apart(dve, s, (s.x_added, n - 3),
                               (s.mv_done, GB * (n - 3)))
        for b in range(GB):
            last = dve.bn_stats(m.bn[:, g, b, :], m.xr[:, columns(GB * g + b)])
        last.then_inc(s.bn_done, 1)
        wait_apart(dve, s, (s.bn_done, n + 1),
                           (s.nmean_done, n - 3), (s.veps_done, n - 3))
        for b in range(GB):
            dve.bn_aggr(m.mv[:, g, b, :], m.bn[:, g, b, :]).then_inc(s.mv_done, 1)

    def first_rest(k, bank, parts, g, bias):
        dve.wait_ge(s.first_ready, k + 1)
        at_least(dve, s.parts_ready, k - 1)
        dve.scalar_tensor_tensor(m.rest[:, k % 2, :], m.bank[bank], m.col[:, bias:bias + 1], parts[:, 0, group(g)], ALU.add, ALU.subtract)\
           .then_inc(s.rest_ready, 1)

    def last_part(k, parts, g):
        dve.wait_ge(s.mid_ready, k + 1)
        dve.tensor_tensor(parts[:, 2, group(g)], m.rest[:, k % 2, :], parts[:, 1, group(g)], ALU.subtract).then_inc(s.parts_ready, 1)

    def values(k, v, g, bias):
        dve.wait_ge(s.v_done, k + 1)
        dve.tensor_tensor(v[:, GB * g:GB * g + GB, :], per_batch(m.bank[V_BANK[k]]), each_batch(m.row[:, bias, :]), ALU.add)\
           .then_inc(s.v_ready, 1)

    def self_parts(g):
        first_rest(M_SELF + 2 * g, PROJ[0], m.q_parts, g, C_BQ)
        first_rest(M_SELF + 2 * g + 1, PROJ[1], m.kp_self, g, C_BK)
        last_part(M_SELF + 2 * g, m.q_parts, g)
        last_part(M_SELF + 2 * g + 1, m.kp_self, g)

    def outcome(g):
        dve.wait_ge(s.x_added, ITEMS - G + g + 1)
        dve.wait_ge(s.x_again, 16)
        dve.wait_ge(s.xn_ready, ITEMS - G + g + 1)
        dve.wait_ge(s.bias_added, ITEMS - G + g + 1)
        dve.tensor_tensor(m.xr[:, group(g)], m.xr[:, group(g)], m.x0[:, group(g)], ALU.add).then_inc(s.b1_sum, 1)
        dve.wait_ge(s.b1_sum, g + 1)
        dve.wait_ge(s.mv_done, GB * (ITEMS - G + g + 1))
        for b in range(GB):
            last = dve.bn_stats(m.bn[:, g, b, :], m.xr[:, columns(GB * g + b)])
        last.then_inc(s.b1_bn, 1)
        dve.wait_ge(s.b1_bn, g + 1)
        dve.wait_ge(s.nmean_done, ITEMS - G + g + 1)
        dve.wait_ge(s.veps_done, ITEMS - G + g + 1)
        for b in range(GB):
            dve.bn_aggr(m.mv[:, g, b, :], m.bn[:, g, b, :]).then_inc(s.b1_mv, 1)

    stats(stage(0, 0, 0), True)
    stats(stage(0, 1, 0), True)
    dve.wait_ge(s.cols_in, 16)
    dve.wait_ge(s.w_qkv_in, 16)
    dve.tensor_copy(m.wq_now[:, :], m.w_qkv[:, 0, 0:P]).then_inc(s.wq_loaded, 1)
    dve.tensor_copy(m.wv_now[:, :], m.w_qkv[:, 0, 2 * P:3 * P]).then_inc(s.wv_loaded, 1)

    dve.wait_ge(s.rows_in, 16)
    for g in range(G):
        first_rest(M_CTX + g, PROJ[g % 2], m.kp_cross, g, C_BK + 2)
        last_part(M_CTX + g, m.kp_cross, g)
        values(V_CTX + g, m.v_cross, g, R_CA_BV)

    def slot(i, c):
        now, one, two, coming = (stage(i, c, back) for back in (0, 1, 2, -2))
        if one:
            n, g = one.n, one.g
            dve.wait_ge(s.ek_ready, n + 1)
            at_least(dve, s.qt_ready, n - 3)
            dve.reciprocal(m.rk[:, g, :], m.ksum[:, g, :]).then_inc(s.rk_ready, 1)
            dve.wait_ge(s.eq_ready, n + 1)
            at_least(dve, s.ms_ready, n - 3)
            dve.reciprocal(m.rq[:, g, :], m.qsum[:, g, :]).then_inc(s.rq_ready, 1)
            dve.wait_ge(s.TQ_done, n + 1)
            dve.wait_ge(s.rk_ready, n + 1)
            at_least(dve, s.M_done, n - 3)
            dve.tensor_tensor(per_batch(m.qt[:, g, :]), per_batch(pTQ), spread(m.rk[:, g, :], P), ALU.mult).then_inc(s.qt_ready, 1)
        if two:
            n, g = two.n, two.g
            dve.wait_ge(s.F_done, n + 1)
            dve.wait_ge(s.bias_added, n + 1)
            dve.tensor_tensor(m.xr[:, group(g)], pF, m.xr[:, group(g)], ALU.add).then_inc(s.x_added, 1)
        if now:
            n, g = now.n, now.g
            if c == G:
                dve.wait_ge(s.V_done, n)
                dve.tensor_copy(m.wv_now[:, :], m.w_qkv[:, now.layer, 2 * P:3 * P]).then_inc(s.wv_loaded, 1)
            dve.wait_ge(s.Q_done, n + 1)
            at_least(dve, s.eq_ready, n - 3)
            dve.tensor_reduce(m.nqmax[:, g, :], per_batch(pQ), AX.X, ALU.max, negate=True).then_inc(s.nqmax_ready, 1)
            after = stage(i, c, -1)
            if c == G - 1 and after:
                dve.tensor_copy(m.wq_now[:, :], m.w_qkv[:, after.layer, 0:P]).then_inc(s.wq_loaded, 1)
        if one:
            n, g = one.n, one.g
            dve.wait_ge(s.M_done, n + 1)
            dve.wait_ge(s.rq_ready, n + 1)
            at_least(dve, s.G_done, n - 3)
            dve.tensor_tensor(per_batch(m.ms[:, g, :]), per_batch(pM), spread(m.rq[:, g, :], P), ALU.mult).then_inc(s.ms_ready, 1)
        if now:
            n, g = now.n, now.g
            dve.wait_ge(s.K_done, n + 1)
            at_least(dve, s.ek_ready, n - 3)
            dve.tensor_reduce(m.nkmax[:, g, :], per_batch(pK), AX.X, ALU.max, negate=True).then_inc(s.nkmax_ready, 1)
        if coming:
            stats(coming, first=isinstance(i, int) and i == 0 and c < 2)
        if two and isinstance(i, int) and i == DEPTH - 1:
            outcome(two.g)
            if c == G:
                dve.wait_ge(s.TQ_done, ITEMS)
                dve.wait_ge(s.V_done, ITEMS)
                self_parts(0)
            if c == G + 1:
                values(V_SELF, m.v_self, 0, R_SA_BV)
                self_parts(1)
                values(V_SELF + 1, m.v_self, 1, R_SA_BV)

    slots(dve, slot)

    for g in range(2, G):
        self_parts(g)
        values(V_SELF + g, m.v_self, g, R_SA_BV)

    for n in range(ALL + 5):
        for u in range(UNITS):
            if n < ALL:
                dve.wait_ge(s.S_done, UNITS * n + u + 1)
                at_least(dve, s.negmax_rest_ready, n - 1)
                dve.tensor_reduce(m.negmax[:, n % 2, GB * u:GB * u + GB], per_batch(m.bank[u % 2]), AX.X, ALU.max, negate=True)\
                   .then_inc(s.max_done, 1)
            gg = (n - 8) // GB
            g = gg % G
            if u == 2 and n % GB == 0 and 0 <= gg < 2 * G:
                dve.wait_ge(s.O_done, gg + 1)
                dve.wait_ge(*((s.y_ready, gg + 1) if gg < G else (s.a_shifted, gg - G + 1)))
                dve.tensor_tensor(m.y[:, group(g)], m.bank[7], m.y[:, group(g)], ALU.add).then_inc(s.y_added, 1)
            cross = (n - 11) // GB
            if u == 1 and n % GB == 3 and 0 <= cross < G:
                first_rest(M_CROSS + cross, 4, m.q_parts, cross, C_BQ + 2)
            if u == 2 and n % GB == 3 and 0 <= cross < G:
                dve.wait_ge(s.rest_ready, M_CROSS + cross + 1)
                dve.tensor_copy(m.q_parts[:, 1, group(cross)], m.rest[:, cross % 2, :]).then_inc(s.mid_ready, 1)
                last_part(M_CROSS + cross, m.q_parts, cross)
        k = n - 4
        if 0 <= k < ALL:
            o = m.bank[4].rearrange("p (h e) -> p h e", e=VW)
            dve.wait_ge(s.AT_done, k + 1)
            at_least(dve, s.o_ready, k - 1)
            dve.reciprocal(m.o_recip[:, k % 2, :].unsqueeze(2), o[:, :, DH:DH + 1]).then_inc(s.o_recip_ready, 1)
            dve.wait_ge(s.o_recip_ready, k + 1)
            at_least(dve, s.AO_done, k - 1)
            dve.tensor_tensor(m.o[:, k % 2, :].rearrange("p (s j d) -> p j s d", s=SIDES, d=DH),
                              m.bank[4].rearrange("p (j s e) -> p j s e", s=SIDES, e=VW)[:, :, :, 0:DH],
                              m.o_recip[:, k % 2, :].rearrange("p (j s) -> p j s", s=SIDES).unsqueeze(3)
                              .to_broadcast([P, TILES, SIDES, DH]), ALU.mult).then_inc(s.o_ready, 1)
        if n < ALL:
            parts = m.negmax_parts[:, n % 2, :].rearrange("p (a h) -> p a h", a=3)
            neg, rest = m.negmax[:, n % 2, :], m.negmax_rest[:, n % 2, :]
            dve.wait_ge(s.max_done, UNITS * n + UNITS)
            at_least(dve, s.TM_done, n - 1)
            dve.tensor_copy(parts[:, 0, :], neg).then_inc(s.negmax_hi, 1)
            dve.wait_ge(s.negmax_hi, n + 1)
            at_least(dve, s.negmax_lo, n - 1)
            dve.tensor_tensor(rest, neg, parts[:, 0, :], ALU.subtract).then_inc(s.negmax_rest_ready, 1)
            dve.wait_ge(s.negmax_rest_ready, n + 1)
            dve.tensor_copy(parts[:, 1, :], rest).then_inc(s.negmax_mid, 1)
            dve.wait_ge(s.negmax_mid, n + 1)
            dve.tensor_tensor(parts[:, 2, :], rest, parts[:, 1, :], ALU.subtract).then_inc(s.negmax_lo, 1)
        if n % GB == 0 and 0 <= gg < 2 * G:
            dve.wait_ge(s.y_added, gg + 1)
            if gg >= G:
                dve.wait_ge(s.a_mv, GB * (gg - G) + GB)
            for b in range(GB):
                last = dve.bn_stats(m.bn[:, g, b, :], m.y[:, columns(GB * g + b)])
            last.then_inc(s.a_bn, 1)
            dve.wait_ge(s.a_bn, gg + 1)
            if gg < G:
                dve.wait_ge(s.b1_nmean, gg + 1)
                dve.wait_ge(s.b1_veps, gg + 1)
            else:
                dve.wait_ge(s.a_nmean, gg - G + 1)
                dve.wait_ge(s.a_veps, gg - G + 1)
            for b in range(GB):
                dve.bn_aggr(m.mv[:, g, b, :], m.bn[:, g, b, :]).then_inc(s.a_mv, 1)

    for k in range(FFN_ITEMS + 1):
        if k < FFN_ITEMS:
            g = k % G
            dve.wait_ge(s.f_D_done, k + 1)
            dve.wait_ge(s.f_base_ready, 2 * k + 2)
            dve.tensor_tensor(m.xr[:, group(g)], m.bank[D_BANK[k % 2]], m.xr[:, group(g)], ALU.add).then_inc(s.f_sum, 1)
            dve.wait_ge(s.f_sum, k + 1)
            if k >= G:
                dve.wait_ge(s.f_mv2, GB * (k - G) + GB)
                dve.wait_ge(s.f_nmean2, k - G + 1)
                dve.wait_ge(s.f_veps2, k - G + 1)
            for b in range(GB):
                last = dve.bn_stats(m.bn[:, g, b, :], m.xr[:, columns(GB * g + b)])
            last.then_inc(s.f_bn1, 1)
            dve.wait_ge(s.f_bn1, k + 1)
            for b in range(GB):
                dve.bn_aggr(m.mv[:, g, b, :], m.bn[:, g, b, :]).then_inc(s.f_mv1, 1)
        if k >= 1:
            j, g = k - 1, (k - 1) % G
            dve.wait_ge(s.f_norm1, j + 1)
            xg = per_batch(m.xr[:, group(g)])
            dve.tensor_tensor(xg, xg, each_batch(m.row[:, R_G + 3 * (j // G), :]), ALU.mult).then_inc(s.f_scaled, 1)
            dve.wait_ge(s.f_scaled, j + 1)
            dve.tensor_tensor(m.xr[:, group(g)], m.xr[:, group(g)], m.x0[:, group(g)], ALU.add).then_inc(s.f_sum2, 1)
            dve.wait_ge(s.f_sum2, j + 1)
            dve.wait_ge(s.f_mv1, GB * j + GB)
            for b in range(GB):
                last = dve.bn_stats(m.bn[:, g, b, :], m.xr[:, columns(GB * g + b)])
            last.then_inc(s.f_bn2, 1)
            dve.wait_ge(s.f_bn2, j + 1)
            for b in range(GB):
                dve.bn_aggr(m.mv[:, g, b, :], m.bn[:, g, b, :]).then_inc(s.f_mv2, 1)



def scalar_program(act, m, s):
    pT, pTQ, pQ, pK, pV, pM, pG, pF = m.bank

    def transposed(t):
        act.wait_ge(s.t_done, t + 1)
        act.activation(m.xT[:, t % G, :], m.bank[0], ACT.Copy).then_inc(s.xT_ready, 1)

    def first_part(k, bank, parts, g, bias):
        act.wait_ge(s.proj_done, k + 1)
        act.activation(parts[:, 0, group(g)], m.bank[bank], ACT.Identity, bias=m.col[:, bias:bias + 1]).then_inc(s.first_ready, 1)

    def middle_part(k, parts, g):
        act.wait_ge(s.rest_ready, k + 1)
        act.activation(parts[:, 1, group(g)], m.rest[:, k % 2, :], ACT.Copy).then_inc(s.mid_ready, 1)

    act.wait_ge(s.cols_in, 16)
    for g in range(G + 1):
        if g < G:
            transposed(T_CTX + g)
        if g:
            first_part(M_CTX + g - 1, PROJ[(g - 1) % 2], m.kp_cross, g - 1, C_BK + 2)
            middle_part(M_CTX + g - 1, m.kp_cross, g - 1)

    def slot(i, c):
        now, one = (stage(i, c, back) for back in (0, 1))
        if now:
            n, g = now.n, now.g
            wait_apart(act, s, (s.T_done, n + 1), (s.V_done, n - 3))
            act.activation(m.hT[:, g, :], pT, ACT.Identity, bias=m.col[:, bass.ds(DEPTH + now.layer, 1)],
                           scale=m.col[:, bass.ds(now.layer, 1)]).then_inc(s.hT_ready, 1)
            act.wait_ge(s.nqmax_ready, n + 1)
            at_least(act, s.TQ_done, n - 3)
            at_least(act, s.rq_ready, n - 3)
            for b in range(GB):
                last = act.activation(m.eq[:, g, columns(b)], pQ[:, columns(b)], ACT.Exp, bias=m.nqmax[:, g, b:b + 1],
                                      accum_out=m.qsum[:, g, b:b + 1])
            last.then_inc(s.eq_ready, 1)
            act.wait_ge(s.nkmax_ready, n + 1)
            at_least(act, s.M_done, n - 3)
            at_least(act, s.rk_ready, n - 3)
            for b in range(GB):
                last = act.activation(m.ek[:, g, columns(b)], pK[:, columns(b)], ACT.Exp, bias=m.nkmax[:, g, b:b + 1],
                                      accum_out=m.ksum[:, g, b:b + 1])
            last.then_inc(s.ek_ready, 1)
        if one:
            n, g = one.n, one.g
            act.wait_ge(s.G_done, n + 1)
            at_least(act, s.F_done, n - 3)
            act.activation(m.gs[:, g, :], pG, ACT.Copy).then_inc(s.gs_ready, 1)
        if now:
            n, g = now.n, now.g
            act.wait_ge(s.V_done, n + 1)
            at_least(act, s.F_done, n - 3)
            act.activation(m.vT[:, g, :], pV, ACT.Copy).then_inc(s.vT_ready, 1)
        if isinstance(i, int) and i == DEPTH - 1 and c >= G - 1:
            if c == G:
                act.wait_ge(s.TQ_done, ITEMS)
                act.wait_ge(s.V_done, ITEMS)
            self_step(c - G + 1)

    def self_step(g):
        if g < G:
            transposed(T_X1 + g)
        if g:
            first_part(M_SELF + 2 * g - 2, PROJ[0], m.q_parts, g - 1, C_BQ)
            first_part(M_SELF + 2 * g - 1, PROJ[1], m.kp_self, g - 1, C_BK)
            middle_part(M_SELF + 2 * g - 2, m.q_parts, g - 1)
            middle_part(M_SELF + 2 * g - 1, m.kp_self, g - 1)

    slots(act, slot)
    for g in range(3, G + 1):
        self_step(g)

    def ffn_tokens(k):
        act.wait_ge(s.t_done, T_FFN + k + 1)
        act.activation(m.xT[:, k % G, :], m.bank[T_BANK[k % 2]], ACT.Copy).then_inc(s.xT_ready, 1)

    def hidden(k):
        for c in range(FC):
            act.wait_ge(s.f_H_done, FC * k + c + 1)
            at_least(act, s.f_D_done, k - 1)
            bias = C_B1 + FC * (k // G) + c
            act.activation(m.hidden[:, k % 2, c, :], m.bank[c], ACT.Relu, bias=m.col[:, bias:bias + 1]).then_inc(s.f_relu, 1)

    act.wait_ge(s.F_done, ITEMS)
    for n in range(ALL + 6):
        for u in range(UNITS):
            g = (n - 8) // GB
            if u == 1 and n % GB == 0 and 0 <= g < 2 * G:
                act.wait_ge(s.AO_done, GB * g + GB)
                at_least(act, s.O_done, g)
                act.activation(m.att_T[:, :], m.bank[7], ACT.Copy).then_inc(s.att_T_ready, 1)
            if u == 3 and n == ALL + 3:
                ffn_tokens(0)
            if u == 3 and n == ALL + 4:
                hidden(0)
            g = (n - 10) // GB
            if u == 1 and n % GB == 2 and 0 <= g < G:
                act.wait_ge(s.t_done, T_X2 + g + 1)
                act.activation(m.xT[:, g, :], m.bank[4], ACT.Identity, bias=m.col[:, C_SA_BT:C_SA_BT + 1],
                               scale=m.col[:, C_SA_G:C_SA_G + 1]).then_inc(s.xT_ready, 1)
            g = (n - 11) // GB
            if u == 1 and n % GB == 3 and 0 <= g < G:
                act.wait_ge(s.q_spilled[g], SIDES * SPILLS)
                first_part(M_CROSS + g, 4, m.q_parts, g, C_BQ + 2)
            k, v = unit_at(n, u, LAG_T)
            if k >= 0:
                act.wait_ge(s.ST_done, UNITS * k + v + 1)
                at_least(act, s.PV_done, UNITS * (k - 1) + v + 1)
                act.activation(m.prob[:, v, :], m.bank[2 + v % 2], ACT.Exp, scale=SCALE).then_inc(s.exp_done, 1)
            g = (n - 9) // GB
            if u in (2, 3) and n % GB == 1 and 0 <= g < 2 * G:
                act.wait_ge(s.a_nmr, g + 1)
                for b in range(2 * u - 4, 2 * u - 2):
                    yb = m.y[:, columns(GB * (g % G) + b)]
                    last = act.activation(yb, yb, ACT.Identity, bias=m.nmr[:, g % G, b:b + 1], scale=m.rstd[:, g % G, b:b + 1])
                last.then_inc(s.a_norm, 1)
            k = n - 1
            if u == 1 and 0 <= k < ALL:
                act.wait_ge(s.TM_done, k + 1)
                at_least(act, s.max_loaded[k % 2], 16 * (k // 2))
                act.activation(m.negmax_T[:, k % 2, :], m.bank[4].bitcast(BF16)[0:3 * H, 0:P], ACT.Copy).then_inc(s.negmax_T_ready, 1)
            for k, when, part in ((n - 3, 2, 0), (n - 4, 0, 1)):
                if u == when and 0 <= k < ALL:
                    act.wait_ge(s.PV_done, UNITS * k + 2 * part + 2)
                    at_least(act, s.AT_done, k)
                    units = slice(2 * P * part, 2 * P * part + 2 * P)
                    act.activation(m.o_T[:, units], m.bank[6 - part][:, 0:2 * P], ACT.Copy).then_inc(s.o_T_ready, 1)

    for k in range(FFN_ITEMS + 2):
        if 0 < k < FFN_ITEMS:
            hidden(k)
        if k + 1 < FFN_ITEMS:
            ffn_tokens(k + 1)
        if 1 <= k <= FFN_ITEMS:
            j, g = k - 1, (k - 1) % G
            act.wait_ge(s.f_nmr1, j + 1)
            for b in range(GB):
                xb = m.xr[:, columns(GB * g + b)]
                last = act.activation(xb, xb, ACT.Identity, bias=m.nmr[:, g, b:b + 1], scale=m.rstd[:, g, b:b + 1])
            last.then_inc(s.f_norm1, 1)
        if k >= 2:
            j, g = k - 2, (k - 2) % G
            act.wait_ge(s.f_nmr2, j + 1)
            act.wait_ge(s.t_done, T_FFN + j + 1)
            act.wait_ge(s.f_base_ready, 2 * j + 2)
            for b in range(GB):
                last = act.activation(m.y[:, columns(GB * g + b)], m.xr[:, columns(GB * g + b)], ACT.Identity,
                                      bias=m.nmr[:, g, b:b + 1], scale=m.rstd[:, g, b:b + 1])
            last.then_inc(s.f_out, 1)



def tensor_program(pe, m, s):
    pT, pTQ, pQ, pK, pV, pM, pG, pF = m.bank

    def transpose(t, src, g, bank=0):
        at_least(pe, s.xT_ready, t)
        for b in range(GB):
            last = pe.transpose(m.bank[bank][:, columns(b)], src[:, columns(GB * g + b)], m.ident[:, :])
        last.then_inc(s.t_done, 1)

    def project(k, t, w, bank=None):
        pe.wait_ge(s.xT_ready, t + 1)
        at_least(pe, s.rest_ready, k - 1)
        pe.matmul(m.bank[PROJ[k % 2] if bank is None else bank], m.w_att[:, w, :], m.xT[:, t % G, :], start=True, stop=True).then_inc(s.proj_done, 1)

    def values(k, t, w):
        before = [j for j in range(k) if V_BANK[j] == V_BANK[k]]
        if before:
            pe.wait_ge(s.v_ready, before[-1] + 1)
        for b in range(GB):
            last = pe.matmul(m.bank[V_BANK[k]][:, columns(b)], m.xT[:, t % G, columns(b)], m.w_att[:, w, :], start=True, stop=True)
        last.then_inc(s.v_done, 1)

    pe.wait_ge(s.ident_set, 2)
    pe.wait_ge(s.w_att_in, 16)
    for g in range(G + 1):
        if g < G:
            pe.wait_ge(s.ctx_in[g], 16)
            transpose(T_CTX + g, m.y, g)
        if g:
            project(M_CTX + g - 1, T_CTX + g - 1, 5)
            values(V_CTX + g - 1, T_CTX + g - 1, 6)
    pe.wait_ge(s.xT_ready, T_CTX + G)

    def slot(i, c):
        now, one, two = (stage(i, c, back) for back in (0, 1, 2))
        if now:
            n, g = now.n, now.g
            pe.wait_ge(s.xn_ready, n + 1)
            at_least(pe, s.hT_ready, n)
            for b in range(GB):
                last = pe.transpose(pT[:, columns(b)], m.xn[:, g, columns(b)], m.ident[:, :])
            last.then_inc(s.T_done, 1)
        if one:
            n, g = one.n, one.g
            pe.wait_ge(s.eq_ready, n + 1)
            at_least(pe, s.qt_ready, n)
            for b in range(GB):
                last = pe.transpose(pTQ[:, columns(b)], m.eq[:, g, columns(b)], m.ident[:, :])
            last.then_inc(s.TQ_done, 1)
        if two:
            n, g = two.n, two.g
            pe.wait_ge(s.gs_ready, n + 1)
            pe.wait_ge(s.vT_ready, n + 1)
            at_least(pe, s.x_added, n)
            for b in range(GB):
                last = pe.matmul(pF[:, columns(b)], m.vT[:, g, columns(b)], m.gs[:, g, columns(b)], start=True, stop=True)
            last.then_inc(s.F_done, 1)
        if now:
            n, g = now.n, now.g
            pe.wait_ge(s.hT_ready, n + 1)
            pe.wait_ge(s.wq_loaded, now.layer + 1)
            if isinstance(n, int) and n == 0:
                pe.wait_ge(s.rest_ready, M_CTX + G)
            at_least(pe, s.eq_ready, n)
            pe.matmul(pQ, m.wq_now[:, :], m.hT[:, g, :], start=True, stop=True).then_inc(s.Q_done, 1)
        if one:
            n, g = one.n, one.g
            pe.wait_ge(s.qt_ready, n + 1)
            pe.wait_ge(s.ek_ready, n + 1)
            at_least(pe, s.ms_ready, n)
            for b in range(GB):
                last = pe.matmul(pM[:, columns(b)], m.qt[:, g, columns(b)], m.ek[:, g, columns(b)], start=True, stop=True)
            last.then_inc(s.M_done, 1)
        if now:
            n, g = now.n, now.g
            at_least(pe, s.ek_ready, n)
            if isinstance(n, int) and n == 0:
                pe.wait_ge(s.v_ready, V_CTX + G)
                pe.wait_ge(s.w_qkv_in, 16)
            for b in range(GB):
                last = pe.matmul(pK[:, columns(b)], m.hT[:, g, columns(b)], m.w_qkv[:, now.layer, P:2 * P], start=True, stop=True)
            last.then_inc(s.K_done, 1)
        if one:
            n, g = one.n, one.g
            if isinstance(i, int) and i == 0 and c == 1:
                pe.wait_ge(s.w_out_in, 16)
            pe.wait_ge(s.ms_ready, n + 1)
            at_least(pe, s.gs_ready, n)
            for b in range(GB):
                last = pe.matmul(pG[:, columns(b)], m.ms[:, g, columns(b)], m.w_out[:, one.layer, :], start=True, stop=True)
            last.then_inc(s.G_done, 1)
        if now:
            n, g = now.n, now.g
            at_least(pe, s.vT_ready, n)
            pe.wait_ge(s.wv_loaded, now.layer + 1)
            pe.matmul(pV, m.wv_now[:, :], m.hT[:, g, :], start=True, stop=True).then_inc(s.V_done, 1)
        if isinstance(i, int) and i == DEPTH - 1 and c >= G - 1:
            if c == G - 1:
                pe.wait_ge(s.hT_ready, ITEMS)
            if c == G:
                pe.wait_ge(s.eq_ready, ITEMS)
                pe.wait_ge(s.ek_ready, ITEMS)
                pe.wait_ge(s.vT_ready, ITEMS)
            if c == G + 1:
                pe.wait_ge(s.qt_ready, ITEMS)
            self_step(c - G + 1)

    def self_step(g):
        if g < G:
            pe.wait_ge(s.x1_ready, g + 1)
            transpose(T_X1 + g, m.x0, g)
        if g:
            project(M_SELF + 2 * g - 2, T_X1 + g - 1, 0)
            project(M_SELF + 2 * g - 1, T_X1 + g - 1, 1)
            values(V_SELF + g - 1, T_X1 + g - 1, 2)

    slots(pe, slot)

    for g in range(3, G + 1):
        self_step(g)

    pe.wait_ge(s.v_ready, V_SELF + G - 1)
    pe.wait_ge(s.mask_set, 2)
    pe.wait_ge(s.ident_bf_set, 2)
    pe.wait_ge(s.qt_ready, ITEMS)
    pe.wait_ge(s.ms_ready, ITEMS)
    pe.wait_ge(s.gs_ready, ITEMS)
    pe.wait_ge(s.x_added, ITEMS)

    def scores(n, u):
        q, k, t, bank = m.q_op[n // GB % 2], m.k_op[n // GB % 2], columns(n % GB), m.bank[u % 2]
        at_least(pe, s.max_done, UNITS * n + u - 1)
        if n < B:
            pe.matmul(bank, m.ident_bf[:, :], m.mask[:, :, :], start=True, stop=False, skip_group_check=True)
        for jj in range(UT):
            for side in range(SIDES):
                j = UT * u + jj
                last = pe.matmul(bank[:, columns(SIDES * jj + side)], q[0:OP, j, side, t], k[0:OP, j, t],
                                 start=n >= B, stop=True, skip_group_check=True)
        last.then_inc(s.S_done, 1)

    def scores_T(n, u):
        q, k, t, bank = m.q_op[n // GB % 2], m.k_op[n // GB % 2], columns(n % GB), m.bank[2 + u % 2]
        at_least(pe, s.exp_done, UNITS * n + u - 1)
        for jj in range(UT):
            j = UT * u + jj
            last = pe.matmul(bank[:, 2 * P * jj:2 * P * jj + 2 * P], k[0:OP + 3, j, t], q[0:OP + 3, j, :, t], start=True, stop=True)
        last.then_inc(s.ST_done, 1)

    def weighted(n, u):
        pe.wait_ge(s.prob_masked if n < B else s.exp_done, UNITS * n + u + 1)
        for jj in range(UT):
            for side in range(SIDES):
                at = SIDES * jj + side
                last = pe.matmul(m.bank[6 - u // 2][VW * at:VW * at + VW, columns(u % 2)], m.v_pad[:, n % 2, TILES * side + UT * u + jj, :],
                                 m.prob[:, u, columns(at)], start=True, stop=True)
        last.then_inc(s.PV_done, 1)

    def ffn_tokens(k):
        f, g = k // G, k % G
        if f == 0:
            pe.wait_ge(s.a_shifted, G + g + 1)
        else:
            pe.wait_ge(s.f_out, g + 1)
        if k >= 2:
            pe.wait_ge(s.xT_ready, T_FFN + k - 1)
        for b in range(GB):
            last = pe.transpose(m.bank[T_BANK[k % 2]][:, columns(b)], m.y[:, columns(GB * g + b)], m.ident[:, :])
        last.then_inc(s.t_done, 1)

    def ffn_hidden(k):
        pe.wait_ge(s.xT_ready, T_FFN + k + 1)
        for c in range(FC):
            at_least(pe, s.f_relu, FC * (k - 1) + c + 1)
            pe.matmul(m.bank[c], m.w1[:, k // G, columns(c)], m.xT[:, k % G, :], start=True, stop=True).then_inc(s.f_H_done, 1)

    for n in range(ALL + 5):
        for u in range(UNITS):
            if n < ALL:
                if u in (0, 2) and n % GB == 0:
                    pe.wait_ge(s.op_loaded[n // GB % 2][u // 2], LOADS * (n // HALF + 1))
                scores(n, u)
            if n == 0 and u == 3:
                pe.wait_ge(s.rest_ready, M_SELF + 2 * G)
                pe.wait_ge(s.v_ready, V_SELF + G)
            k, v = unit_at(n, u, LAG_T)
            if k >= 0:
                if v == 0:
                    pe.wait_ge(s.max_loaded[k % 2], 16 * (k // 2 + 1))
                scores_T(k, v)
            k = n - 4
            if u == 3 and 0 <= k < ALL:
                pe.wait_ge(s.o_T_ready, 2 * k + 2)
                pe.wait_ge(s.negmax_T_ready, min(n, ALL))
                for at in range(UNITS):
                    last = pe.transpose(m.bank[4][:, columns(at)], m.o_T[:, columns(at)], m.ident[:, :])
                last.then_inc(s.AT_done, 1)
            k, v = unit_at(n, u, LAG_V)
            if k >= 0:
                if v == 0:
                    pe.wait_ge(s.v_pad_ready, k + 1)
                at_least(pe, s.o_T_ready, 2 * (k - 1) + v // 2 + 1)
                weighted(k, v)
            k = n - 5
            if u == 0 and 0 <= k < ALL:
                pe.wait_ge(s.o_ready, k + 1)
                if k % GB == 0:
                    at_least(pe, s.y_added, k // GB)
                pe.transpose(m.bank[7][:, columns(k % GB)], m.o[:, k % 2, :], m.ident[:, :]).then_inc(s.AO_done, 1)
            g = (n - 10) // GB
            if u == 0 and n % GB == 2 and 0 <= g < G:
                pe.wait_ge(s.a_norm, 2 * g + 2)
                transpose(T_X2 + g, m.y, g, 4)
            g = (n - 11) // GB
            if u == 0 and n % GB == 3 and 0 <= g < G:
                project(M_CROSS + g, T_X2 + g, 4, 4)
            g = (n - 8) // GB
            if u == 1 and n % GB == 0 and 0 <= g < 2 * G:
                pe.wait_ge(s.att_T_ready, g + 1)
                for b in range(GB):
                    last = pe.matmul(m.bank[7][:, columns(b)], m.att_T[:, columns(b)], m.w_att[:, 4 * (g // G) + 3, :],
                                     start=True, stop=True)
                last.then_inc(s.O_done, 1)
            k = n - 1
            if u == 1 and 0 <= k < ALL:
                pe.wait_ge(s.negmax_lo, k + 1)
                at_least(pe, s.negmax_T_ready, k)
                at_least(pe, s.o_ready, n - 5)
                if 10 <= n < 10 + B and n % GB == 2:
                    pe.wait_ge(s.xT_ready, T_X2 + (n - 10) // GB + 1)
                if 11 <= n < 11 + B and n % GB == 3:
                    pe.wait_ge(s.rest_ready, M_CROSS + (n - 11) // GB + 1)
                pe.transpose(m.bank[4].bitcast(BF16)[0:3 * H, 0:P], m.negmax_parts[:, k % 2, :], m.ident_bf[:, :]).then_inc(s.TM_done, 1)
        if n == ALL + 3:
            pe.wait_ge(s.w_ffn_in, 32)
            pe.wait_ge(s.o_T_ready, 2 * ALL)
            ffn_tokens(0)
        if n == ALL + 4:
            pe.wait_ge(s.max_done, UNITS * ALL)
            pe.wait_ge(s.exp_done, UNITS * ALL)
            ffn_hidden(0)
    pe.wait_ge(s.y_added, 2 * G)
    pe.wait_ge(s.o_ready, ALL)

    for k in range(1, FFN_ITEMS + 1):
        if k < FFN_ITEMS:
            ffn_tokens(k)
        j = k - 1
        at_least(pe, s.f_sum, j - 1)
        for c in range(FC):
            pe.wait_ge(s.f_relu, FC * j + c + 1)
            for b in range(GB):
                last = pe.matmul(m.bank[D_BANK[j % 2]][:, columns(b)], m.hidden[:, j % 2, c, columns(b)], m.w2[:, j // G, c, :],
                                 start=c == 0 and b == 0, stop=c == FC - 1, skip_group_check=True)
        last.then_inc(s.f_D_done, 1)
        if k < FFN_ITEMS:
            ffn_hidden(k)


def decoder_kernel(nc, x, context, w_qkv, w_out, w_att, w1, w2, rows, cols, q_rows, k_rows, out):
    a = Names()
    a.x, a.context, a.w_qkv, a.w_out, a.w_att, a.w1, a.w2, a.rows, a.cols, a.q_rows, a.k_rows, a.out = \
        x, context, w_qkv, w_out, w_att, w1, w2, rows, cols, q_rows, k_rows, out
    with ExitStack() as ctx:
        m = allocate(nc, ctx)
        s = semaphores(nc, ctx)
        block = ctx.enter_context(nc.Block())

        @block.sync
        def _(sp):
            sync_program(sp, m, s, a)

        @block.gpsimd
        def _(pool):
            gpsimd_program(pool, m, s, a)

        @block.vector
        def _(dve):
            vector_program(dve, m, s)

        @block.scalar
        def _(act):
            scalar_program(act, m, s)

        @block.tensor
        def _(pe):
            tensor_program(pe, m, s)



def kernel(**inputs):
    import numpy as _np
    import concourse.bacc as _bacc
    from concourse import mybir as _mybir
    from concourse.bass_utils import run_bass_kernel_spmd as _run

    def by_feature(w):
        w = _np.asarray(w)
        return w.reshape(w.shape[:-1] + (SIDES, TILES, DH)).swapaxes(-1, -2).reshape(w.shape)

    v = {k: _np.asarray(a) for k, a in inputs.items()}
    att, xat, ffn = "L0_attn_", "L0_xattn_", "L0_ffn_"
    arrays = {
        "x": v["x"],
        "context": v["ctx_1024"],
        "w_qkv": v[att + "w_qkv"],
        "w_out": v[att + "w_out"],
        "w_att": _np.stack([by_feature(v[f"{xat}{p}_w{n}"]) if n in "qk" else v[f"{xat}{p}_w{n}"]
                            for p in ("sa", "ca") for n in "qkvo"]),
        "w1": _np.stack([v[xat + "f_w1"], v[ffn + "w1"][0]]),
        "w2": _np.stack([v[xat + "f_w2"], v[ffn + "w2"][0]]),
        "rows": _np.concatenate([v[att + "b_out"]] + [v[f"{xat}{p}_{n}"][None] for p in ("sa", "ca") for n in ("bv", "bo", "g", "bt")]
                                + [v[xat + n][None] for n in ("f_b2", "f_g", "f_bt")]
                                + [v[ffn + "b2"][0:1], v[ffn + "gamma"][None], v[ffn + "beta"][None]]),
        "cols": _np.concatenate([v[att + "gamma"].T, v[att + "beta"].T]
                                + [by_feature(v[f"{xat}{p}_b{n}"])[:, None] for p in ("sa", "ca") for n in "qk"]
                                + [v[xat + "f_b1"].reshape(FC, P).T, v[ffn + "b1"][0].reshape(FC, P).T]
                                + [v[f"{xat}sa_{n}"][:, None] for n in ("g", "bt")], axis=1),
    }
    nc = _bacc.Bacc("TRN2", target_bir_lowering=False, num_devices=1)
    args = []
    arrays = {f"in_{name}": _np.ascontiguousarray(array) for name, array in arrays.items()}
    for name, array in arrays.items():
        args.append(nc.dram_tensor(name, array.shape, _mybir.dt.from_np(array.dtype), kind="ExternalInput").ap())
    for name in ("q_rows", "k_rows"):
        args.append(nc.dram_tensor(name, (2 * G, SIDES, PAIRS, DH * TILES, W), _mybir.dt.bfloat16, kind="Internal").ap())
    args.append(nc.dram_tensor("out", (B, P, P), _mybir.dt.float32, kind="ExternalOutput").ap())
    decoder_kernel(nc, *args)
    r = _run(nc, [arrays], core_ids=[0])
    return r.results[0]["out"]
```
